# Optimizing a Trainium2 kernel written in Bass

```python
import numpy as np
import jax
import jax.numpy as jnp

def _softmax(x, axis=-1):
    return jax.nn.softmax(x, axis=axis)

def _gelu(x):
    return jax.nn.gelu(x, approximate=True)

def _silu(x):
    return jax.nn.silu(x)

def _sigmoid(x):
    return jax.nn.sigmoid(x)

def _layernorm(x, axis=-1, eps=1e-05):
    m = jnp.mean(x, axis=axis, keepdims=True)
    v = jnp.var(x, axis=axis, keepdims=True)
    return (x - m) / jnp.sqrt(v + eps)

def _scatter_add(tgt, idx, src, axis=0):
    return tgt.at[idx].add(src)

def _segment_sum(src, seg, n):
    return jax.ops.segment_sum(src, seg, n)
kernel_name = 'mk_flamingo_gated_d1_seqx_r4_dae9aa'

def setup_inputs(seed: int=0):
    np.random.seed(seed)
    _w = jnp.asarray

    def _rec_inputs():
        import jax
        import jax.numpy as jnp
        _rk = jax.random.key(seed)
        x = -0.0002928 + 1 * jax.random.normal(jax.random.fold_in(_rk, 1), (64, 128, 256), jnp.float32)
        _lenS = 128 - jax.random.randint(jax.random.fold_in(_rk, 7), (64,), 0, max(1, 128 // 4) + 1, jnp.int32)
        _lenS2 = 128 - jax.random.randint(jax.random.fold_in(_rk, 8), (64,), 0, max(1, 128 // 4) + 1, jnp.int32)
        _ctx_1024P = jax.random.normal(jax.random.fold_in(_rk, 11), (64, 16, 256), jnp.float32)
        _ctx_1024c = jax.random.dirichlet(jax.random.fold_in(_rk, 511), 0.3 * jnp.ones((16,), jnp.float32), (64, 128))
        _ctx_1024t = jnp.einsum('bsk,bkd->bsd', _ctx_1024c, _ctx_1024P)
        _ctx_1024t = _ctx_1024t * jax.lax.rsqrt(jnp.mean(jnp.square(_ctx_1024t)) + 1e-12) * 0.953939
        ctx_1024 = -1.39393e-06 + 0.999914 * (_ctx_1024t + 0.3 * jax.random.normal(jax.random.fold_in(_rk, 611), (64, 128, 256), jnp.float32))
        _validS = jnp.arange(128)[None, :] < _lenS[:, None]
        _validS2 = jnp.arange(128)[None, :] < _lenS2[:, None]
        _causal = jnp.tril(jnp.ones((128, 128), dtype=bool))
        mask_BxSxS2_ff1 = jnp.where(jnp.ones((64, 128, 128), dtype=bool), 1.0, 0.0).astype(jnp.float32)
        _g = jax.random.normal(jax.random.fold_in(_rk, 9001), (2, 1), jnp.float32)
        _g = jnp.sign(_g) * jnp.maximum(jnp.abs(_g), 1.0) + (_g == 0) * 1.0
        g_xattn = _g[0]
        g_ffn = _g[1]
        return (x, ctx_1024, mask_BxSxS2_ff1, g_xattn, g_ffn)
    x, ctx_1024, mask_BxSxS2_ff1, g_xattn, g_ffn = _rec_inputs()

    def _L0_xattn_setup():
        import jax, jax.numpy as jnp
        import numpy as np
        D_MODEL = 256
        H = 16
        HEAD = D_MODEL // H
        key = jax.random.key(seed)
        ks = jax.random.split(key, 10)
        B, S = (2, 512)
        x = jax.random.normal(ks[0], (B, S, D_MODEL), dtype=jnp.float32)
        y = jax.random.normal(ks[1], (B, S, D_MODEL), dtype=jnp.float32)
        mask = jnp.ones((B, S, S), dtype=jnp.float32)
        s = 1.0 / np.sqrt(D_MODEL)
        Wq = jax.random.normal(ks[2], (D_MODEL, D_MODEL), dtype=jnp.float32) * s
        Wk = jax.random.normal(ks[3], (D_MODEL, D_MODEL), dtype=jnp.float32) * s
        Wv = jax.random.normal(ks[4], (D_MODEL, D_MODEL), dtype=jnp.float32) * s
        Wo = jax.random.normal(ks[5], (D_MODEL, D_MODEL), dtype=jnp.float32) * s
        bq = jnp.zeros((D_MODEL,), jnp.float32)
        bk = jnp.zeros((D_MODEL,), jnp.float32)
        bv = jnp.zeros((D_MODEL,), jnp.float32)
        bo = jnp.zeros((D_MODEL,), jnp.float32)
        return {'x': x, 'y': y, 'mask': mask, 'Wq': Wq, 'bq': bq, 'Wk': Wk, 'bk': bk, 'Wv': Wv, 'bv': bv, 'Wo': Wo, 'bo': bo}
    _L0_xattn_all = _L0_xattn_setup()
    _L0_xattn_in = {k: v for k, v in _L0_xattn_all.items() if k in ('Wq', 'bq', 'Wk', 'bk', 'Wv', 'bv', 'Wo', 'bo')}
    del _L0_xattn_all

    def _L0_ffn_setup():
        import jax, jax.numpy as jnp
        import numpy as np
        CAPACITY = 2
        B, S, D, E, I = (4, 1024, 256, 8, 1024)
        key = jax.random.key(seed)
        k0, k1, k2, k3, k4 = jax.random.split(key, 5)
        x = jax.random.normal(k0, (B, S, D), dtype=jnp.float32)
        gate_w = jax.random.normal(k1, (E, D), dtype=jnp.float32) * 0.006
        w_gate = jax.random.normal(k2, (E, I, D), dtype=jnp.float32) * (1.0 / np.sqrt(D))
        w_up = jax.random.normal(k3, (E, I, D), dtype=jnp.float32) * (1.0 / np.sqrt(D))
        w_down = jax.random.normal(k4, (E, D, I), dtype=jnp.float32) * (1.0 / np.sqrt(I))
        return {'x': x, 'gate_w': gate_w, 'w_gate': w_gate, 'w_up': w_up, 'w_down': w_down}
    _L0_ffn_all = _L0_ffn_setup()
    _L0_ffn_in = {k: v for k, v in _L0_ffn_all.items() if k in ('gate_w', 'w_gate', 'w_up', 'w_down')}
    del _L0_ffn_all
    return {'x': x, 'ctx_1024': ctx_1024, 'mask_BxSxS2_ff1': mask_BxSxS2_ff1, 'g_xattn': g_xattn, 'g_ffn': g_ffn, 'L0_xattn_Wq': _L0_xattn_in['Wq'], 'L0_xattn_bq': _L0_xattn_in['bq'], 'L0_xattn_Wk': _L0_xattn_in['Wk'], 'L0_xattn_bk': _L0_xattn_in['bk'], 'L0_xattn_Wv': _L0_xattn_in['Wv'], 'L0_xattn_bv': _L0_xattn_in['bv'], 'L0_xattn_Wo': _L0_xattn_in['Wo'], 'L0_xattn_bo': _L0_xattn_in['bo'], 'L0_ffn_gate_w': _L0_ffn_in['gate_w'], 'L0_ffn_w_gate': _L0_ffn_in['w_gate'], 'L0_ffn_w_up': _L0_ffn_in['w_up'], 'L0_ffn_w_down': _L0_ffn_in['w_down']}

def reference(x, ctx_1024, mask_BxSxS2_ff1, g_xattn, g_ffn, L0_xattn_Wq, L0_xattn_bq, L0_xattn_Wk, L0_xattn_bk, L0_xattn_Wv, L0_xattn_bv, L0_xattn_Wo, L0_xattn_bo, L0_ffn_gate_w, L0_ffn_w_gate, L0_ffn_w_up, L0_ffn_w_down):
    import jax
    import jax.numpy as jnp

    def _L0_xattn_ref(x, y, mask, Wq, bq, Wk, bk, Wv, bv, Wo, bo):
        import jax, jax.numpy as jnp
        import numpy as np
        D_MODEL = 256
        H = 16
        HEAD = D_MODEL // H
        B, Sq, D = x.shape
        Skv = y.shape[1]
        q = x @ Wq.T + bq
        k = y @ Wk.T + bk
        v = y @ Wv.T + bv
        q = q.reshape(B, Sq, H, HEAD)
        k = k.reshape(B, Skv, H, HEAD)
        v = v.reshape(B, Skv, H, HEAD)
        score = jnp.einsum('bqhd,bkhd->bhqk', q, k) / np.sqrt(HEAD)
        score = score + (1.0 - mask[:, None, :, :]) * -1000000000.0
        attn = jax.nn.softmax(score, axis=-1)
        out = jnp.einsum('bhqk,bkhd->bqhd', attn, v).reshape(B, Sq, D)
        return out @ Wo.T + bo

    def _L0_ffn_ref(x, gate_w, w_gate, w_up, w_down):
        import jax, jax.numpy as jnp
        import numpy as np
        CAPACITY = 2
        B, S, D = x.shape
        E = gate_w.shape[0]
        k = S // E * CAPACITY
        logits = jnp.einsum('bsd,ed->bse', x, gate_w)
        affinity = jax.nn.softmax(logits, axis=-1)
        affinity = jnp.transpose(affinity, (0, 2, 1))
        gating, idx = jax.lax.top_k(affinity, k)
        bidx = jnp.arange(B)[:, None, None]
        x_in = x[bidx, idx]
        h = jax.nn.silu(jnp.einsum('bekd,eid->beki', x_in, w_gate)) * jnp.einsum('bekd,eid->beki', x_in, w_up)
        x_e = jnp.einsum('beki,edi->bekd', h, w_down)
        out = jnp.zeros_like(x).at[bidx, idx].add(gating[..., None] * x_e)
        return out
    x = x + jnp.tanh(g_xattn[0]) * _L0_xattn_ref(_layernorm(x, axis=-1), ctx_1024, mask_BxSxS2_ff1, L0_xattn_Wq, L0_xattn_bq, L0_xattn_Wk, L0_xattn_bk, L0_xattn_Wv, L0_xattn_bv, L0_xattn_Wo, L0_xattn_bo)
    x = x + jnp.tanh(g_ffn[0]) * _L0_ffn_ref(_layernorm(x, axis=-1), L0_ffn_gate_w, L0_ffn_w_gate, L0_ffn_w_up, L0_ffn_w_down)
    return x

_drawn_inputs = setup_inputs


def setup_inputs(seed=0):
    import zlib

    import numpy as np

    out = dict(_drawn_inputs(seed))
    spreads = {'L0_xattn_bq': (0.0, 0.393),
     'L0_xattn_bk': (0.0, 0.8),
     'L0_xattn_bv': (0.0, 0.1),
     'L0_xattn_bo': (0.0, 0.1)}
    factors = {}
    for name, (base, spread) in spreads.items():
        noise = np.random.default_rng([zlib.crc32(name.encode()), seed]).standard_normal(out[name].shape)
        drawn = base * np.exp(spread * noise) if base else spread * noise
        out[name] = jnp.asarray(drawn.astype(out[name].dtype))
    for name, factor in factors.items():
        out[name] = (out[name] * factor).astype(out[name].dtype)
    return out
```

```python
from contextlib import ExitStack

import concourse.bass as bass
from concourse import mybir

F32 = mybir.dt.float32
F32R = mybir.dt.float32r
F16 = mybir.dt.float16
BF16 = mybir.dt.bfloat16
ALU = mybir.AluOpType
ACT = mybir.ActivationFunctionType
AXX = mybir.AxisListType.X

B, S, D = 64, 128, 256
H, DH = 16, 16
E, FF, K = 8, 1024, 32
P = 128
DC = D // P
FC = FF // P
GB = 4
G = B // GB
T = GB * S
HU = 4
UB = H // HU
U = GB * UB
HC = P // DH
VP = 3 * DH
EPS = 1e-5
RB = P // E
RT = B // RB
EC = P // K
SLOTS = B * K
NT = SLOTS // 512


class Chain:

    def __init__(self, eng, sem, base=0):
        self.eng, self.sem, self.base, self.n = eng, sem, base, 0

    def mark(self, ins):
        self.n += 1
        ins.then_inc(self.sem, 1)

    def settle(self):
        self.eng.wait_ge(self.sem, self.base + self.n)

    def link(self, ins):
        self.mark(ins)
        self.settle()


class Room:

    def __init__(self, nc, ctx, tag):
        self.nc, self.ctx, self.tag = nc, ctx, tag

    def sb(self, name, shape, dt):
        return self.ctx.enter_context(self.nc.sbuf_tensor(f"{self.tag}_{name}", shape, dt))

    def ps(self, name, shape, dt):
        return self.ctx.enter_context(self.nc.psum_tensor(f"{self.tag}_{name}", shape, dt))

    def sem(self, name):
        return self.ctx.enter_context(self.nc.semaphore(f"{self.tag}_{name}"))


def raw(ap):
    return ap.bitcast(F32)


def constants(nc, keep, a):
    c = {
        "id32": keep.sb("id32", [P, P], F32),
        "id16": keep.sb("id16", [P, P], F16),
        "idb": keep.sb("idb", [P, P], BF16),
        "slot": keep.sb("slot", [P, K], F32),
        "own": keep.sb("own", [P, DC, 3, E], F32),
        "tg": keep.sb("tg", [P, 2], F32),
        "aff": keep.sb("aff", [P, B * E], F32),
        "gating": keep.sb("gating", [P, B, DC], F32),
    }
    with ExitStack() as ctx:
        r = Room(nc, ctx, "c")
        g = r.sb("g", [P, 2], F32)
        loaded, pooled, pool_link = r.sem("loaded"), r.sem("pooled"), r.sem("pool_link")
        block = ctx.enter_context(nc.Block())

        @block.sync
        def _(sp):
            sp.dma_start(g[:, 0:1], a["g_xattn"].partition_broadcast(P)).then_inc(loaded, 16)
            sp.dma_start(g[:, 1:2], a["g_ffn"].partition_broadcast(P)).then_inc(loaded, 16)

        @block.scalar
        def _(act):
            act.wait_ge(loaded, 32)
            nc.scalar.activation(c["tg"][:], g[:], ACT.Tanh).then_inc(pooled, 1)

        @block.gpsimd
        def _(pool):
            chain = Chain(pool, pool_link)
            for name in ("id32", "id16", "idb"):
                chain.mark(nc.gpsimd.memset(c[name][:], 0.0))
            chain.mark(nc.gpsimd.memset(c["own"][:], 1.0))
            chain.mark(nc.gpsimd.iota(c["slot"][:], pattern=[[1, K]], base=0, channel_multiplier=0,
                                      allow_small_or_imprecise_dtypes=True))
            chain.settle()
            for name in ("id32", "id16", "idb"):
                chain.mark(nc.gpsimd.affine_select(out=c[name][:], in_=c[name][:], compare_op=ALU.not_equal, fill=1.0,
                                                   base=0, pattern=[[-1, P]], channel_multiplier=1))
            for half in range(DC):
                v = c["own"][:, half, :, :]
                for sign, base in ((1, K * EC * half), (-1, K - 1 - K * EC * half)):
                    chain.link(nc.gpsimd.affine_select(out=v, in_=v, compare_op=ALU.is_ge, fill=0.0, base=base,
                                                       pattern=[[0, 3], [-sign * K, E]], channel_multiplier=sign))
            chain.settle()
    return c


LT, LP = 3, 4


def attention(nc, c, a, x2_dram, xln_dram):
    with ExitStack() as ctx:
        r = Room(nc, ctx, "a")
        WN = ("q", "k", "v", "o")
        wraw = r.sb("wraw", [P, DC, D], F32)
        whi = {n: r.sb(f"w{n}hi", [P, DC, D], F32R) for n in WN}
        wlo = {n: r.sb(f"w{n}lo", [P, DC, D], F32R) for n in WN}
        gateT = r.sb("gateT", [P, DC, E], F32)
        bqk = r.sb("bqk", [P, 2, DC], F32)
        bvo = r.sb("bvo", [P, 2, D], F32)
        minus_half = r.sb("minus_half", [P, GB], F32)
        after = r.sb("after", [P, 4], F32)
        eps = r.sb("eps", [P, GB], F32)
        x_in = r.sb("x_in", [P, GB, D], F32)
        x_res = r.sb("x_res", [P, GB, D], F32)
        yT = r.sb("yT", [P, DC, T], F32)
        yhi = r.sb("yhi", [P, DC, T], F32R)
        ylo = r.sb("ylo", [P, DC, T], F32R)
        mask = r.sb("mask", [P, GB, S], F32)
        far = r.sb("far", [P, 2, GB, S], F32)
        stats = r.sb("stats", [P, 2, GB, 6], F32)
        mv = r.sb("mv", [P, 2, GB, 2], F32)
        rstd = r.sb("rstd", [P, 2, GB], F32)
        xn = r.sb("xn", [P, GB, D], F32)
        xnhi = r.sb("xnhi", [P, DC, T], F32R)
        xnlo = r.sb("xnlo", [P, DC, T], F32R)
        qhi = r.sb("qhi", [P, 2, DC, T], F32R)
        qlo = r.sb("qlo", [P, 2, DC, T], F32R)
        kk = r.sb("kk", [P, 2, DC, T], F32R)
        kb = [r.sb(f"kb{i}", [P, 2, DC, HC, 2 * S], F32R) for i in range(2)]
        v32 = r.sb("v32", [P, 2, D], F32)
        vr = r.sb("vr", [P, 2, D], F32)
        v3 = r.sb("v3", [P, 2, GB, H, 3, DH], BF16)
        negs = r.sb("negs", [P, 2, HU, S], F32)
        negmax = r.sb("negmax", [P, 2, HU], F32)
        prob = r.sb("prob", [P, 2, HU, S], F32)
        sums = r.sb("sums", [P, 2, H], F32)
        rinv = r.sb("rinv", [P, H], F32)
        phl = r.sb("phl", [P, 4, 2, HU, S], F16)
        pT = r.sb("pT", [P, 2, 2, HU, S], F16)
        osum = r.sb("osum", [P, 2, H // 2, DH], F32)
        on = r.sb("on", [P, 2, GB, D], F32)
        ohi, olo = xnhi, xnlo
        x2 = r.sb("x2", [P, GB, D], F32)
        xln = r.sb("xln", [P, GB, D], F32)
        xlnT = r.sb("xlnT", [P, DC, T], F32)
        lg = r.sb("lg", [P, GB, E], F32)
        lgx = r.sb("lgx", [P, GB, E], F32)
        lmax = r.sb("lmax", [P, GB], F32)
        lsum = r.sb("lsum", [P, GB], F32)
        score_ps = [r.ps(f"score{i}", [P, HU, S], F32) for i in range(2)]
        pT_ps = [r.ps(f"pT_ps{i}", [P, 2, HU, S], F16) for i in range(2)]
        o_ps = [r.ps(f"o_ps{i}", [P, 512], F32) for i in range(2)]
        m_ps = [r.ps(f"m_ps{i}", [P, 512], F32) for i in range(2)]

        w_loaded, w_split, w_link = r.sem("w_loaded"), r.sem("w_split"), r.sem("w_link")
        w_hi = r.sem("w_hi")
        const_loaded, bias_ready = r.sem("const_loaded"), r.sem("bias_ready")
        kb_zero = r.sem("kb_zero")
        x_loaded, y_loaded, mask_loaded, xres_loaded = (r.sem(n) for n in ("x_loaded", "y_loaded", "mask_loaded", "xres_loaded"))
        y_split, yhi_ready = r.sem("y_split"), r.sem("yhi_ready")
        ln_link, ln2_link, v_link, soft_link, on_link = (r.sem(n) for n in ("ln_link", "ln2_link", "v_link", "soft_link", "on_link"))
        stats_ready, rstd_ready, xn_ready, rstd_link = (r.sem(n) for n in ("stats_ready", "rstd_ready", "xn_ready", "rstd_link"))
        xnT_full, xnhi_ready, xn_split = r.sem("xnT_full"), r.sem("xnhi_ready"), r.sem("xn_split")
        q_full, qhi_ready, q_split = r.sem("q_full"), r.sem("qhi_ready"), r.sem("q_split")
        k_full, khi_ready, k_split = r.sem("k_full"), r.sem("khi_ready"), r.sem("k_split")
        k_spread = [r.sem("k_spread0"), r.sem("k_spread1")]
        v_full, v_ready, far_ready = r.sem("v_full"), r.sem("v_ready"), r.sem("far_ready")
        score_full, negs_ready, prob_ready = r.sem("score_full"), r.sem("negs_ready"), r.sem("prob_ready")
        phi_ready, plo_ready = r.sem("phi_ready"), r.sem("plo_ready")
        pT_full, pv_done = r.sem("pT_full"), r.sem("pv_done")
        pT_out = [r.sem("pT_out_even"), r.sem("pT_out_odd")]
        o_read, on_ready = r.sem("o_read"), r.sem("on_ready")
        oT_full, ohi_ready, o_split = r.sem("oT_full"), r.sem("ohi_ready"), r.sem("o_split")
        wo_full, x2_ready, stats2_ready, rstd2_ready, xln_ready = (
            r.sem(n) for n in ("wo_full", "x2_ready", "stats2_ready", "rstd2_ready", "xln_ready"))
        xres_biased = r.sem("xres_biased")
        xlnT_full, xlnT_out, lg_full, lg_out, lgx_ready, aff_ready = (
            r.sem(n) for n in ("xlnT_full", "xlnT_out", "lg_full", "lg_out", "lgx_ready", "aff_ready"))
        x2_stored, xln_stored = r.sem("x2_stored"), r.sem("xln_stored")

        x_v = a["x"].rearrange("(g b) p d -> g p b d", b=GB)
        y_v = a["ctxT"].rearrange("(c p) (g t) -> g p c t", p=P, t=T)
        mask_v = a["mask"].rearrange("(g b) q k -> g q b k", b=GB)
        x2_v = x2_dram.rearrange("(g b) p d -> g p b d", b=GB)
        xln_v = xln_dram.rearrange("(g b) p d -> g p b d", b=GB)

        def steps(eng, step):
            step(0, 0, True, False, False)
            step(1, 1, True, True, False)
            step(2, 0, True, True, True)
            step(3, 1, True, True, True)
            with eng.Fori(2, G // 2) as i:
                step(i * 2, 0, True, True, True)
                step(i * 2 + 1, 1, True, True, True)
            step(G, 0, False, True, True)
            step(G + 1, 1, False, False, True)

        C_OT, C_WO, C_LNT, C_LG = 0, 2, 7, 9
        C_RSTD = 5
        A_XT, A_Q, A_K, A_V = 10, 12, 13, 14
        SLOT = U + LP

        block = ctx.enter_context(nc.Block())

        @block.sync
        def _(sp):
            for n, name in enumerate(WN):
                if n:
                    sp.wait_ge(w_split, n)
                sp.dma_start(wraw[:], a[f"w{name}T"].rearrange("(c p) n -> p c n", p=P)).then_inc(w_loaded, 16)
            sp.dma_start(gateT[:], a["gateT"].rearrange("(c p) n -> p c n", p=P)).then_inc(const_loaded, 16)
            with nc.allow_non_contiguous_dma(reason="bias columns, once"):
                sp.dma_start(bqk[:, 0, :], a["bq"].rearrange("(c p) -> p c", p=P)).then_inc(const_loaded, 16)
                sp.dma_start(bqk[:, 1, :], a["bk"].rearrange("(c p) -> p c", p=P)).then_inc(const_loaded, 16)
            sp.dma_start(bvo[:, 0, :], a["bv"].partition_broadcast(P)).then_inc(const_loaded, 16)
            sp.dma_start(bvo[:, 1, :], a["bo"].partition_broadcast(P)).then_inc(const_loaded, 16)

            def step(g, par, has_a, has_b, has_c):
                if has_a:
                    if not isinstance(g, int) or g > 0:
                        sp.wait_ge(y_split, g * 2)
                        sp.wait_ge(xn_ready, g)
                        sp.wait_ge(far_ready, g)
                    sp.dma_start(x_in[:], x_v[g]).then_inc(x_loaded, 16)
                    sp.dma_start(yT[:], y_v[g]).then_inc(y_loaded, 16)
                    sp.dma_start(mask[:], mask_v[g]).then_inc(mask_loaded, 16)
                if has_c:
                    if not isinstance(g, int) or g > 2:
                        sp.wait_ge(x2_ready, (g - 2) * 2)
                    sp.dma_start(x_res[:], x_v[g - 2]).then_inc(xres_loaded, 16)
                    sp.wait_ge(x2_ready, (g - 1) * 2)
                    sp.dma_start(x2_v[g - 2], x2[:]).then_inc(x2_stored, 16)
                    sp.wait_ge(xln_ready, g - 1)
                    sp.dma_start(xln_v[g - 2], xln[:]).then_inc(xln_stored, 16)
                if has_a:
                    sp.wait_ge(k_split, (g + 1) * 2)
                    for pair in range(2):
                        if not isinstance(g, int) or g > 0:
                            sp.wait_ge(score_full, g * U - U // 2 + pair * U // 2)
                        for h in range(HC):
                            for x in range(2):
                                sp.dma_start(raw(kb[pair][h * DH:(h + 1) * DH, x, :, h, :]),
                                             raw(kk[h * DH:(h + 1) * DH, x, :, pair * 2 * S:(pair + 1) * 2 * S])
                                             ).then_inc(k_spread[pair], 16)

            sp.wait_ge(kb_zero, 2)
            steps(sp, step)
            sp.wait_ge(x2_stored, 16 * G)
            sp.wait_ge(xln_stored, 16 * G)

        @block.gpsimd
        def _(pool):
            nc.gpsimd.memset(eps[:], EPS)
            nc.gpsimd.memset(minus_half[:], -0.5).then_inc(rstd_link, 1)
            for i in range(2):
                nc.gpsimd.memset(raw(kb[i][:]), 0.0).then_inc(kb_zero, 1)
            pool.wait_ge(rstd_link, 1)
            pool.wait_ge(bias_ready, 1)

            def rsqrt(n, ready, done, base):
                nc.gpsimd.tensor_tensor(rstd[:, n, :], mv[:, n, :, 1], eps[:], ALU.add).then_inc(rstd_link, 1)
                pool.wait_ge(rstd_link, base)
                nc.gpsimd.tensor_tensor(rstd[:, n, :], rstd[:, n, :], minus_half[:], ALU.pow).then_inc(done, 1)

            def step(g, par, has_a, has_b, has_c):
                if has_a:
                    pool.wait_ge(stats_ready, g + 1)
                    first = g if isinstance(g, int) and g < 2 else g + (g - 2)
                    rsqrt(0, stats_ready, rstd_ready, first + 2)
                    for h in range(DC):
                        pool.wait_ge(yhi_ready, g + 1)
                        nc.gpsimd.tensor_tensor(ylo[:, h, :], yT[:, h, :], yhi[:, h, :], ALU.subtract).then_inc(y_split, 1)
                for s in range(U + 1):
                    if has_b and s < U:
                        u = (g - 1) * U + s
                        pool.wait_ge(phi_ready, u + 1)
                        nc.gpsimd.tensor_tensor(phl[:, s % 4, 1], prob[:, s % 2], phl[:, s % 4, 0],
                                                ALU.subtract).then_inc(plo_ready, 1)
                    if has_c and s == 2:
                        pool.wait_ge(xres_loaded, (g - 1) * 16)
                        nc.gpsimd.tensor_tensor(x_res[:], x_res[:], bvo[:, 1:2, :].to_broadcast([P, GB, D]),
                                                ALU.add).then_inc(xres_biased, 1)
                    if has_c and s == C_RSTD:
                        pool.wait_ge(stats2_ready, g - 1)
                        before = G if isinstance(g, int) and g >= G else g + 1
                        rsqrt(1, stats2_ready, rstd2_ready, 1 + before + (g - 1))

            steps(pool, step)

        @block.tensor
        def _(pe):
            pe.wait_ge(w_split, 4)
            pe.wait_ge(const_loaded, 80)

            def three(out, whi_, wlo_, xhi_, xlo_, first, last):
                nc.tensor.matmul(out, whi_, xhi_, start=first, stop=False)
                nc.tensor.matmul(out, whi_, xlo_, start=False, stop=False)
                return nc.tensor.matmul(out, wlo_, xhi_, start=False, stop=last)

            def step(g, par, has_a, has_b, has_c):
                old = 1 - par
                c_ = g - 2

                def scores(s):
                    b, m = s // UB, s % UB
                    ch, h0 = m // 2, (m % 2) * HU
                    pair, t = b // 2, slice((b % 2) * S, (b % 2 + 1) * S)
                    u = (g - 1) * U + s
                    if s == 0:
                        pe.wait_ge(q_split, g * 2)
                    if s % (U // 2) == 0:
                        pe.wait_ge(k_spread[pair], g * 16 * 2 * HC)
                    if not isinstance(g, int) or g > 1 or s >= 2:
                        pe.wait_ge(negs_ready, u - 1)
                    q1 = qhi[:, old, ch, b * S:(b + 1) * S]
                    q2 = qlo[:, old, ch, b * S:(b + 1) * S]
                    k1 = kb[pair][:, 0, ch, h0:h0 + HU, t]
                    k2 = kb[pair][:, 1, ch, h0:h0 + HU, t]
                    three(score_ps[s % 2][:], q1, q2, k1, k2, True, True).then_inc(score_full, 1)

                def transposes(s):
                    u = (g - 1) * U + s
                    pe.wait_ge(plo_ready, u + 1)
                    if not isinstance(g, int) or g > 1 or s >= 2:
                        pe.wait_ge(pT_out[s % 2], (g - 1) * (U // 2) + s // 2)
                    for part in range(2):
                        for h in range(HU):
                            last = nc.tensor.transpose(pT_ps[s % 2][:, part, h, :], phl[:, s % 4, part, h, :], c["id16"][:])
                    last.then_inc(pT_full, 1)

                def values(s):
                    b, m = s // UB, s % UB
                    u = (g - 1) * U + s
                    if s == 0:
                        pe.wait_ge(v_ready, g * 2)
                    pe.wait_ge(pT_out[s % 2], (g - 1) * (U // 2) + s // 2 + 1)
                    if m % 2 == 0 and (not isinstance(g, int) or g > 1 or s >= UB):
                        pe.wait_ge(o_read, (g - 1) * GB * 2 + b * 2 + m // 2 - 1)
                    bank = o_ps[m // 2]
                    for h in range(HU):
                        at = ((m % 2) * HU + h) * VP
                        for part in range(2):
                            last = nc.tensor.matmul(bank[:, at:at + VP], pT[:, s % 2, part, h, :],
                                                    v3[:, old, b, m * HU + h, :, :].rearrange("p n d -> p (n d)"),
                                                    start=(part == 0), stop=(part == 1))
                    last.then_inc(pv_done, 1)

                for s in range(SLOT):
                    if has_b and s < U:
                        scores(s)
                    if has_b and 0 <= s - LT < U:
                        transposes(s - LT)
                    if has_b and 0 <= s - LP < U:
                        values(s - LP)
                    if has_c and s == C_OT:
                        pe.wait_ge(on_ready, (g - 1) * GB * 2)
                        if isinstance(g, int) and g > G:
                            pe.wait_ge(lg_out, g - 2)
                        else:
                            pe.wait_ge(v_ready, g * 2)
                        for ch in range(DC):
                            for b in range(GB):
                                last = nc.tensor.transpose(m_ps[ch][:, b * S:(b + 1) * S],
                                                           on[:, par, b, ch * P:(ch + 1) * P], c["id32"][:])
                            last.then_inc(oT_full, 1)
                    if has_c and C_WO <= s < C_WO + GB:
                        b = s - C_WO
                        if b == 0:
                            pe.wait_ge(o_split, (g - 1) * 2)
                        t = slice(b * S, (b + 1) * S)
                        for ch in range(DC):
                            last = three(m_ps[b // 2][:, (b % 2) * D:(b % 2 + 1) * D], ohi[:, ch, t], olo[:, ch, t],
                                         whi["o"][:, ch, :], wlo["o"][:, ch, :], ch == 0, ch == DC - 1)
                        if b % 2:
                            last.then_inc(wo_full, 1)
                    if has_c and s == C_LNT:
                        pe.wait_ge(xln_ready, g - 1)
                        for ch in range(DC):
                            for b in range(GB):
                                last = nc.tensor.transpose(m_ps[ch][:, b * S:(b + 1) * S],
                                                           xln[:, b, ch * P:(ch + 1) * P], c["id32"][:])
                            last.then_inc(xlnT_full, 1)
                    if has_c and s == C_LG:
                        pe.wait_ge(xlnT_out, (g - 1) * 2)
                        for b in range(GB):
                            for ch in range(DC):
                                last = nc.tensor.matmul(m_ps[0][:, b * E:(b + 1) * E], xlnT[:, ch, b * S:(b + 1) * S],
                                                        gateT[:, ch, :], start=(ch == 0), stop=(ch == DC - 1))
                        last.then_inc(lg_full, 1)
                    if has_a and s == A_XT:
                        pe.wait_ge(xn_ready, g + 1)
                        if has_c:
                            pe.wait_ge(lg_out, g - 1)
                            pe.wait_ge(xlnT_out, (g - 1) * 2)
                        elif g > 0:
                            pe.wait_ge(v_ready, g * 2)
                        for ch in range(DC):
                            for b in range(GB):
                                last = nc.tensor.transpose(m_ps[ch][:, b * S:(b + 1) * S],
                                                           xn[:, b, ch * P:(ch + 1) * P], c["id32"][:])
                            last.then_inc(xnT_full, 1)
                    if has_a and s in (A_Q, A_K):
                        name, hi, lo, full = ("q", xnhi, xnlo, q_full) if s == A_Q else ("k", yhi, ylo, k_full)
                        if s == A_Q:
                            pe.wait_ge(xn_split, (g + 1) * 2)
                        else:
                            pe.wait_ge(y_split, (g + 1) * 2)
                            pe.wait_ge(yhi_ready, g + 1)
                            pe.wait_ge(q_split, (g + 1) * 2)
                        for n in range(DC):
                            for ch in range(DC):
                                last = three(m_ps[n][:], whi[name][:, ch, n * P:(n + 1) * P],
                                             wlo[name][:, ch, n * P:(n + 1) * P], hi[:, ch, :], lo[:, ch, :],
                                             ch == 0, ch == DC - 1)
                            last.then_inc(full, 1)
                    if has_a and A_V <= s < A_V + GB:
                        b = s - A_V
                        if b == 0:
                            pe.wait_ge(k_split, (g + 1) * 2)
                        t = slice(b * S, (b + 1) * S)
                        for ch in range(DC):
                            last = three(m_ps[b // 2][:, (b % 2) * D:(b % 2 + 1) * D], yhi[:, ch, t], ylo[:, ch, t],
                                         whi["v"][:, ch, :], wlo["v"][:, ch, :], ch == 0, ch == DC - 1)
                        if b % 2:
                            last.then_inc(v_full, 1)

            steps(pe, step)

        @block.scalar
        def _(act):
            for n, name in enumerate(WN):
                act.wait_ge(w_loaded, 16 * (n + 1))
                nc.scalar.activation(whi[name][:], wraw[:], ACT.Copy, scale=-0.25 if name == "q" else 1.0).then_inc(w_hi, 1)
            act.wait_ge(bias_ready, 1)

            def step(g, par, has_a, has_b, has_c):
                old = 1 - par
                for s in range(SLOT):
                    if has_b and s < U:
                        u = (g - 1) * U + s
                        act.wait_ge(negs_ready, u + 1)
                        if not isinstance(g, int) or g > 1 or s >= 2:
                            act.wait_ge(plo_ready, u - 1)
                        b, m = s // UB, s % UB
                        if s % UB == 0 and (not isinstance(g, int) or g > 1 or b >= 2):
                            act.wait_ge(on_ready, ((g - 1) * GB + b - 1) * 2)
                        for h in range(HU):
                            last = nc.scalar.activation(prob[:, s % 2, h, :], negs[:, s % 2, h, :], ACT.Exp, scale=-1.0,
                                                        bias=negmax[:, s % 2, h:h + 1],
                                                        accum_out=sums[:, b % 2, m * HU + h:m * HU + h + 1])
                        last.then_inc(prob_ready, 1)
                    if has_b and 0 <= s - LT < U and (s - LT) % 2 == 0:
                        v = s - LT
                        u = (g - 1) * U + v
                        act.wait_ge(pT_full, u + 1)
                        if not isinstance(g, int) or g > 1 or v >= 2:
                            act.wait_ge(pv_done, u - 1)
                        nc.scalar.activation(pT[:, 0], pT_ps[0][:], ACT.Copy).then_inc(pT_out[0], 1)
                    if has_c and s == C_OT:
                        for ch in range(DC):
                            act.wait_ge(oT_full, (g - 2) * 2 + ch + 1)
                            act.wait_ge(q_full, (g if not isinstance(g, int) or g < G else G) * 2)
                            nc.scalar.activation(ohi[:, ch, :], m_ps[ch][:], ACT.Copy).then_inc(ohi_ready, 1)
                    if has_c and s == C_LNT:
                        for ch in range(DC):
                            act.wait_ge(xlnT_full, (g - 2) * 2 + ch + 1)
                            if not isinstance(g, int) or g > 2:
                                act.wait_ge(lg_full, g - 2)
                            nc.scalar.activation(xlnT[:, ch, :], m_ps[ch][:], ACT.Copy).then_inc(xlnT_out, 1)
                    if has_c and s == C_LG:
                        act.wait_ge(lgx_ready, g - 1)
                        nc.scalar.activation(lgx[:], lg[:], ACT.Exp).then_inc(lg_out, 1)
                    if has_a and s == A_XT:
                        for ch in range(DC):
                            act.wait_ge(xnT_full, g * 2 + ch + 1)
                            if has_c:
                                act.wait_ge(wo_full, (g - 1) * 2)
                            elif g > 0:
                                act.wait_ge(q_full, g * 2)
                            nc.scalar.activation(xnhi[:, ch, :], m_ps[ch][:], ACT.Copy).then_inc(xnhi_ready, 1)
                    if has_a and s == A_Q:
                        for ch in range(DC):
                            act.wait_ge(q_full, g * 2 + ch + 1)
                            nc.scalar.activation(qhi[:, par, ch, :], m_ps[ch][:], ACT.Identity,
                                                 bias=bqk[:, 0, ch:ch + 1]).then_inc(qhi_ready, 1)
                    if has_a and s == A_K:
                        for ch in range(DC):
                            act.wait_ge(k_full, g * 2 + ch + 1)
                            if not isinstance(g, int) or g > 0:
                                for pair in range(2):
                                    act.wait_ge(k_spread[pair], g * 16 * 2 * HC)
                            nc.scalar.activation(kk[:, 0, ch, :], m_ps[ch][:], ACT.Identity,
                                                 bias=bqk[:, 1, ch:ch + 1]).then_inc(khi_ready, 1)

            steps(act, step)

        @block.vector
        def _(dve):
            for n, name in enumerate(WN):
                dve.wait_ge(w_hi, n + 1)
                nc.vector.scalar_tensor_tensor(out=wlo[name][:], in0=wraw[:], scalar=-0.25 if name == "q" else 1.0,
                                               in1=whi[name][:], op0=ALU.mult, op1=ALU.subtract).then_inc(w_split, 1)
            dve.wait_ge(const_loaded, 80)
            nc.vector.tensor_scalar(bvo[:, 1, :], bvo[:, 1, :], c["tg"][:, 0:1], None, ALU.mult).then_inc(w_link, 1)
            nc.vector.tensor_scalar(bqk[:, 0, :], bqk[:, 0, :], -0.25, None, ALU.mult).then_inc(w_link, 1)
            dve.wait_ge(w_link, 2)
            nc.vector.tensor_copy(after[:, 0:2], bqk[:, 0, :]).then_inc(bias_ready, 1)

            def norm(x_tile, out, n, chain, ready, rstd_done, count, done):
                for b in range(GB):
                    chain.mark(nc.vector.bn_stats(stats[:, n, b, :], x_tile[:, b, :]))
                chain.settle()
                nc.vector.tensor_copy(after[:, 2 + n:3 + n], stats[:, n, 0, 0:1])
                for b in range(GB):
                    last = nc.vector.bn_aggr(mv[:, n, b, :], stats[:, n, b, :])
                last.then_inc(ready, 1)

            def normalise(x_tile, out, n, rstd_done, count, done):
                dve.wait_ge(rstd_done, count)
                for b in range(GB):
                    last = nc.vector.tensor_scalar(out[:, b, :], x_tile[:, b, :], mv[:, n, b, 0:1], rstd[:, n, b:b + 1],
                                                   ALU.subtract, ALU.mult)
                last.then_inc(done, 1)

            def step(g, par, has_a, has_b, has_c):
                old = 1 - par
                if has_a:
                    dve.wait_ge(x_loaded, (g + 1) * 16)
                    norm(x_in, xn, 0, Chain(dve, ln_link, g * GB), stats_ready, None, None, None)
                    dve.wait_ge(y_loaded, (g + 1) * 16)
                    if not isinstance(g, int) or g > 0:
                        dve.wait_ge(v_full, g * 2)
                    nc.vector.tensor_copy(yhi[:], yT[:]).then_inc(yhi_ready, 1)
                    dve.wait_ge(mask_loaded, (g + 1) * 16)
                    nc.vector.tensor_scalar(far[:, par], mask[:], -1.0, -1e9, ALU.add, ALU.mult).then_inc(far_ready, 1)
                    if not isinstance(g, int) or g > 0:
                        dve.wait_ge(xnT_full, g * 2)
                    normalise(x_in, xn, 0, rstd_ready, g + 1, xn_ready)
                for s in range(SLOT + 2):
                    if has_b and s < U:
                        u = (g - 1) * U + s
                        b = s // UB
                        dve.wait_ge(score_full, u + 1)
                        if s == 0:
                            dve.wait_ge(far_ready, g)
                        if not isinstance(g, int) or g > 1 or s >= 2:
                            dve.wait_ge(prob_ready, u - 1)
                        nc.vector.tensor_copy(after[:, s % 2:s % 2 + 1], score_ps[s % 2][:, 0, 0:1])
                        for h in range(HU):
                            last = nc.vector.tensor_tensor_reduce(
                                out=negs[:, s % 2, h, :], in0=score_ps[s % 2][:, h, :], in1=far[:, old, b, :], scale=1.0,
                                scalar=3.0e38, op0=ALU.add, op1=ALU.min, accum_out=negmax[:, s % 2, h:h + 1])
                        last.then_inc(negs_ready, 1)
                    if has_b and 0 <= s - 1 < U:
                        v = s - 1
                        u = (g - 1) * U + v
                        dve.wait_ge(prob_ready, u + 1)
                        if not isinstance(g, int) or g > 1 or v >= 4:
                            dve.wait_ge(pT_full, u - 3)
                        nc.vector.tensor_copy(phl[:, v % 4, 0], prob[:, v % 2]).then_inc(phi_ready, 1)
                    if has_b and 0 <= s - LT < U and (s - LT) % 2:
                        v = s - LT
                        u = (g - 1) * U + v
                        dve.wait_ge(pT_full, u + 1)
                        if not isinstance(g, int) or g > 1 or v >= 2:
                            dve.wait_ge(pv_done, u - 1)
                        nc.vector.tensor_copy(pT[:, 1], pT_ps[1][:]).then_inc(pT_out[1], 1)
                    v = s - LP - 1
                    if has_b and 0 <= v < U and v % 2:
                        u = (g - 1) * U + v
                        b, half = v // UB, (v % UB) // 2
                        hs = slice(half * HC, (half + 1) * HC)
                        chain = Chain(dve, on_link, (g - 1) * (U // 2) + (v - 1) // 2)
                        dve.wait_ge(pv_done, u + 1)
                        nc.vector.tensor_reduce(osum[:, half], o_ps[half][:, 0:HC * VP].rearrange("p (h n d) -> p h d n", n=3, d=DH),
                                                AXX, ALU.add).then_inc(o_read, 1)
                        chain.link(nc.vector.reciprocal(rinv[:, hs], sums[:, b % 2, hs]))
                        dve.wait_ge(o_read, (g - 1) * GB * 2 + b * 2 + half + 1)
                        nc.vector.tensor_tensor(
                            on[:, old, b, half * P:(half + 1) * P].rearrange("p (h d) -> p h d", d=DH), osum[:, half],
                            rinv[:, hs].unsqueeze(2).to_broadcast([P, HC, DH]), ALU.mult).then_inc(on_ready, 1)
                    if has_c and s == C_OT:
                        for ch in range(DC):
                            dve.wait_ge(ohi_ready, (g - 2) * 2 + ch + 1)
                            nc.vector.tensor_tensor(olo[:, ch, :], m_ps[ch][:], ohi[:, ch, :], ALU.subtract).then_inc(o_split, 1)
                    if has_c and s in (C_WO + 1, C_WO + 3):
                        n = (s - C_WO) // 2
                        dve.wait_ge(wo_full, (g - 2) * 2 + n + 1)
                        if n == 0:
                            dve.wait_ge(xres_biased, g - 1)
                            if not isinstance(g, int) or g > 2:
                                dve.wait_ge(x2_stored, (g - 2) * 16)
                        nc.vector.scalar_tensor_tensor(
                            out=x2[:, 2 * n:2 * n + 2, :], in0=m_ps[n][:].rearrange("p (b d) -> p b d", b=2), scalar=c["tg"][:, 0:1],
                            in1=x_res[:, 2 * n:2 * n + 2, :], op0=ALU.mult, op1=ALU.add).then_inc(x2_ready, 1)
                    if has_c and s == C_WO + 3:
                        dve.wait_ge(x2_ready, (g - 1) * 2)
                        norm(x2, xln, 1, Chain(dve, ln2_link, (g - 2) * GB), stats2_ready, None, None, None)
                    if has_c and s == C_WO + 4:
                        if not isinstance(g, int) or g > 2:
                            dve.wait_ge(xln_stored, (g - 2) * 16)
                            dve.wait_ge(xlnT_full, (g - 2) * 2)
                        normalise(x2, xln, 1, rstd2_ready, g - 1, xln_ready)
                    if has_c and s == C_LG:
                        chain = Chain(dve, soft_link, (g - 2) * 5)
                        dve.wait_ge(lg_full, g - 1)
                        l3 = m_ps[0][:, 0:GB * E].rearrange("p (b e) -> p b e", e=E)
                        chain.link(nc.vector.tensor_reduce(lmax[:], l3, AXX, ALU.max))
                        nc.vector.tensor_tensor(lg[:], l3, lmax[:].unsqueeze(2).to_broadcast([P, GB, E]),
                                                ALU.subtract).then_inc(lgx_ready, 1)
                        dve.wait_ge(lg_out, g - 1)
                        chain.link(nc.vector.tensor_reduce(lsum[:], lgx[:], AXX, ALU.add))
                        chain.link(nc.vector.reciprocal(lmax[:], lsum[:]))
                        chain.link(nc.vector.tensor_tensor(lgx[:], lgx[:], lmax[:].unsqueeze(2).to_broadcast([P, GB, E]), ALU.mult))
                        chain.link(nc.vector.tensor_copy(c["aff"][:, bass.ds((g - 2) * (GB * E), GB * E)],
                                                         lgx[:].rearrange("p b e -> p (b e)")))
                    if has_a and s == A_XT:
                        for ch in range(DC):
                            dve.wait_ge(xnhi_ready, g * 2 + ch + 1)
                            nc.vector.tensor_tensor(xnlo[:, ch, :], m_ps[ch][:], xnhi[:, ch, :], ALU.subtract).then_inc(xn_split, 1)
                    if has_a and s == A_Q:
                        for ch in range(DC):
                            dve.wait_ge(qhi_ready, g * 2 + ch + 1)
                            nc.vector.scalar_tensor_tensor(out=qlo[:, par, ch, :], in0=m_ps[ch][:], scalar=bqk[:, 0, ch:ch + 1],
                                                           in1=qhi[:, par, ch, :], op0=ALU.add, op1=ALU.subtract).then_inc(q_split, 1)
                    if has_a and s == A_K:
                        for ch in range(DC):
                            dve.wait_ge(khi_ready, g * 2 + ch + 1)
                            nc.vector.scalar_tensor_tensor(out=kk[:, 1, ch, :], in0=m_ps[ch][:], scalar=bqk[:, 1, ch:ch + 1],
                                                           in1=kk[:, 0, ch, :], op0=ALU.add, op1=ALU.subtract).then_inc(k_split, 1)
                    if has_a and s in (A_V + 1, A_V + 3):
                        n = (s - A_V) // 2
                        chain = Chain(dve, v_link, (g * 2 + n) * 4)
                        dve.wait_ge(v_full, g * 2 + n + 1)
                        part = [v3[:, par, 2 * n:2 * n + 2, :, i, :].rearrange("p b h d -> p (b h) d") for i in range(3)]
                        flat = lambda t: t[:].rearrange("p b (h d) -> p (b h) d", d=DH)
                        chain.link(nc.vector.tensor_tensor(v32[:], m_ps[n][:].rearrange("p (b d) -> p b d", b=2),
                                                           bvo[:, 0:1, :].to_broadcast([P, 2, D]), ALU.add))
                        chain.link(nc.vector.tensor_copy(part[0], flat(v32)))
                        chain.link(nc.vector.tensor_tensor(flat(vr), flat(v32), part[0], ALU.subtract))
                        chain.link(nc.vector.tensor_copy(part[1], flat(vr)))
                        nc.vector.tensor_tensor(part[2], flat(vr), part[1], ALU.subtract).then_inc(v_ready, 1)

            steps(dve, step)


def gather(nc, c, a, xln_dram, rows_dram):
    with ExitStack() as ctx:
        r = Room(nc, ctx, "g")
        work = r.sb("work", [P, RT, S], F32)
        top = r.sb("top", [P, RT, 8], F32)
        sel = r.sb("sel", [P, RT, S], F32)
        ones = r.sb("ones", [P, S], F32)
        rank = r.sb("rank", [P, RT, S], F32)
        pos = r.sb("pos", [P, B * E], F32)
        aff3 = r.sb("aff3", [P, B, 3, E], BF16)
        rest = r.sb("rest", [P, B, E], F32)
        aff_now = r.sb("aff_now", [P, 2, GB, 3, E], BF16)
        xg = r.sb("xg", [P, 2, GB, D], F32)
        xhi = r.sb("xhi", [P, GB, D], F32R)
        xlo = r.sb("xlo", [P, GB, D], F32R)
        hot = r.sb("hot", [P, 2, GB, E, K], F32R)
        hotb = r.sb("hotb", [P, GB, E, K], BF16)
        gsel = r.sb("gsel", [P, GB * DC, 3 * E], F32)
        ghi = r.sb("ghi", [P, 2, DC, E, GB, K], F32R)
        glo = r.sb("glo", [P, 2, DC, E, GB, K], F32R)
        t_ps = r.ps("t", [P, RT, S], F32)
        hT_ps = r.ps("hT", [P, GB, DC, P], BF16)
        g_ps = r.ps("g", [P, GB * DC, 3 * E], F32)
        x_ps = [r.ps(f"x{i}", [P, 2, E, K], F32) for i in range(4)]
        link, tr_full, pos_full, pos_out, aff_split = (r.sem(n) for n in ("link", "tr_full", "pos_full", "pos_out", "aff_split"))
        rank_ready = r.sem("rank_ready")
        x_loaded = [r.sem("x_loaded0"), r.sem("x_loaded1")]
        xhi_ready, xlo_ready, hot_ready, hotb_ready = (r.sem(n) for n in ("xhi_ready", "xlo_ready", "hot_ready", "hotb_ready"))
        hT_full, hT_out, g_full, g_read, g_out, g_link = (r.sem(n) for n in ("hT_full", "hT_out", "g_full", "g_read", "g_out", "g_link"))
        x_full, ghi_ready, glo_ready = r.sem("x_full"), r.sem("ghi_ready"), r.sem("glo_ready")
        stored = [r.sem("stored0"), r.sem("stored1")]
        xln_v = xln_dram.rearrange("(g b) p d -> g p b d", b=GB)
        block = ctx.enter_context(nc.Block())

        def pairs(eng, step):
            step(0, 0)
            step(1, 1)
            with eng.Fori(1, G // 2) as i:
                step(i * 2, 0)
                step(i * 2 + 1, 1)

        def later(g):
            return not isinstance(g, int) or g > 1

        @block.sync
        def _(sp):
            def load(g, par):
                sp.dma_start(xg[:, par], xln_v[g]).then_inc(x_loaded[par], 16)

            load(0, 0)
            load(1, 1)

            def step(g, par):
                sp.wait_ge(ghi_ready, (g + 1) * 4)
                sp.wait_ge(glo_ready, (g + 1) * 4)
                for x, t in ((0, ghi), (1, glo)):
                    for ch in range(DC):
                        dst = rows_dram[x, ch, g].rearrange("e p n -> p e n")
                        sp.dma_start(dst, raw(t[:, par, ch]).rearrange("p e b k -> p e (b k)")).then_inc(stored[par], 16)

            def step_and_load(g, par):
                step(g, par)
                load(g + 2, par)

            step_and_load(0, 0)
            step_and_load(1, 1)
            with sp.Fori(1, G // 2 - 1) as i:
                step_and_load(i * 2, 0)
                step_and_load(i * 2 + 1, 1)
            step(G - 2, 0)
            step(G - 1, 1)
            for par in range(2):
                sp.wait_ge(stored[par], 16 * 4 * G // 2)

        @block.tensor
        def _(pe):
            for t in range(RT):
                last = nc.tensor.transpose(t_ps[:, t, :], c["aff"][:, t * P:(t + 1) * P], c["id32"][:])
            last.then_inc(tr_full, 1)
            pe.wait_ge(rank_ready, 1)
            for t in range(RT):
                last = nc.tensor.transpose(t_ps[:, t, :], rank[:, t, :], c["id32"][:])
            last.then_inc(pos_full, 1)

            def step(g, par):
                pe.wait_ge(hot_ready, g + 1)
                pe.wait_ge(xlo_ready, g + 1)
                for ch in range(DC):
                    for n in range(2):
                        bank = x_ps[ch * 2 + n]
                        if not isinstance(g, int) or g > 0:
                            pe.wait_ge(glo_ready, (g - 1) * 4 + ch * 2 + n + 1)
                        for b in range(2):
                            for part, x in enumerate((xhi, xlo)):
                                last = nc.tensor.matmul(bank[:, b].rearrange("p e k -> p (e k)"),
                                                        x[:, 2 * n + b, ch * P:(ch + 1) * P],
                                                        hot[:, par, 2 * n + b].rearrange("p e k -> p (e k)"),
                                                        start=(part == 0), stop=(part == 1))
                        last.then_inc(x_full, 1)
                pe.wait_ge(hotb_ready, g + 1)
                if not isinstance(g, int) or g > 0:
                    pe.wait_ge(hT_out, g)
                    pe.wait_ge(g_read, g)
                for b in range(GB):
                    for half in range(DC):
                        last = nc.tensor.transpose(hT_ps[:, b, half, :],
                                                   hotb[:, b, half * EC:(half + 1) * EC, :].rearrange("p e k -> p (e k)"), c["idb"][:])
                last.then_inc(hT_full, 1)
                for b in range(GB):
                    for half in range(DC):
                        last = nc.tensor.matmul(g_ps[:, b * DC + half, :],
                                                hotb[:, b, half * EC:(half + 1) * EC, :].rearrange("p e k -> p (e k)"),
                                                aff_now[:, par, b].rearrange("p n e -> p (n e)"), start=True, stop=True)
                last.then_inc(g_full, 1)

            pairs(pe, step)

        @block.scalar
        def _(act):
            def step(g, par):
                act.wait_ge(x_loaded[par], (g - par) * 8 + 16)
                if not isinstance(g, int) or g > 0:
                    act.wait_ge(x_full, g * 4)
                nc.scalar.activation(xhi[:], xg[:, par], ACT.Copy).then_inc(xhi_ready, 1)
                act.wait_ge(hot_ready, g + 1)
                if not isinstance(g, int) or g > 0:
                    act.wait_ge(g_full, g)
                nc.scalar.activation(hotb[:], hot[:, par].bitcast(F32), ACT.Copy).then_inc(hotb_ready, 1)
                for ch in range(DC):
                    for n in range(2):
                        act.wait_ge(x_full, g * 4 + ch * 2 + n + 1)
                        if later(g) and ch == 0 and n == 0:
                            act.wait_ge(stored[par], (g - par) * 32)
                        nc.scalar.activation(ghi[:, par, ch, :, 2 * n:2 * n + 2, :].rearrange("p e b k -> p b e k"),
                                             x_ps[ch * 2 + n][:], ACT.Copy).then_inc(ghi_ready, 1)
                act.wait_ge(hT_full, g + 1)
                nc.scalar.activation(c["onehotT"][:, bass.ds(g * GB, GB)], hT_ps[:], ACT.Copy).then_inc(hT_out, 1)

            pairs(act, step)

        @block.gpsimd
        def _(pool):
            def step(g, par):
                pool.wait_ge(xhi_ready, g + 1)
                nc.gpsimd.tensor_tensor(xlo[:], xg[:, par], xhi[:], ALU.subtract).then_inc(xlo_ready, 1)

            pairs(pool, step)

        @block.vector
        def _(dve):
            chain = Chain(dve, link)
            aff = c["aff"][:].rearrange("p (b e) -> p b e", e=E)
            chain.link(nc.vector.tensor_copy(aff3[:, :, 0, :], aff))
            chain.link(nc.vector.tensor_tensor(rest[:], aff, aff3[:, :, 0, :], ALU.subtract))
            chain.link(nc.vector.tensor_copy(aff3[:, :, 1, :], rest[:]))
            chain.link(nc.vector.tensor_tensor(aff3[:, :, 2, :], rest[:], aff3[:, :, 1, :], ALU.subtract))
            chain.link(nc.vector.memset(ones[:], 1.0))
            dve.wait_ge(tr_full, 1)
            chain.link(nc.vector.tensor_copy(work[:], t_ps[:]))
            for _ in range(K // 8):
                for t in range(RT):
                    chain.mark(nc.vector.max(top[:, t, :], work[:, t, :]))
                chain.settle()
                for t in range(RT):
                    chain.mark(nc.vector.match_replace(work[:, t, :], top[:, t, :], work[:, t, :], -1.0))
                chain.settle()
            chain.link(nc.vector.tensor_scalar(sel[:], work[:], 0.0, None, ALU.is_lt))
            for t in range(RT):
                chain.mark(nc.vector.tensor_tensor_scan(rank[:, t, :], ones[:], sel[:, t, :], 0.0, ALU.mult, ALU.add))
            chain.settle()
            chain.link(nc.vector.tensor_tensor(rank[:], rank[:], sel[:], ALU.mult))
            nc.vector.tensor_scalar(rank[:], rank[:], -1.0, None, ALU.add).then_inc(rank_ready, 1)
            dve.wait_ge(pos_full, 1)
            chain.link(nc.vector.tensor_copy(pos[:], t_ps[:].rearrange("p t n -> p (t n)")))

            def step(g, par):
                if later(g):
                    dve.wait_ge(g_full, g - 1)
                nc.vector.tensor_copy(aff_now[:, par], aff3[:, bass.ds(g * GB, GB)]).then_inc(g_link, 1)
                nc.vector.tensor_tensor(hot[:, par].rearrange("p b e k -> p (b e) k"),
                                        pos[:, bass.ds(g * (GB * E), GB * E)].unsqueeze(2).to_broadcast([P, GB * E, K]),
                                        c["slot"][:].unsqueeze(1).to_broadcast([P, GB * E, K]), ALU.is_equal).then_inc(hot_ready, 1)
                for ch in range(DC):
                    for n in range(2):
                        dve.wait_ge(ghi_ready, g * 4 + ch * 2 + n + 1)
                        nc.vector.tensor_tensor(glo[:, par, ch, :, 2 * n:2 * n + 2, :].rearrange("p e b k -> p b e k"),
                                                x_ps[ch * 2 + n][:],
                                                ghi[:, par, ch, :, 2 * n:2 * n + 2, :].rearrange("p e b k -> p b e k"),
                                                ALU.subtract).then_inc(glo_ready, 1)
                dve.wait_ge(g_full, g + 1)
                if not isinstance(g, int) or g > 0:
                    dve.wait_ge(g_out, g)
                nc.vector.tensor_tensor(gsel[:].rearrange("p (b h) n -> p b h n", h=DC),
                                        g_ps[:].rearrange("p (b h) n -> p b h n", h=DC),
                                        c["own"][:].rearrange("p h n e -> p h (n e)").unsqueeze(1).to_broadcast([P, GB, DC, 3 * E]),
                                        ALU.mult).then_inc(g_read, 1)
                dve.wait_ge(g_read, g + 1)
                nc.vector.tensor_reduce(c["gating"][:, bass.ds(g * GB, GB), :].rearrange("p b h -> p (b h)"),
                                        gsel[:], AXX, ALU.add).then_inc(g_out, 1)

            pairs(dve, step)


def experts(nc, c, a, rows_dram, out_dram):
    with ExitStack() as ctx:
        r = Room(nc, ctx, "e")
        WK = ("g", "u", "d")
        shape = {"g": [P, DC, FF], "u": [P, DC, FF], "d": [P, FC, D]}
        stage = r.sb("stage", [P, DC * FF], F32)
        whi = [{k: r.sb(f"w{k}hi{i}", shape[k], F32R) for k in WK} for i in range(2)]
        wlo = [{k: r.sb(f"w{k}lo{i}", shape[k], F32R) for k in WK} for i in range(2)]
        xr = r.sb("xr", [P, 2, 2, DC, 512], F32R)
        sg = r.sb("sg", [P, 2, 512], F32)
        hh = r.sb("hh", [P, 2, 512], F32)
        hhi = r.sb("hhi", [P, 2, 512], F32R)
        hlo = r.sb("hlo", [P, 2, 512], F32R)
        yT = r.sb("yT", [P, DC, 512], F32)
        yr = r.sb("yr", [P, 4, D], F32)
        g_ps = [r.ps(f"g{i}", [P, 512], F32) for i in range(2)]
        u_ps = [r.ps(f"u{i}", [P, 512], F32) for i in range(2)]
        y_ps = [r.ps(f"y{i}", [P, 512], F32) for i in range(DC)]
        t_ps = [r.ps(f"t{i}", [P, 2, D], F32) for i in range(2)]
        w_loaded, w_hi, w_split = r.sem("w_loaded"), r.sem("w_hi"), r.sem("w_split")
        x_loaded = [r.sem("x_loaded0"), r.sem("x_loaded1")]
        g_full, u_full, sg_ready, hh_ready, hhi_ready, h_ready = (
            r.sem(n) for n in ("g_full", "u_full", "sg_ready", "hh_ready", "hhi_ready", "h_ready"))
        h_used, y_out, t_full, t_out, stored = (r.sem(n) for n in ("h_used", "y_out", "t_full", "t_out", "stored"))

        w_view = {
            "g": a["wgT"].rearrange("e (c p) i -> e p c i", p=P),
            "u": a["wuT"].rearrange("e (c p) i -> e p c i", p=P),
            "d": a["wdT"].rearrange("e (c p) d -> e p c d", p=P),
        }
        NG = T // S

        def turns(eng, expert):
            expert(0, 0)
            expert(1, 1)
            with eng.Fori(1, E // 2) as i:
                expert(i * 2, 0)
                expert(i * 2 + 1, 1)

        block = ctx.enter_context(nc.Block())

        def later(e, n=0):
            return not isinstance(e, int) or e > n

        @block.sync
        def _(sp):
            def load_weights(e, n):
                k = WK[n]
                if later(e) or n:
                    sp.wait_ge(w_split, e * 3 + n)
                sp.dma_start(stage[:].rearrange("p (c i) -> p c i", c=shape[k][1]), w_view[k][e]).then_inc(w_loaded, 16)

            def chunk_in(e, n):
                for x in range(2):
                    for ch in range(DC):
                        src = rows_dram[x, ch, n * NG:(n + 1) * NG, e].rearrange("g p k -> p g k")
                        sp.dma_start(raw(xr[:, n % 2, x, ch, :]).rearrange("p (g k) -> p g k", g=NG), src).then_inc(x_loaded[n % 2], 16)

            def chunk_out(e, n):
                sp.wait_ge(t_out, (e * NT + n) * 2 + 2)
                for g in range(4):
                    b0 = n * RB + g * 4
                    for b in range(4):
                        sp.dma_start(out_dram[b0 + b, e], yr[b * K:(b + 1) * K, g, :]).then_inc(stored, 16)

            def expert(e, par):
                for n in range(NT):
                    t = e * NT + n
                    if later(e) or n >= 2:
                        sp.wait_ge(u_full, (t - 1) * FC)
                    chunk_in(e, n)
                    if later(e) or n:
                        if n:
                            chunk_out(e, n - 1)
                        else:
                            chunk_out(e - 1, NT - 1)
                    if n < 3 and not (isinstance(e, int) and e == E - 1):
                        load_weights(e + 1, n)

            for n in range(3):
                load_weights(0, n)
            expert(0, 0)
            expert(1, 1)
            with sp.Fori(1, E // 2 - 1) as i:
                expert(i * 2, 0)
                expert(i * 2 + 1, 1)
            expert(E - 2, 0)
            expert(E - 1, 1)
            chunk_out(E - 1, NT - 1)
            sp.wait_ge(stored, 16 * 16 * NT * E)

        @block.tensor
        def _(pe):
            def expert(e, par):
                hi, lo = whi[par], wlo[par]
                pe.wait_ge(w_split, (e + 1) * 3)

                def down(n, j):
                    t = (e * NT + n) * FC + j
                    pe.wait_ge(h_ready, t + 1)
                    pe.wait_ge(hhi_ready, t + 1)
                    if j == 0 and (later(e) or n):
                        pe.wait_ge(y_out, (e * NT + n) * 2)
                    for d in range(DC):
                        w1, w2 = hi["d"][:, j, d * P:(d + 1) * P], lo["d"][:, j, d * P:(d + 1) * P]
                        nc.tensor.matmul(y_ps[d][:], w1, hhi[:, j % 2, :], start=(j == 0), stop=False)
                        nc.tensor.matmul(y_ps[d][:], w1, hlo[:, j % 2, :], start=False, stop=False)
                        last = nc.tensor.matmul(y_ps[d][:], w2, hhi[:, j % 2, :], start=False, stop=(j == FC - 1))
                    last.then_inc(h_used, 1)

                def rows(n):
                    t = e * NT + n
                    pe.wait_ge(y_out, (t + 1) * 2)
                    for g in range(4):
                        if g % 2 == 0 and (later(e) or n):
                            pe.wait_ge(t_out, (t - 1) * 2 + g // 2 + 1)
                        for d in range(DC):
                            last = nc.tensor.transpose(t_ps[g // 2][:, g % 2, d * P:(d + 1) * P], yT[:, d, g * P:(g + 1) * P], c["id32"][:])
                        if g % 2:
                            last.then_inc(t_full, 1)

                for n in range(NT):
                    t0 = (e * NT + n) * FC
                    pe.wait_ge(x_loaded[n % 2], (e * (NT // 2) + n // 2 + 1) * 64)
                    for j in range(FC):
                        i = slice(j * P, (j + 1) * P)
                        if later(e) or n or j >= 2:
                            pe.wait_ge(hh_ready, t0 + j - 1)
                        for k, banks, full in (("g", g_ps, g_full), ("u", u_ps, u_full)):
                            for ch in range(DC):
                                nc.tensor.matmul(banks[j % 2][:], hi[k][:, ch, i], xr[:, n % 2, 0, ch, :], start=(ch == 0), stop=False)
                                nc.tensor.matmul(banks[j % 2][:], hi[k][:, ch, i], xr[:, n % 2, 1, ch, :], start=False, stop=False)
                                last = nc.tensor.matmul(banks[j % 2][:], lo[k][:, ch, i], xr[:, n % 2, 0, ch, :], start=False,
                                                        stop=(ch == DC - 1))
                            last.then_inc(full, 1)
                        if j:
                            down(n, j - 1)
                        if j == 1 and n:
                            rows(n - 1)
                    down(n, FC - 1)
                rows(NT - 1)

            turns(pe, expert)

        @block.scalar
        def _(act):
            def split_hi(e, par, n):
                k = WK[n]
                act.wait_ge(w_loaded, (e * 3 + n + 1) * 16)
                if n == 0 and later(e, 1):
                    act.wait_ge(h_used, (e - 1) * NT * FC)
                nc.scalar.activation(whi[par][k][:], stage[:].rearrange("p (c i) -> p c i", c=shape[k][1]), ACT.Copy).then_inc(w_hi, 1)

            def expert(e, par):
                for n in range(NT):
                    for j in range(FC):
                        t = (e * NT + n) * FC + j
                        act.wait_ge(g_full, t + 1)
                        if later(e) or n or j >= 2:
                            act.wait_ge(hh_ready, t - 1)
                        nc.scalar.activation(sg[:, j % 2, :], g_ps[j % 2][:], ACT.Silu).then_inc(sg_ready, 1)
                        if n < 3 and j == 4 and not (isinstance(e, int) and e == E - 1):
                            split_hi(e + 1, 1 - par, n)
                    act.wait_ge(h_used, (e * NT + n + 1) * FC)
                    if later(e) or n:
                        act.wait_ge(t_full, (e * NT + n) * 2)
                    for d in range(DC):
                        nc.scalar.activation(yT[:, d, :], y_ps[d][:], ACT.Copy).then_inc(y_out, 1)

            for n in range(3):
                split_hi(0, 0, n)
            expert(0, 0)
            expert(1, 1)
            with act.Fori(1, E // 2 - 1) as i:
                expert(i * 2, 0)
                expert(i * 2 + 1, 1)
            expert(E - 2, 0)
            expert(E - 1, 1)

        @block.vector
        def _(dve):
            def split_lo(e, par, n):
                k = WK[n]
                dve.wait_ge(w_hi, e * 3 + n + 1)
                nc.vector.tensor_tensor(wlo[par][k][:], stage[:].rearrange("p (c i) -> p c i", c=shape[k][1]), whi[par][k][:],
                                        ALU.subtract).then_inc(w_split, 1)

            def rows_out(e, n):
                for g in range(2):
                    t = (e * NT + n) * 2 + g
                    dve.wait_ge(t_full, t + 1)
                    if g == 0 and (later(e) or n):
                        dve.wait_ge(stored, (e * NT + n) * 16 * 16)
                    nc.vector.tensor_copy(yr[:, 2 * g:2 * g + 2, :], t_ps[g][:]).then_inc(t_out, 1)

            def expert(e, par):
                for n in range(NT):
                    for j in range(FC):
                        t = (e * NT + n) * FC + j
                        dve.wait_ge(sg_ready, t + 1)
                        dve.wait_ge(u_full, t + 1)
                        if later(e) or n or j >= 2:
                            dve.wait_ge(h_used, t - 1)
                        nc.vector.tensor_tensor(hh[:, j % 2, :], u_ps[j % 2][:], sg[:, j % 2, :], ALU.mult).then_inc(hh_ready, 1)
                        dve.wait_ge(hh_ready, t + 1)
                        nc.vector.tensor_copy(hhi[:, j % 2, :], hh[:, j % 2, :]).then_inc(hhi_ready, 1)
                        dve.wait_ge(hhi_ready, t + 1)
                        nc.vector.tensor_tensor(hlo[:, j % 2, :], hh[:, j % 2, :], hhi[:, j % 2, :], ALU.subtract).then_inc(h_ready, 1)
                        if n < 3 and j == 5 and not (isinstance(e, int) and e == E - 1):
                            split_lo(e + 1, 1 - par, n)
                        if n and j == 2:
                            rows_out(e, n - 1)
                rows_out(e, NT - 1)

            for n in range(3):
                split_lo(0, 0, n)
            expert(0, 0)
            expert(1, 1)
            with dve.Fori(1, E // 2 - 1) as i:
                expert(i * 2, 0)
                expert(i * 2 + 1, 1)
            expert(E - 2, 0)
            expert(E - 1, 1)


def combine(nc, c, a, x2_dram, rows_out_dram, y_dram):
    CB = 2
    with ExitStack() as ctx:
        r = Room(nc, ctx, "o")
        rows = r.sb("rows", [P, 2, CB, DC, D], F32)
        xres = r.sb("xres", [P, 2, CB, D], F32)
        rhi = r.sb("rhi", [P, 2, CB, DC, D], F32R)
        rlo = r.sb("rlo", [P, 2, CB, DC, D], F32R)
        hot = r.sb("hot", [P, 2, CB, DC, S], F32R)
        gate = r.sb("gate", [P, 2, CB, DC], F32)
        y = r.sb("y", [P, 2, CB, D], F32)
        ps = [r.ps(f"ps{i}", [P, CB, D], F32) for i in range(2)]
        loaded = [r.sem("loaded0"), r.sem("loaded1")]
        res_loaded = [r.sem("res_loaded0"), r.sem("res_loaded1")]
        stored = [r.sem("stored0"), r.sem("stored1")]
        gate_ready, hi_ready, lo_ready, hot_ready, full, y_ready = (
            r.sem(n) for n in ("gate_ready", "hi_ready", "lo_ready", "hot_ready", "full", "y_ready"))
        rows_v = rows_out_dram.rearrange("(n b) (h e) k d -> n (e k) b h d", b=CB, e=EC)
        x2_v = x2_dram.rearrange("(n b) p d -> n p b d", b=CB)
        y_v = y_dram.rearrange("(n b) p d -> n p b d", b=CB)
        N = B // CB
        block = ctx.enter_context(nc.Block())

        def pairs(eng, step):
            step(0, 0)
            step(1, 1)
            with eng.Fori(1, N // 2) as i:
                step(i * 2, 0)
                step(i * 2 + 1, 1)

        def later(n, k=0):
            return not isinstance(n, int) or n > k

        @block.sync
        def _(sp):
            def step(n, par):
                if later(n, 1):
                    sp.wait_ge(lo_ready, n - 1)
                    sp.wait_ge(y_ready, n - 1)
                sp.dma_start(rows[:, par], rows_v[n]).then_inc(loaded[par], 16)
                sp.dma_start(xres[:, par], x2_v[n]).then_inc(res_loaded[par], 16)

            pairs(sp, step)

        @block.gpsimd
        def _(pool):
            def step(n, par):
                if later(n, 1):
                    pool.wait_ge(full, n - 1)
                nc.gpsimd.tensor_copy(hot[:, par], c["onehotT"][:, bass.ds(n * CB, CB)]).then_inc(hot_ready, 1)

            pairs(pool, step)

        @block.scalar
        def _(act):
            def step(n, par):
                act.wait_ge(gate_ready, n + 1)
                act.wait_ge(loaded[par], (n - par) * 8 + 16)
                if later(n, 1):
                    act.wait_ge(full, n - 1)
                for b in range(CB):
                    for h in range(DC):
                        last = nc.scalar.activation(rhi[:, par, b, h, :], rows[:, par, b, h, :], ACT.Copy,
                                                    scale=gate[:, par, b, h:h + 1])
                last.then_inc(hi_ready, 1)
                act.wait_ge(y_ready, n + 1)
                act.dma_start(y_v[n], y[:, par]).then_inc(stored[par], 16)

            pairs(act, step)
            for par in range(2):
                act.wait_ge(stored[par], 16 * N // 2)

        @block.tensor
        def _(pe):
            def step(n, par):
                pe.wait_ge(hot_ready, n + 1)
                pe.wait_ge(lo_ready, n + 1)
                if later(n, 1):
                    pe.wait_ge(y_ready, n - 1)
                for b in range(CB):
                    for h in range(DC):
                        for part, x in enumerate((rhi, rlo)):
                            last = nc.tensor.matmul(ps[par][:, b, :], hot[:, par, b, h, :], x[:, par, b, h, :],
                                                    start=(h == 0 and part == 0), stop=(h == DC - 1 and part == 1))
                last.then_inc(full, 1)

            pairs(pe, step)

        @block.vector
        def _(dve):
            def step(n, par):
                if later(n, 1):
                    dve.wait_ge(lo_ready, n - 1)
                    dve.wait_ge(hi_ready, n - 1)
                nc.vector.tensor_copy(gate[:, par], c["gating"][:, bass.ds(n * CB, CB), :]).then_inc(gate_ready, 1)
                dve.wait_ge(hi_ready, n + 1)
                for b in range(CB):
                    for h in range(DC):
                        last = nc.vector.scalar_tensor_tensor(out=rlo[:, par, b, h, :], in0=rows[:, par, b, h, :],
                                                              scalar=gate[:, par, b, h:h + 1], in1=rhi[:, par, b, h, :],
                                                              op0=ALU.mult, op1=ALU.subtract)
                last.then_inc(lo_ready, 1)
                dve.wait_ge(full, n + 1)
                dve.wait_ge(res_loaded[par], (n - par) * 8 + 16)
                if later(n, 1):
                    dve.wait_ge(stored[par], (n - par) * 8)
                nc.vector.scalar_tensor_tensor(out=y[:, par], in0=ps[par][:], scalar=c["tg"][:, 1:2], in1=xres[:, par],
                                               op0=ALU.mult, op1=ALU.add).then_inc(y_ready, 1)

            pairs(dve, step)


def program(nc, a, y_dram):
    x2_dram = nc.dram_tensor("x2_scratch", [B, S, D], F32, kind="Internal").ap()
    xln_dram = nc.dram_tensor("xln_scratch", [B, S, D], F32, kind="Internal").ap()
    rows_in = nc.dram_tensor("rows_in", [2, DC, G, E, P, GB * K], F32, kind="Internal").ap()
    rows_out = nc.dram_tensor("rows_out", [B, E, K, D], F32, kind="Internal").ap()
    with ExitStack() as ctx:
        keep = Room(nc, ctx, "keep")
        c = constants(nc, keep, a)
        attention(nc, c, a, x2_dram, xln_dram)
        c["onehotT"] = keep.sb("onehotT", [P, B, DC, S], BF16)
        gather(nc, c, a, xln_dram, rows_in)
        experts(nc, c, a, rows_in, rows_out)
        combine(nc, c, a, x2_dram, rows_out, y_dram)


def kernel(x, ctx_1024, mask_BxSxS2_ff1, g_xattn, g_ffn, L0_xattn_Wq, L0_xattn_bq, L0_xattn_Wk, L0_xattn_bk,
           L0_xattn_Wv, L0_xattn_bv, L0_xattn_Wo, L0_xattn_bo, L0_ffn_gate_w, L0_ffn_w_gate, L0_ffn_w_up, L0_ffn_w_down):
    import numpy as np
    import concourse.bacc as bacc
    from concourse.bass_utils import run_bass_kernel_spmd

    n = np.asarray
    arrays = {
        "x": n(x), "ctxT": n(ctx_1024).reshape(B * S, D).T, "mask": n(mask_BxSxS2_ff1), "g_xattn": n(g_xattn), "g_ffn": n(g_ffn),
        "wqT": n(L0_xattn_Wq).T, "wkT": n(L0_xattn_Wk).T, "wvT": n(L0_xattn_Wv).T, "woT": n(L0_xattn_Wo).T,
        "bq": n(L0_xattn_bq), "bk": n(L0_xattn_bk), "bv": n(L0_xattn_bv), "bo": n(L0_xattn_bo),
        "gateT": n(L0_ffn_gate_w).T, "wgT": n(L0_ffn_w_gate).transpose(0, 2, 1), "wuT": n(L0_ffn_w_up).transpose(0, 2, 1),
        "wdT": n(L0_ffn_w_down).transpose(0, 2, 1),
    }
    arrays = {k: np.ascontiguousarray(v) for k, v in arrays.items()}
    nc = bacc.Bacc("TRN2", target_bir_lowering=False, num_devices=1)
    aps = {k: nc.dram_tensor(k, v.shape, mybir.dt.from_np(v.dtype), kind="ExternalInput").ap() for k, v in arrays.items()}
    y = nc.dram_tensor("y", (B, S, D), F32, kind="ExternalOutput").ap()
    program(nc, aps, y)
    out = run_bass_kernel_spmd(nc, [arrays], core_ids=[0])
    return out.results[0]["y"]
```

```python
from contextlib import ExitStack

import concourse.bass as bass
from concourse import mybir

F32 = mybir.dt.float32
F32R = mybir.dt.float32r
F16 = mybir.dt.float16
BF16 = mybir.dt.bfloat16
ALU = mybir.AluOpType
ACT = mybir.ActivationFunctionType
AXX = mybir.AxisListType.X

B, S, D = 64, 128, 256
H, DH = 16, 16
E, FF, K = 8, 1024, 32
P = 128
DC = D // P
FC = FF // P
GB = 4
G = B // GB
T = GB * S
HU = 4
UB = H // HU
U = GB * UB
HC = P // DH
VP = 3 * DH
EPS = 1e-5
RB = P // E
RT = B // RB
EC = P // K
SLOTS = B * K
NT = SLOTS // 512


class Chain:

    def __init__(self, eng, sem, base=0):
        self.eng, self.sem, self.base, self.n = eng, sem, base, 0

    def mark(self, ins):
        self.n += 1
        ins.then_inc(self.sem, 1)

    def settle(self):
        self.eng.wait_ge(self.sem, self.base + self.n)

    def link(self, ins):
        self.mark(ins)
        self.settle()


class Room:

    def __init__(self, nc, ctx, tag):
        self.nc, self.ctx, self.tag = nc, ctx, tag

    def sb(self, name, shape, dt):
        return self.ctx.enter_context(self.nc.sbuf_tensor(f"{self.tag}_{name}", shape, dt))

    def ps(self, name, shape, dt):
        return self.ctx.enter_context(self.nc.psum_tensor(f"{self.tag}_{name}", shape, dt))

    def sem(self, name):
        return self.ctx.enter_context(self.nc.semaphore(f"{self.tag}_{name}"))


def raw(ap):
    return ap.bitcast(F32)


def constants(nc, keep, a):
    c = {
        "id32": keep.sb("id32", [P, P], F32),
        "id16": keep.sb("id16", [P, P], F16),
        "idb": keep.sb("idb", [P, P], BF16),
        "slot": keep.sb("slot", [P, K], F32),
        "own": keep.sb("own", [P, DC, 3, E], F32),
        "tg": keep.sb("tg", [P, 2], F32),
        "aff": keep.sb("aff", [P, B * E], F32),
        "gating": keep.sb("gating", [P, B, DC], F32),
    }
    with ExitStack() as ctx:
        r = Room(nc, ctx, "c")
        g = r.sb("g", [P, 2], F32)
        loaded, pooled, pool_link = r.sem("loaded"), r.sem("pooled"), r.sem("pool_link")
        block = ctx.enter_context(nc.Block())

        @block.sync
        def _(sp):
            sp.dma_start(g[:, 0:1], a["g_xattn"].partition_broadcast(P)).then_inc(loaded, 16)
            sp.dma_start(g[:, 1:2], a["g_ffn"].partition_broadcast(P)).then_inc(loaded, 16)

        @block.scalar
        def _(act):
            act.wait_ge(loaded, 32)
            nc.scalar.activation(c["tg"][:], g[:], ACT.Tanh).then_inc(pooled, 1)

        @block.gpsimd
        def _(pool):
            chain = Chain(pool, pool_link)
            for name in ("id32", "id16", "idb"):
                chain.mark(nc.gpsimd.memset(c[name][:], 0.0))
            chain.mark(nc.gpsimd.memset(c["own"][:], 1.0))
            chain.mark(nc.gpsimd.iota(c["slot"][:], pattern=[[1, K]], base=0, channel_multiplier=0,
                                      allow_small_or_imprecise_dtypes=True))
            chain.settle()
            for name in ("id32", "id16", "idb"):
                chain.mark(nc.gpsimd.affine_select(out=c[name][:], in_=c[name][:], compare_op=ALU.not_equal, fill=1.0,
                                                   base=0, pattern=[[-1, P]], channel_multiplier=1))
            for half in range(DC):
                v = c["own"][:, half, :, :]
                for sign, base in ((1, K * EC * half), (-1, K - 1 - K * EC * half)):
                    chain.link(nc.gpsimd.affine_select(out=v, in_=v, compare_op=ALU.is_ge, fill=0.0, base=base,
                                                       pattern=[[0, 3], [-sign * K, E]], channel_multiplier=sign))
            chain.settle()
    return c


LE, LH, LO, LT, LP, LD = 0, 2, 2, 4, 5, 6


def attention(nc, c, a, x2_dram, xln_dram):
    with ExitStack() as ctx:
        r = Room(nc, ctx, "a")
        WN = ("q", "k", "v", "o")
        wraw = r.sb("wraw", [P, DC, D], F32)
        whi = {n: r.sb(f"w{n}hi", [P, DC, D], F32R) for n in WN}
        wlo = {n: r.sb(f"w{n}lo", [P, DC, D], F32R) for n in WN}
        gateT = r.sb("gateT", [P, DC, E], F32)
        bqk = r.sb("bqk", [P, 2, DC], F32)
        bvo = r.sb("bvo", [P, 2, D], F32)
        minus_half = r.sb("minus_half", [P, GB], F32)
        after = r.sb("after", [P, 4], F32)
        eps = r.sb("eps", [P, GB], F32)
        x_in = r.sb("x_in", [P, GB, D], F32)
        x_res = r.sb("x_res", [P, GB, D], F32)
        yT = r.sb("yT", [P, DC, T], F32)
        yhi = r.sb("yhi", [P, DC, T], F32R)
        ylo = r.sb("ylo", [P, DC, T], F32R)
        mask = wraw[:].rearrange("p c n -> p (c n)").rearrange("p (b q) -> p b q", b=GB)
        far = r.sb("far", [P, 2, GB, S], F32)
        stats = r.sb("stats", [P, 2, GB, 6], F32)
        mv = r.sb("mv", [P, 2, GB, 2], F32)
        rstd = r.sb("rstd", [P, 2, GB], F32)
        xn = r.sb("xn", [P, GB, D], F32)
        xnhi = r.sb("xnhi", [P, DC, T], F32R)
        xnlo = r.sb("xnlo", [P, DC, T], F32R)
        qhi = r.sb("qhi", [P, 2, DC, T], F32R)
        qlo = r.sb("qlo", [P, 2, DC, T], F32R)
        kk = r.sb("kk", [P, 2, DC, T], F32R)
        kb = [r.sb(f"kb{i}", [P, 2, DC, HC, 2 * S], F32R) for i in range(2)]
        v32 = r.sb("v32", [P, 2, D], F32)
        vr = r.sb("vr", [P, 2, D], F32)
        v3 = r.sb("v3", [P, 2, GB, H, 3, DH], BF16)
        negs = r.sb("negs", [P, 2, HU, S], F32)
        negmax = r.sb("negmax", [P, 2, HU], F32)
        prob = r.sb("prob", [P, 4, HU, S], F32)
        sums = r.sb("sums", [P, GB, H], F32)
        rinv = r.sb("rinv", [P, 2, H], F32)
        phl = r.sb("phl", [P, 4, 2, HU, S], F16)
        pT = r.sb("pT", [P, 2, 2, HU, S], F16)
        osum = r.sb("osum", [P, 2, H // 2, DH], F32)
        on = r.sb("on", [P, 2, GB, D], F32)
        ohi, olo = xnhi, xnlo
        x2 = r.sb("x2", [P, GB, D], F32)
        xln = r.sb("xln", [P, GB, D], F32)
        xlnT = x_in[:].rearrange("p b d -> p (b d)").rearrange("p (c t) -> p c t", c=DC)
        lg = r.sb("lg", [P, GB, E], F32)
        lgx = r.sb("lgx", [P, GB, E], F32)
        lmax = r.sb("lmax", [P, GB], F32)
        lsum = r.sb("lsum", [P, GB], F32)
        score_ps = [r.ps(f"score{i}", [P, HU, S], F32) for i in range(2)]
        pT_ps = [r.ps(f"pT_ps{i}", [P, 2, HU, S], F16) for i in range(2)]
        o_ps = [r.ps(f"o_ps{i}", [P, 512], F32) for i in range(2)]
        m_ps = [r.ps(f"m_ps{i}", [P, 512], F32) for i in range(2)]

        w_loaded, w_split, w_link = r.sem("w_loaded"), r.sem("w_split"), r.sem("w_link")
        w_hi = r.sem("w_hi")
        const_loaded, bias_ready = r.sem("const_loaded"), r.sem("bias_ready")
        kb_zero = r.sem("kb_zero")
        x_loaded, y_loaded, mask_loaded, xres_loaded = (r.sem(n) for n in ("x_loaded", "y_loaded", "mask_loaded", "xres_loaded"))
        y_split, yhi_ready = r.sem("y_split"), r.sem("yhi_ready")
        ln_link, ln2_link, soft_link, on_link = (r.sem(n) for n in ("ln_link", "ln2_link", "soft_link", "on_link"))
        stats_ready, rstd_ready, xn_ready, rstd_link = (r.sem(n) for n in ("stats_ready", "rstd_ready", "xn_ready", "rstd_link"))
        xnT_full, xnhi_ready, xn_split = r.sem("xnT_full"), r.sem("xnhi_ready"), r.sem("xn_split")
        q_full, qhi_ready, q_split = r.sem("q_full"), r.sem("qhi_ready"), r.sem("q_split")
        k_full, khi_ready, k_split = r.sem("k_full"), r.sem("khi_ready"), r.sem("k_split")
        k_spread = [r.sem("k_spread0"), r.sem("k_spread1")]
        v_full, v_ready, far_ready = r.sem("v_full"), r.sem("v_ready"), r.sem("far_ready")
        v32_ready, v1_ready, vr_ready, v2_ready = (r.sem(n) for n in ("v32_ready", "v1_ready", "vr_ready", "v2_ready"))
        score_full, negs_ready, prob_ready = r.sem("score_full"), r.sem("negs_ready"), r.sem("prob_ready")
        phi_ready, plo_ready = r.sem("phi_ready"), r.sem("plo_ready")
        pT_full, pv_done = r.sem("pT_full"), r.sem("pv_done")
        pT_out = [r.sem("pT_out_even"), r.sem("pT_out_odd")]
        o_read, on_ready = r.sem("o_read"), r.sem("on_ready")
        oT_full, ohi_ready, o_split = r.sem("oT_full"), r.sem("ohi_ready"), r.sem("o_split")
        wo_full, x2_ready, stats2_ready, rstd2_ready, xln_ready = (
            r.sem(n) for n in ("wo_full", "x2_ready", "stats2_ready", "rstd2_ready", "xln_ready"))
        xres_biased = r.sem("xres_biased")
        xlnT_full, xlnT_out, lg_full, lg_out, lgx_ready, aff_ready = (
            r.sem(n) for n in ("xlnT_full", "xlnT_out", "lg_full", "lg_out", "lgx_ready", "aff_ready"))
        x2_stored, xln_stored = r.sem("x2_stored"), r.sem("xln_stored")

        x_v = a["x"].rearrange("(g b) p d -> g p b d", b=GB)
        y_v = a["ctxT"].rearrange("(c p) (g t) -> g p c t", p=P, t=T)
        mask_v = a["mask"].rearrange("(g b) q k -> g q b k", b=GB)
        x2_v = x2_dram.rearrange("(g b) p d -> g p b d", b=GB)
        xln_v = xln_dram.rearrange("(g b) p d -> g p b d", b=GB)

        def steps(eng, step):
            step(-1, 1, False, False, False, True)
            step(0, 0, True, False, False, True)
            step(1, 1, True, True, False, True)
            step(2, 0, True, True, True, True)
            step(3, 1, True, True, True, True)
            with eng.Fori(2, G // 2 - 1) as i:
                step(i * 2, 0, True, True, True, True)
                step(i * 2 + 1, 1, True, True, True, True)
            step(G - 2, 0, True, True, True, True)
            step(G - 1, 1, True, True, True, False)
            step(G, 0, False, True, True, False)
            step(G + 1, 1, False, False, True, False)

        def by_head(t):
            return t[:].rearrange("p b (h d) -> p (b h) d", d=DH)

        def v_parts(par, n):
            return [v3[:, par, 2 * n:2 * n + 2, :, i, :].rearrange("p b h d -> p (b h) d") for i in range(3)]

        def lagging(g, s, lag, has_b, has_c):
            if s >= lag:
                return (s - lag, 1, (g - 1) * U + s - lag) if has_b else None
            return (s - lag + U, 2, (g - 2) * U + s - lag + U) if has_c else None

        def early(n, first):
            return isinstance(n, int) and n < first

        A_XT, A_Q, A_K, A_V = 0, 1, 3, 4
        C_OT, C_WO, C_LNT, C_LG = 8, 9, 14, 15
        C_RSTD = 13
        L_STATS, L_Y, L_XN, A_FAR = 7, 8, 10, 3
        block = ctx.enter_context(nc.Block())

        @block.sync
        def _(sp):
            for n, name in enumerate(WN):
                if n:
                    sp.wait_ge(w_split, n)
                sp.dma_start(wraw[:], a[f"w{name}T"].rearrange("(c p) n -> p c n", p=P)).then_inc(w_loaded, 16)
            sp.dma_start(gateT[:], a["gateT"].rearrange("(c p) n -> p c n", p=P)).then_inc(const_loaded, 16)
            with nc.allow_non_contiguous_dma(reason="bias columns, once"):
                sp.dma_start(bqk[:, 0, :], a["bq"].rearrange("(c p) -> p c", p=P)).then_inc(const_loaded, 16)
                sp.dma_start(bqk[:, 1, :], a["bk"].rearrange("(c p) -> p c", p=P)).then_inc(const_loaded, 16)
            sp.dma_start(bvo[:, 0, :], a["bv"].partition_broadcast(P)).then_inc(const_loaded, 16)
            sp.dma_start(bvo[:, 1, :], a["bo"].partition_broadcast(P)).then_inc(const_loaded, 16)

            def step(g, par, has_a, has_b, has_c, has_l):
                if has_l:
                    if not early(g, 0):
                        if not early(g, 3):
                            sp.wait_ge(lg_full, g - 2)
                        sp.wait_ge(y_split, (g + 1) * 2)
                        sp.wait_ge(xn_ready, g + 1)
                    sp.dma_start(x_in[:], x_v[g + 1]).then_inc(x_loaded, 16)
                    sp.dma_start(yT[:], y_v[g + 1]).then_inc(y_loaded, 16)
                if has_a:
                    if not early(g, 1):
                        sp.wait_ge(far_ready, g)
                    else:
                        sp.wait_ge(w_split, 4)
                    sp.dma_start(mask, mask_v[g]).then_inc(mask_loaded, 16)
                if has_c:
                    if not early(g, 3):
                        sp.wait_ge(x2_ready, (g - 2) * 2)
                    sp.dma_start(x_res[:], x_v[g - 2]).then_inc(xres_loaded, 16)
                for pair in range(2):
                    if has_a:
                        sp.wait_ge(k_split, (g + 1) * 2)
                        if not early(g, 1):
                            sp.wait_ge(score_full, g * U - U // 2 + pair * U // 2)
                        for h in range(HC):
                            for x in range(2):
                                sp.dma_start(raw(kb[pair][h * DH:(h + 1) * DH, x, :, h, :]),
                                             raw(kk[h * DH:(h + 1) * DH, x, :, pair * 2 * S:(pair + 1) * 2 * S])
                                             ).then_inc(k_spread[pair], 16)
                    if has_c and pair == 0:
                        sp.wait_ge(x2_ready, (g - 1) * 2)
                        sp.dma_start(x2_v[g - 2], x2[:]).then_inc(x2_stored, 16)
                if has_c:
                    sp.wait_ge(xln_ready, g - 1)
                    sp.dma_start(xln_v[g - 2], xln[:]).then_inc(xln_stored, 16)

            sp.wait_ge(kb_zero, 2)
            steps(sp, step)
            sp.wait_ge(x2_stored, 16 * G)
            sp.wait_ge(xln_stored, 16 * G)

        @block.gpsimd
        def _(pool):
            nc.gpsimd.memset(eps[:], EPS)
            nc.gpsimd.memset(minus_half[:], -0.5).then_inc(rstd_link, 1)
            for i in range(2):
                nc.gpsimd.memset(raw(kb[i][:]), 0.0).then_inc(kb_zero, 1)
            pool.wait_ge(rstd_link, 1)
            pool.wait_ge(bias_ready, 1)

            def rsqrt(n, ready, done, base):
                nc.gpsimd.tensor_tensor(rstd[:, n, :], mv[:, n, :, 1], eps[:], ALU.add).then_inc(rstd_link, 1)
                pool.wait_ge(rstd_link, base)
                nc.gpsimd.tensor_tensor(rstd[:, n, :], rstd[:, n, :], minus_half[:], ALU.pow).then_inc(done, 1)

            def step(g, par, has_a, has_b, has_c, has_l):
                for s in range(U):
                    if at := lagging(g, s, LO, has_b, has_c):
                        v, back, u = at
                        pool.wait_ge(phi_ready, u + 1)
                        nc.gpsimd.tensor_tensor(phl[:, v % 4, 1], prob[:, v % 4], phl[:, v % 4, 0],
                                                ALU.subtract).then_inc(plo_ready, 1)
                    if has_l and s == L_STATS:
                        pool.wait_ge(stats_ready, g + 2)
                        rsqrt(0, stats_ready, rstd_ready, 1 + (g + 2) + (0 if early(g, 2) else g - 2))
                    if has_l and s == L_Y:
                        for h in range(DC):
                            pool.wait_ge(yhi_ready, g + 2)
                            nc.gpsimd.tensor_tensor(ylo[:, h, :], yT[:, h, :], yhi[:, h, :], ALU.subtract).then_inc(y_split, 1)
                    if has_c and s == 2:
                        pool.wait_ge(xres_loaded, (g - 1) * 16)
                        nc.gpsimd.tensor_tensor(x_res[:], x_res[:], bvo[:, 1:2, :].to_broadcast([P, GB, D]),
                                                ALU.add).then_inc(xres_biased, 1)
                    if has_c and s == C_RSTD:
                        pool.wait_ge(stats2_ready, g - 1)
                        norms = G if isinstance(g, int) and g >= G - 1 else g + 2
                        rsqrt(1, stats2_ready, rstd2_ready, 1 + norms + (g - 1))
                    if has_a and s in (A_V + 2, A_V + 4):
                        n = (s - A_V) // 2 - 1
                        v1, v2, v3_ = v_parts(par, n)
                        pool.wait_ge(v1_ready, g * 2 + n + 1)
                        nc.gpsimd.tensor_tensor(by_head(vr), by_head(v32), v1, ALU.subtract).then_inc(vr_ready, 1)
                        pool.wait_ge(v2_ready, g * 2 + n + 1)
                        nc.gpsimd.tensor_tensor(v3_, by_head(vr), v2, ALU.subtract).then_inc(v_ready, 1)

            steps(pool, step)

        @block.tensor
        def _(pe):
            pe.wait_ge(w_split, 4)
            pe.wait_ge(const_loaded, 80)

            def three(out, whi_, wlo_, xhi_, xlo_, first, last):
                nc.tensor.matmul(out, whi_, xhi_, start=first, stop=False)
                nc.tensor.matmul(out, whi_, xlo_, start=False, stop=False)
                return nc.tensor.matmul(out, wlo_, xhi_, start=False, stop=last)

            def step(g, par, has_a, has_b, has_c, has_l):
                old = 1 - par

                def scores(s):
                    b, m = s // UB, s % UB
                    ch, h0 = m // 2, (m % 2) * HU
                    pair, t = b // 2, slice((b % 2) * S, (b % 2 + 1) * S)
                    u = (g - 1) * U + s
                    if s == 0:
                        pe.wait_ge(q_split, g * 2)
                    if s % (U // 2) == 0:
                        pe.wait_ge(k_spread[pair], g * 16 * 2 * HC)
                    if not isinstance(g, int) or g > 1 or s >= 2:
                        pe.wait_ge(negs_ready, u - 1)
                    q1 = qhi[:, old, ch, b * S:(b + 1) * S]
                    q2 = qlo[:, old, ch, b * S:(b + 1) * S]
                    k1 = kb[pair][:, 0, ch, h0:h0 + HU, t]
                    k2 = kb[pair][:, 1, ch, h0:h0 + HU, t]
                    three(score_ps[s % 2][:], q1, q2, k1, k2, True, True).then_inc(score_full, 1)

                def transposes(v, back, u):
                    pe.wait_ge(plo_ready, u + 1)
                    if not early(u, 2):
                        pe.wait_ge(pT_out[v % 2], (g - back) * (U // 2) + v // 2)
                    for part in range(2):
                        for h in range(HU):
                            last = nc.tensor.transpose(pT_ps[v % 2][:, part, h, :], phl[:, v % 4, part, h, :], c["id16"][:])
                    last.then_inc(pT_full, 1)

                def values(v, back, u):
                    b, m = v // UB, v % UB
                    pe.wait_ge(v_ready, (g - back + 1) * 2)
                    pe.wait_ge(pT_out[v % 2], (g - back) * (U // 2) + v // 2 + 1)
                    if m % 2 == 0 and not early(u, UB):
                        pe.wait_ge(o_read, (g - back) * GB * 2 + b * 2 + m // 2 - 1)
                    bank = o_ps[m // 2]
                    for h in range(HU):
                        at = ((m % 2) * HU + h) * VP
                        for part in range(2):
                            last = nc.tensor.matmul(bank[:, at:at + VP], pT[:, v % 2, part, h, :],
                                                    v3[:, old if back == 1 else par, b, m * HU + h, :, :].rearrange("p n d -> p (n d)"),
                                                    start=(part == 0), stop=(part == 1))
                    last.then_inc(pv_done, 1)

                for s in range(U):
                    if has_b:
                        scores(s)
                    if at := lagging(g, s, LT, has_b, has_c):
                        transposes(*at)
                    if at := lagging(g, s, LP, has_b, has_c):
                        values(*at)
                    if has_c and s == C_OT:
                        pe.wait_ge(on_ready, (g - 1) * GB * 2)
                        if has_a:
                            pe.wait_ge(v32_ready, (g + 1) * 2)
                        else:
                            pe.wait_ge(v32_ready, G * 2)
                            pe.wait_ge(lgx_ready, g - 2)
                        for ch in range(DC):
                            for b in range(GB):
                                last = nc.tensor.transpose(m_ps[ch][:, b * S:(b + 1) * S],
                                                           on[:, par, b, ch * P:(ch + 1) * P], c["id32"][:])
                            last.then_inc(oT_full, 1)
                    if has_c and C_WO <= s < C_WO + GB:
                        b = s - C_WO
                        if b == 0:
                            pe.wait_ge(o_split, (g - 1) * 2)
                        t = slice(b * S, (b + 1) * S)
                        for ch in range(DC):
                            last = three(m_ps[b // 2][:, (b % 2) * D:(b % 2 + 1) * D], ohi[:, ch, t], olo[:, ch, t],
                                         whi["o"][:, ch, :], wlo["o"][:, ch, :], ch == 0, ch == DC - 1)
                        if b % 2:
                            last.then_inc(wo_full, 1)
                    if has_c and s == C_LNT:
                        pe.wait_ge(xln_ready, g - 1)
                        for ch in range(DC):
                            for b in range(GB):
                                last = nc.tensor.transpose(m_ps[ch][:, b * S:(b + 1) * S],
                                                           xln[:, b, ch * P:(ch + 1) * P], c["id32"][:])
                            last.then_inc(xlnT_full, 1)
                    if has_c and s == C_LG:
                        pe.wait_ge(xlnT_out, (g - 1) * 2)
                        for b in range(GB):
                            for ch in range(DC):
                                last = nc.tensor.matmul(m_ps[0][:, b * E:(b + 1) * E], xlnT[:, ch, b * S:(b + 1) * S],
                                                        gateT[:, ch, :], start=(ch == 0), stop=(ch == DC - 1))
                        last.then_inc(lg_full, 1)
                    if has_a and s == A_XT:
                        pe.wait_ge(xn_ready, g + 1)
                        if not early(g, 3):
                            pe.wait_ge(lgx_ready, g - 2)
                            pe.wait_ge(xlnT_out, (g - 2) * 2)
                        elif not early(g, 1):
                            pe.wait_ge(v32_ready, g * 2)
                        for ch in range(DC):
                            for b in range(GB):
                                last = nc.tensor.transpose(m_ps[ch][:, b * S:(b + 1) * S],
                                                           xn[:, b, ch * P:(ch + 1) * P], c["id32"][:])
                            last.then_inc(xnT_full, 1)
                    if has_a and s in (A_Q, A_K):
                        name, hi, lo, full = ("q", xnhi, xnlo, q_full) if s == A_Q else ("k", yhi, ylo, k_full)
                        if s == A_Q:
                            pe.wait_ge(xn_split, (g + 1) * 2)
                        else:
                            pe.wait_ge(y_split, (g + 1) * 2)
                            pe.wait_ge(yhi_ready, g + 1)
                            pe.wait_ge(q_split, (g + 1) * 2)
                        for n in range(DC):
                            for ch in range(DC):
                                last = three(m_ps[n][:], whi[name][:, ch, n * P:(n + 1) * P],
                                             wlo[name][:, ch, n * P:(n + 1) * P], hi[:, ch, :], lo[:, ch, :],
                                             ch == 0, ch == DC - 1)
                            last.then_inc(full, 1)
                    if has_a and A_V <= s < A_V + GB:
                        b = s - A_V
                        if b == 0:
                            pe.wait_ge(k_split, (g + 1) * 2)
                        t = slice(b * S, (b + 1) * S)
                        for ch in range(DC):
                            last = three(m_ps[b // 2][:, (b % 2) * D:(b % 2 + 1) * D], yhi[:, ch, t], ylo[:, ch, t],
                                         whi["v"][:, ch, :], wlo["v"][:, ch, :], ch == 0, ch == DC - 1)
                        if b % 2:
                            last.then_inc(v_full, 1)

            steps(pe, step)

        @block.scalar
        def _(act):
            for n, name in enumerate(WN):
                act.wait_ge(w_loaded, 16 * (n + 1))
                nc.scalar.activation(whi[name][:], wraw[:], ACT.Copy, scale=-0.25 if name == "q" else 1.0).then_inc(w_hi, 1)
            act.wait_ge(bias_ready, 1)

            def step(g, par, has_a, has_b, has_c, has_l):
                for s in range(U):
                    if at := lagging(g, s, LE, has_b, has_c):
                        v, back, u = at
                        b, m = v // UB, v % UB
                        act.wait_ge(negs_ready, u + 1)
                        if not early(u, 4):
                            act.wait_ge(plo_ready, u - 3)
                        if m == 0 and not early(u, U):
                            act.wait_ge(on_ready, (g - back - 1) * GB * 2 + (b + 1) * 2)
                        for h in range(HU):
                            last = nc.scalar.activation(prob[:, v % 4, h, :], negs[:, v % 2, h, :], ACT.Exp, scale=-1.0,
                                                        bias=negmax[:, v % 2, h:h + 1],
                                                        accum_out=sums[:, b, m * HU + h:m * HU + h + 1])
                        last.then_inc(prob_ready, 1)
                    if (at := lagging(g, s, LT, has_b, has_c)) and at[0] % 2 == 0:
                        v, back, u = at
                        act.wait_ge(pT_full, u + 1)
                        if not early(u, 2):
                            act.wait_ge(pv_done, u - 1)
                        nc.scalar.activation(pT[:, 0], pT_ps[0][:], ACT.Copy).then_inc(pT_out[0], 1)
                    if has_c and s == C_OT:
                        for ch in range(DC):
                            act.wait_ge(oT_full, (g - 2) * 2 + ch + 1)
                            act.wait_ge(q_full, (g + 1 if has_a else G) * 2)
                            nc.scalar.activation(ohi[:, ch, :], m_ps[ch][:], ACT.Copy).then_inc(ohi_ready, 1)
                    if has_c and s == C_LNT:
                        for ch in range(DC):
                            act.wait_ge(xlnT_full, (g - 2) * 2 + ch + 1)
                            act.wait_ge(xn_ready, g + 2 if has_l else G)
                            nc.scalar.activation(xlnT[:, ch, :], m_ps[ch][:], ACT.Copy).then_inc(xlnT_out, 1)
                    if has_c and s == C_LG:
                        act.wait_ge(lgx_ready, g - 1)
                        nc.scalar.activation(lgx[:], lg[:], ACT.Exp).then_inc(lg_out, 1)
                    if has_a and s == A_XT:
                        for ch in range(DC):
                            act.wait_ge(xnT_full, g * 2 + ch + 1)
                            if not early(g, 3):
                                act.wait_ge(wo_full, (g - 2) * 2)
                            elif not early(g, 1):
                                act.wait_ge(q_full, g * 2)
                            nc.scalar.activation(xnhi[:, ch, :], m_ps[ch][:], ACT.Copy).then_inc(xnhi_ready, 1)
                    if has_a and s == A_Q:
                        for ch in range(DC):
                            act.wait_ge(q_full, g * 2 + ch + 1)
                            if not early(g, 2):
                                act.wait_ge(score_full, (g - 1) * U)
                            nc.scalar.activation(qhi[:, par, ch, :], m_ps[ch][:], ACT.Identity,
                                                 bias=bqk[:, 0, ch:ch + 1]).then_inc(qhi_ready, 1)
                    if has_a and s == A_K:
                        for ch in range(DC):
                            act.wait_ge(k_full, g * 2 + ch + 1)
                            if not isinstance(g, int) or g > 0:
                                for pair in range(2):
                                    act.wait_ge(k_spread[pair], g * 16 * 2 * HC)
                            nc.scalar.activation(kk[:, 0, ch, :], m_ps[ch][:], ACT.Identity,
                                                 bias=bqk[:, 1, ch:ch + 1]).then_inc(khi_ready, 1)

                    if has_a and s in (A_V + 2, A_V + 4):
                        n = (s - A_V) // 2 - 1
                        v1, v2, _ = v_parts(par, n)
                        act.wait_ge(v32_ready, g * 2 + n + 1)
                        if not early(g, 2):
                            act.wait_ge(pv_done, (g - 1) * U)
                        nc.scalar.activation(v1, by_head(v32), ACT.Copy).then_inc(v1_ready, 1)
                        act.wait_ge(vr_ready, g * 2 + n + 1)
                        nc.scalar.activation(v2, by_head(vr), ACT.Copy).then_inc(v2_ready, 1)

            steps(act, step)

        @block.vector
        def _(dve):
            for n, name in enumerate(WN):
                dve.wait_ge(w_hi, n + 1)
                nc.vector.scalar_tensor_tensor(out=wlo[name][:], in0=wraw[:], scalar=-0.25 if name == "q" else 1.0,
                                               in1=whi[name][:], op0=ALU.mult, op1=ALU.subtract).then_inc(w_split, 1)
            dve.wait_ge(const_loaded, 80)
            nc.vector.tensor_scalar(bvo[:, 1, :], bvo[:, 1, :], c["tg"][:, 0:1], None, ALU.mult).then_inc(w_link, 1)
            nc.vector.tensor_scalar(bqk[:, 0, :], bqk[:, 0, :], -0.25, None, ALU.mult).then_inc(w_link, 1)
            dve.wait_ge(w_link, 2)
            nc.vector.tensor_copy(after[:, 0:2], bqk[:, 0, :]).then_inc(bias_ready, 1)

            def norm(x_tile, out, n, chain, ready, rstd_done, count, done):
                for b in range(GB):
                    chain.mark(nc.vector.bn_stats(stats[:, n, b, :], x_tile[:, b, :]))
                chain.settle()
                nc.vector.tensor_copy(after[:, 2 + n:3 + n], stats[:, n, 0, 0:1])
                for b in range(GB):
                    last = nc.vector.bn_aggr(mv[:, n, b, :], stats[:, n, b, :])
                last.then_inc(ready, 1)

            def normalise(x_tile, out, n, rstd_done, count, done):
                dve.wait_ge(rstd_done, count)
                for b in range(GB):
                    last = nc.vector.tensor_scalar(out[:, b, :], x_tile[:, b, :], mv[:, n, b, 0:1], rstd[:, n, b:b + 1],
                                                   ALU.subtract, ALU.mult)
                last.then_inc(done, 1)

            def step(g, par, has_a, has_b, has_c, has_l):
                old = 1 - par
                for s in range(U):
                    if has_b:
                        u = (g - 1) * U + s
                        b = s // UB
                        dve.wait_ge(score_full, u + 1)
                        if s == 0:
                            dve.wait_ge(far_ready, g)
                        if not early(u, 2):
                            dve.wait_ge(prob_ready, u - 1)
                        nc.vector.tensor_copy(after[:, s % 2:s % 2 + 1], score_ps[s % 2][:, 0, 0:1])
                        for h in range(HU):
                            last = nc.vector.tensor_tensor_reduce(
                                out=negs[:, s % 2, h, :], in0=score_ps[s % 2][:, h, :], in1=far[:, old, b, :], scale=1.0,
                                scalar=3.0e38, op0=ALU.add, op1=ALU.min, accum_out=negmax[:, s % 2, h:h + 1])
                        last.then_inc(negs_ready, 1)
                    if at := lagging(g, s, LH, has_b, has_c):
                        v, back, u = at
                        dve.wait_ge(prob_ready, u + 1)
                        if not early(u, 4):
                            dve.wait_ge(pT_full, u - 3)
                        nc.vector.tensor_copy(phl[:, v % 4, 0], prob[:, v % 4]).then_inc(phi_ready, 1)
                    if (at := lagging(g, s, LT, has_b, has_c)) and at[0] % 2:
                        v, back, u = at
                        dve.wait_ge(pT_full, u + 1)
                        if not early(u, 2):
                            dve.wait_ge(pv_done, u - 1)
                        nc.vector.tensor_copy(pT[:, 1], pT_ps[1][:]).then_inc(pT_out[1], 1)
                    if (at := lagging(g, s, LD, has_b, has_c)) and at[0] % 2:
                        v, back, u = at
                        b, half = v // UB, (v % UB) // 2
                        n = (g - back) * (U // 2) + (v - 1) // 2
                        hs = slice(half * HC, (half + 1) * HC)
                        chain = Chain(dve, on_link, n)
                        chain.mark(nc.vector.reciprocal(rinv[:, b % 2, hs], sums[:, b, hs]))
                        dve.wait_ge(pv_done, u + 1)
                        nc.vector.tensor_reduce(osum[:, half], o_ps[half][:, 0:HC * VP].rearrange("p (h n d) -> p h d n", n=3, d=DH),
                                                AXX, ALU.add).then_inc(o_read, 1)
                        chain.settle()
                        dve.wait_ge(o_read, n + 1)
                        nc.vector.tensor_tensor(
                            on[:, old if back == 1 else par, b, half * P:(half + 1) * P].rearrange("p (h d) -> p h d", d=DH),
                            osum[:, half], rinv[:, b % 2, hs].unsqueeze(2).to_broadcast([P, HC, DH]), ALU.mult).then_inc(on_ready, 1)
                    if has_a and s == A_FAR:
                        dve.wait_ge(mask_loaded, (g + 1) * 16)
                        nc.vector.tensor_scalar(far[:, par], mask, -1.0, -1e9, ALU.add, ALU.mult).then_inc(far_ready, 1)
                    if has_l and s == L_STATS:
                        dve.wait_ge(x_loaded, (g + 2) * 16)
                        norm(x_in, xn, 0, Chain(dve, ln_link, (g + 1) * GB), stats_ready, None, None, None)
                    if has_l and s == L_Y:
                        dve.wait_ge(y_loaded, (g + 2) * 16)
                        if has_a:
                            dve.wait_ge(v_full, (g + 1) * 2)
                        nc.vector.tensor_copy(yhi[:], yT[:]).then_inc(yhi_ready, 1)
                    if has_l and s == L_XN:
                        if has_a:
                            dve.wait_ge(xnT_full, (g + 1) * 2)
                        normalise(x_in, xn, 0, rstd_ready, g + 2, xn_ready)
                    if has_c and s == C_OT:
                        for ch in range(DC):
                            dve.wait_ge(ohi_ready, (g - 2) * 2 + ch + 1)
                            nc.vector.tensor_tensor(olo[:, ch, :], m_ps[ch][:], ohi[:, ch, :], ALU.subtract).then_inc(o_split, 1)
                    if has_c and s in (C_WO + 1, C_WO + 3):
                        n = (s - C_WO) // 2
                        dve.wait_ge(wo_full, (g - 2) * 2 + n + 1)
                        if n == 0:
                            dve.wait_ge(xres_biased, g - 1)
                            if not early(g, 3):
                                dve.wait_ge(x2_stored, (g - 2) * 16)
                        nc.vector.scalar_tensor_tensor(
                            out=x2[:, 2 * n:2 * n + 2, :], in0=m_ps[n][:].rearrange("p (b d) -> p b d", b=2), scalar=c["tg"][:, 0:1],
                            in1=x_res[:, 2 * n:2 * n + 2, :], op0=ALU.mult, op1=ALU.add).then_inc(x2_ready, 1)
                    if has_c and s == C_WO + 3:
                        dve.wait_ge(x2_ready, (g - 1) * 2)
                        norm(x2, xln, 1, Chain(dve, ln2_link, (g - 2) * GB), stats2_ready, None, None, None)
                    if has_c and s == C_WO + 4:
                        if not isinstance(g, int) or g > 2:
                            dve.wait_ge(xln_stored, (g - 2) * 16)
                            dve.wait_ge(xlnT_full, (g - 2) * 2)
                        normalise(x2, xln, 1, rstd2_ready, g - 1, xln_ready)
                    if has_c and s == C_LG:
                        chain = Chain(dve, soft_link, (g - 2) * 5)
                        dve.wait_ge(lg_full, g - 1)
                        l3 = m_ps[0][:, 0:GB * E].rearrange("p (b e) -> p b e", e=E)
                        chain.link(nc.vector.tensor_reduce(lmax[:], l3, AXX, ALU.max))
                        nc.vector.tensor_tensor(lg[:], l3, lmax[:].unsqueeze(2).to_broadcast([P, GB, E]),
                                                ALU.subtract).then_inc(lgx_ready, 1)
                        dve.wait_ge(lg_out, g - 1)
                        chain.link(nc.vector.tensor_reduce(lsum[:], lgx[:], AXX, ALU.add))
                        chain.link(nc.vector.reciprocal(lmax[:], lsum[:]))
                        chain.link(nc.vector.tensor_tensor(lgx[:], lgx[:], lmax[:].unsqueeze(2).to_broadcast([P, GB, E]), ALU.mult))
                        chain.link(nc.vector.tensor_copy(c["aff"][:, bass.ds((g - 2) * (GB * E), GB * E)],
                                                         lgx[:].rearrange("p b e -> p (b e)")))
                    if has_a and s == A_XT:
                        for ch in range(DC):
                            dve.wait_ge(xnhi_ready, g * 2 + ch + 1)
                            nc.vector.tensor_tensor(xnlo[:, ch, :], m_ps[ch][:], xnhi[:, ch, :], ALU.subtract).then_inc(xn_split, 1)
                    if has_a and s == A_Q:
                        for ch in range(DC):
                            dve.wait_ge(qhi_ready, g * 2 + ch + 1)
                            nc.vector.scalar_tensor_tensor(out=qlo[:, par, ch, :], in0=m_ps[ch][:], scalar=bqk[:, 0, ch:ch + 1],
                                                           in1=qhi[:, par, ch, :], op0=ALU.add, op1=ALU.subtract).then_inc(q_split, 1)
                    if has_a and s == A_K:
                        for ch in range(DC):
                            dve.wait_ge(khi_ready, g * 2 + ch + 1)
                            nc.vector.scalar_tensor_tensor(out=kk[:, 1, ch, :], in0=m_ps[ch][:], scalar=bqk[:, 1, ch:ch + 1],
                                                           in1=kk[:, 0, ch, :], op0=ALU.add, op1=ALU.subtract).then_inc(k_split, 1)
                    if has_a and s in (A_V + 1, A_V + 3):
                        n = (s - A_V) // 2
                        dve.wait_ge(v_full, g * 2 + n + 1)
                        if not early(g, 1) or n:
                            dve.wait_ge(v_ready, g * 2 + n)
                        nc.vector.tensor_tensor(v32[:], m_ps[n][:].rearrange("p (b d) -> p b d", b=2),
                                                bvo[:, 0:1, :].to_broadcast([P, 2, D]), ALU.add).then_inc(v32_ready, 1)

            steps(dve, step)


def gather(nc, c, a, xln_dram, rows_dram):
    with ExitStack() as ctx:
        r = Room(nc, ctx, "g")
        work = r.sb("work", [P, RT, S], F32)
        top = r.sb("top", [P, RT, 8], F32)
        sel = r.sb("sel", [P, RT, S], F32)
        ones = r.sb("ones", [P, S], F32)
        rank = r.sb("rank", [P, RT, S], F32)
        pos = r.sb("pos", [P, B * E], F32)
        aff3 = r.sb("aff3", [P, B, 3, E], BF16)
        rest = r.sb("rest", [P, B, E], F32)
        aff_now = r.sb("aff_now", [P, 2, GB, 3, E], BF16)
        xg = r.sb("xg", [P, 2, GB, D], F32)
        xhi = r.sb("xhi", [P, GB, D], F32R)
        xlo = r.sb("xlo", [P, GB, D], F32R)
        hot = r.sb("hot", [P, 2, GB, E, K], F32R)
        hotb = r.sb("hotb", [P, GB, E, K], BF16)
        gsel = r.sb("gsel", [P, GB * DC, 3 * E], F32)
        ghi = r.sb("ghi", [P, 2, DC, E, GB, K], F32R)
        glo = r.sb("glo", [P, 2, DC, E, GB, K], F32R)
        t_ps = r.ps("t", [P, RT, S], F32)
        hT_ps = r.ps("hT", [P, GB, DC, P], BF16)
        g_ps = r.ps("g", [P, GB * DC, 3 * E], F32)
        x_ps = [r.ps(f"x{i}", [P, 2, E, K], F32) for i in range(4)]
        link, tr_full, pos_full, pos_out, aff_split = (r.sem(n) for n in ("link", "tr_full", "pos_full", "pos_out", "aff_split"))
        rank_ready = r.sem("rank_ready")
        x_loaded = [r.sem("x_loaded0"), r.sem("x_loaded1")]
        xhi_ready, xlo_ready, hot_ready, hotb_ready = (r.sem(n) for n in ("xhi_ready", "xlo_ready", "hot_ready", "hotb_ready"))
        hT_full, hT_out, g_full, g_read, g_out, g_link = (r.sem(n) for n in ("hT_full", "hT_out", "g_full", "g_read", "g_out", "g_link"))
        x_full, ghi_ready, glo_ready = r.sem("x_full"), r.sem("ghi_ready"), r.sem("glo_ready")
        stored = [r.sem("stored0"), r.sem("stored1")]
        xln_v = xln_dram.rearrange("(g b) p d -> g p b d", b=GB)
        block = ctx.enter_context(nc.Block())

        def pairs(eng, step):
            step(0, 0)
            step(1, 1)
            with eng.Fori(1, G // 2) as i:
                step(i * 2, 0)
                step(i * 2 + 1, 1)

        def later(g):
            return not isinstance(g, int) or g > 1

        @block.sync
        def _(sp):
            def load(g, par):
                sp.dma_start(xg[:, par], xln_v[g]).then_inc(x_loaded[par], 16)

            load(0, 0)
            load(1, 1)

            def step(g, par):
                sp.wait_ge(ghi_ready, (g + 1) * 4)
                sp.wait_ge(glo_ready, (g + 1) * 4)
                for x, t in ((0, ghi), (1, glo)):
                    for ch in range(DC):
                        dst = rows_dram[x, ch, g].rearrange("e p n -> p e n")
                        sp.dma_start(dst, raw(t[:, par, ch]).rearrange("p e b k -> p e (b k)")).then_inc(stored[par], 16)

            def step_and_load(g, par):
                step(g, par)
                load(g + 2, par)

            step_and_load(0, 0)
            step_and_load(1, 1)
            with sp.Fori(1, G // 2 - 1) as i:
                step_and_load(i * 2, 0)
                step_and_load(i * 2 + 1, 1)
            step(G - 2, 0)
            step(G - 1, 1)
            for par in range(2):
                sp.wait_ge(stored[par], 16 * 4 * G // 2)

        @block.tensor
        def _(pe):
            for t in range(RT):
                last = nc.tensor.transpose(t_ps[:, t, :], c["aff"][:, t * P:(t + 1) * P], c["id32"][:])
            last.then_inc(tr_full, 1)
            pe.wait_ge(rank_ready, 1)
            for t in range(RT):
                last = nc.tensor.transpose(t_ps[:, t, :], rank[:, t, :], c["id32"][:])
            last.then_inc(pos_full, 1)

            def step(g, par):
                pe.wait_ge(hot_ready, g + 1)
                pe.wait_ge(xlo_ready, g + 1)
                for ch in range(DC):
                    for n in range(2):
                        bank = x_ps[ch * 2 + n]
                        if not isinstance(g, int) or g > 0:
                            pe.wait_ge(glo_ready, (g - 1) * 4 + ch * 2 + n + 1)
                        for b in range(2):
                            for part, x in enumerate((xhi, xlo)):
                                last = nc.tensor.matmul(bank[:, b].rearrange("p e k -> p (e k)"),
                                                        x[:, 2 * n + b, ch * P:(ch + 1) * P],
                                                        hot[:, par, 2 * n + b].rearrange("p e k -> p (e k)"),
                                                        start=(part == 0), stop=(part == 1))
                        last.then_inc(x_full, 1)
                pe.wait_ge(hotb_ready, g + 1)
                if not isinstance(g, int) or g > 0:
                    pe.wait_ge(hT_out, g)
                    pe.wait_ge(g_read, g)
                for b in range(GB):
                    for half in range(DC):
                        last = nc.tensor.transpose(hT_ps[:, b, half, :],
                                                   hotb[:, b, half * EC:(half + 1) * EC, :].rearrange("p e k -> p (e k)"), c["idb"][:])
                last.then_inc(hT_full, 1)
                for b in range(GB):
                    for half in range(DC):
                        last = nc.tensor.matmul(g_ps[:, b * DC + half, :],
                                                hotb[:, b, half * EC:(half + 1) * EC, :].rearrange("p e k -> p (e k)"),
                                                aff_now[:, par, b].rearrange("p n e -> p (n e)"), start=True, stop=True)
                last.then_inc(g_full, 1)

            pairs(pe, step)

        @block.scalar
        def _(act):
            def step(g, par):
                act.wait_ge(x_loaded[par], (g - par) * 8 + 16)
                if not isinstance(g, int) or g > 0:
                    act.wait_ge(x_full, g * 4)
                nc.scalar.activation(xhi[:], xg[:, par], ACT.Copy).then_inc(xhi_ready, 1)
                act.wait_ge(hot_ready, g + 1)
                if not isinstance(g, int) or g > 0:
                    act.wait_ge(g_full, g)
                nc.scalar.activation(hotb[:], hot[:, par].bitcast(F32), ACT.Copy).then_inc(hotb_ready, 1)
                for ch in range(DC):
                    for n in range(2):
                        act.wait_ge(x_full, g * 4 + ch * 2 + n + 1)
                        if later(g) and ch == 0 and n == 0:
                            act.wait_ge(stored[par], (g - par) * 32)
                        nc.scalar.activation(ghi[:, par, ch, :, 2 * n:2 * n + 2, :].rearrange("p e b k -> p b e k"),
                                             x_ps[ch * 2 + n][:], ACT.Copy).then_inc(ghi_ready, 1)
                act.wait_ge(hT_full, g + 1)
                nc.scalar.activation(c["onehotT"][:, bass.ds(g * GB, GB)], hT_ps[:], ACT.Copy).then_inc(hT_out, 1)

            pairs(act, step)

        @block.gpsimd
        def _(pool):
            def step(g, par):
                pool.wait_ge(xhi_ready, g + 1)
                nc.gpsimd.tensor_tensor(xlo[:], xg[:, par], xhi[:], ALU.subtract).then_inc(xlo_ready, 1)

            pairs(pool, step)

        @block.vector
        def _(dve):
            chain = Chain(dve, link)
            aff = c["aff"][:].rearrange("p (b e) -> p b e", e=E)
            chain.link(nc.vector.tensor_copy(aff3[:, :, 0, :], aff))
            chain.link(nc.vector.tensor_tensor(rest[:], aff, aff3[:, :, 0, :], ALU.subtract))
            chain.link(nc.vector.tensor_copy(aff3[:, :, 1, :], rest[:]))
            chain.link(nc.vector.tensor_tensor(aff3[:, :, 2, :], rest[:], aff3[:, :, 1, :], ALU.subtract))
            chain.link(nc.vector.memset(ones[:], 1.0))
            dve.wait_ge(tr_full, 1)
            chain.link(nc.vector.tensor_copy(work[:], t_ps[:]))
            for _ in range(K // 8):
                for t in range(RT):
                    chain.mark(nc.vector.max(top[:, t, :], work[:, t, :]))
                chain.settle()
                for t in range(RT):
                    chain.mark(nc.vector.match_replace(work[:, t, :], top[:, t, :], work[:, t, :], -1.0))
                chain.settle()
            chain.link(nc.vector.tensor_scalar(sel[:], work[:], 0.0, None, ALU.is_lt))
            for t in range(RT):
                chain.mark(nc.vector.tensor_tensor_scan(rank[:, t, :], ones[:], sel[:, t, :], 0.0, ALU.mult, ALU.add))
            chain.settle()
            chain.link(nc.vector.tensor_tensor(rank[:], rank[:], sel[:], ALU.mult))
            nc.vector.tensor_scalar(rank[:], rank[:], -1.0, None, ALU.add).then_inc(rank_ready, 1)
            dve.wait_ge(pos_full, 1)
            chain.link(nc.vector.tensor_copy(pos[:], t_ps[:].rearrange("p t n -> p (t n)")))

            def step(g, par):
                if later(g):
                    dve.wait_ge(g_full, g - 1)
                nc.vector.tensor_copy(aff_now[:, par], aff3[:, bass.ds(g * GB, GB)]).then_inc(g_link, 1)
                nc.vector.tensor_tensor(hot[:, par].rearrange("p b e k -> p (b e) k"),
                                        pos[:, bass.ds(g * (GB * E), GB * E)].unsqueeze(2).to_broadcast([P, GB * E, K]),
                                        c["slot"][:].unsqueeze(1).to_broadcast([P, GB * E, K]), ALU.is_equal).then_inc(hot_ready, 1)
                for ch in range(DC):
                    for n in range(2):
                        dve.wait_ge(ghi_ready, g * 4 + ch * 2 + n + 1)
                        nc.vector.tensor_tensor(glo[:, par, ch, :, 2 * n:2 * n + 2, :].rearrange("p e b k -> p b e k"),
                                                x_ps[ch * 2 + n][:],
                                                ghi[:, par, ch, :, 2 * n:2 * n + 2, :].rearrange("p e b k -> p b e k"),
                                                ALU.subtract).then_inc(glo_ready, 1)
                dve.wait_ge(g_full, g + 1)
                if not isinstance(g, int) or g > 0:
                    dve.wait_ge(g_out, g)
                nc.vector.tensor_tensor(gsel[:].rearrange("p (b h) n -> p b h n", h=DC),
                                        g_ps[:].rearrange("p (b h) n -> p b h n", h=DC),
                                        c["own"][:].rearrange("p h n e -> p h (n e)").unsqueeze(1).to_broadcast([P, GB, DC, 3 * E]),
                                        ALU.mult).then_inc(g_read, 1)
                dve.wait_ge(g_read, g + 1)
                nc.vector.tensor_reduce(c["gating"][:, bass.ds(g * GB, GB), :].rearrange("p b h -> p (b h)"),
                                        gsel[:], AXX, ALU.add).then_inc(g_out, 1)

            pairs(dve, step)


def experts(nc, c, a, rows_dram, out_dram):
    with ExitStack() as ctx:
        r = Room(nc, ctx, "e")
        WK = ("g", "u", "d")
        shape = {"g": [P, DC, FF], "u": [P, DC, FF], "d": [P, FC, D]}
        stage = r.sb("stage", [P, DC * FF], F32)
        whi = [{k: r.sb(f"w{k}hi{i}", shape[k], F32R) for k in WK} for i in range(2)]
        wlo = [{k: r.sb(f"w{k}lo{i}", shape[k], F32R) for k in WK} for i in range(2)]
        xr = r.sb("xr", [P, 2, 2, DC, 512], F32R)
        sg = r.sb("sg", [P, 2, 512], F32)
        hh = r.sb("hh", [P, 2, 512], F32)
        hhi = r.sb("hhi", [P, 2, 512], F32R)
        hlo = r.sb("hlo", [P, 2, 512], F32R)
        yT = r.sb("yT", [P, DC, 512], F32)
        yr = r.sb("yr", [P, 4, D], F32)
        g_ps = [r.ps(f"g{i}", [P, 512], F32) for i in range(2)]
        u_ps = [r.ps(f"u{i}", [P, 512], F32) for i in range(2)]
        y_ps = [r.ps(f"y{i}", [P, 512], F32) for i in range(DC)]
        t_ps = [r.ps(f"t{i}", [P, 2, D], F32) for i in range(2)]
        w_loaded, w_hi, w_split = r.sem("w_loaded"), r.sem("w_hi"), r.sem("w_split")
        x_loaded = [r.sem("x_loaded0"), r.sem("x_loaded1")]
        g_full, u_full, sg_ready, hh_ready, hhi_ready, h_ready = (
            r.sem(n) for n in ("g_full", "u_full", "sg_ready", "hh_ready", "hhi_ready", "h_ready"))
        h_used, y_out, t_full, t_out, stored = (r.sem(n) for n in ("h_used", "y_out", "t_full", "t_out", "stored"))

        w_view = {
            "g": a["wgT"].rearrange("e (c p) i -> e p c i", p=P),
            "u": a["wuT"].rearrange("e (c p) i -> e p c i", p=P),
            "d": a["wdT"].rearrange("e (c p) d -> e p c d", p=P),
        }
        NG = T // S

        def turns(eng, expert):
            expert(0, 0)
            expert(1, 1)
            with eng.Fori(1, E // 2) as i:
                expert(i * 2, 0)
                expert(i * 2 + 1, 1)

        block = ctx.enter_context(nc.Block())

        def later(e, n=0):
            return not isinstance(e, int) or e > n

        @block.sync
        def _(sp):
            def load_weights(e, n):
                k = WK[n]
                if later(e) or n:
                    sp.wait_ge(w_split, e * 3 + n)
                sp.dma_start(stage[:].rearrange("p (c i) -> p c i", c=shape[k][1]), w_view[k][e]).then_inc(w_loaded, 16)

            def chunk_in(e, n):
                for x in range(2):
                    for ch in range(DC):
                        src = rows_dram[x, ch, n * NG:(n + 1) * NG, e].rearrange("g p k -> p g k")
                        sp.dma_start(raw(xr[:, n % 2, x, ch, :]).rearrange("p (g k) -> p g k", g=NG), src).then_inc(x_loaded[n % 2], 16)

            def chunk_out(e, n):
                sp.wait_ge(t_out, (e * NT + n) * 2 + 2)
                for g in range(4):
                    b0 = n * RB + g * 4
                    for b in range(4):
                        sp.dma_start(out_dram[b0 + b, e], yr[b * K:(b + 1) * K, g, :]).then_inc(stored, 16)

            def expert(e, par):
                for n in range(NT):
                    t = e * NT + n
                    if later(e) or n >= 2:
                        sp.wait_ge(u_full, (t - 1) * FC)
                    chunk_in(e, n)
                    if later(e) or n:
                        if n:
                            chunk_out(e, n - 1)
                        else:
                            chunk_out(e - 1, NT - 1)
                    if n < 3 and not (isinstance(e, int) and e == E - 1):
                        load_weights(e + 1, n)

            for n in range(3):
                load_weights(0, n)
            expert(0, 0)
            expert(1, 1)
            with sp.Fori(1, E // 2 - 1) as i:
                expert(i * 2, 0)
                expert(i * 2 + 1, 1)
            expert(E - 2, 0)
            expert(E - 1, 1)
            chunk_out(E - 1, NT - 1)
            sp.wait_ge(stored, 16 * 16 * NT * E)

        @block.tensor
        def _(pe):
            def expert(e, par):
                hi, lo = whi[par], wlo[par]
                pe.wait_ge(w_split, (e + 1) * 3)

                def down(n, j):
                    t = (e * NT + n) * FC + j
                    pe.wait_ge(h_ready, t + 1)
                    pe.wait_ge(hhi_ready, t + 1)
                    if j == 0 and (later(e) or n):
                        pe.wait_ge(y_out, (e * NT + n) * 2)
                    for d in range(DC):
                        w1, w2 = hi["d"][:, j, d * P:(d + 1) * P], lo["d"][:, j, d * P:(d + 1) * P]
                        nc.tensor.matmul(y_ps[d][:], w1, hhi[:, j % 2, :], start=(j == 0), stop=False)
                        nc.tensor.matmul(y_ps[d][:], w1, hlo[:, j % 2, :], start=False, stop=False)
                        last = nc.tensor.matmul(y_ps[d][:], w2, hhi[:, j % 2, :], start=False, stop=(j == FC - 1))
                    last.then_inc(h_used, 1)

                def rows(n):
                    t = e * NT + n
                    pe.wait_ge(y_out, (t + 1) * 2)
                    for g in range(4):
                        if g % 2 == 0 and (later(e) or n):
                            pe.wait_ge(t_out, (t - 1) * 2 + g // 2 + 1)
                        for d in range(DC):
                            last = nc.tensor.transpose(t_ps[g // 2][:, g % 2, d * P:(d + 1) * P], yT[:, d, g * P:(g + 1) * P], c["id32"][:])
                        if g % 2:
                            last.then_inc(t_full, 1)

                for n in range(NT):
                    t0 = (e * NT + n) * FC
                    pe.wait_ge(x_loaded[n % 2], (e * (NT // 2) + n // 2 + 1) * 64)
                    for j in range(FC):
                        i = slice(j * P, (j + 1) * P)
                        if later(e) or n or j >= 2:
                            pe.wait_ge(hh_ready, t0 + j - 1)
                        for k, banks, full in (("g", g_ps, g_full), ("u", u_ps, u_full)):
                            for ch in range(DC):
                                nc.tensor.matmul(banks[j % 2][:], hi[k][:, ch, i], xr[:, n % 2, 0, ch, :], start=(ch == 0), stop=False)
                                nc.tensor.matmul(banks[j % 2][:], hi[k][:, ch, i], xr[:, n % 2, 1, ch, :], start=False, stop=False)
                                last = nc.tensor.matmul(banks[j % 2][:], lo[k][:, ch, i], xr[:, n % 2, 0, ch, :], start=False,
                                                        stop=(ch == DC - 1))
                            last.then_inc(full, 1)
                        if j:
                            down(n, j - 1)
                        if j == 1 and n:
                            rows(n - 1)
                    down(n, FC - 1)
                rows(NT - 1)

            turns(pe, expert)

        @block.scalar
        def _(act):
            def split_hi(e, par, n):
                k = WK[n]
                act.wait_ge(w_loaded, (e * 3 + n + 1) * 16)
                if n == 0 and later(e, 1):
                    act.wait_ge(h_used, (e - 1) * NT * FC)
                nc.scalar.activation(whi[par][k][:], stage[:].rearrange("p (c i) -> p c i", c=shape[k][1]), ACT.Copy).then_inc(w_hi, 1)

            def expert(e, par):
                for n in range(NT):
                    for j in range(FC):
                        t = (e * NT + n) * FC + j
                        act.wait_ge(g_full, t + 1)
                        if later(e) or n or j >= 2:
                            act.wait_ge(hh_ready, t - 1)
                        nc.scalar.activation(sg[:, j % 2, :], g_ps[j % 2][:], ACT.Silu).then_inc(sg_ready, 1)
                        if n < 3 and j == 4 and not (isinstance(e, int) and e == E - 1):
                            split_hi(e + 1, 1 - par, n)
                    act.wait_ge(h_used, (e * NT + n + 1) * FC)
                    if later(e) or n:
                        act.wait_ge(t_full, (e * NT + n) * 2)
                    for d in range(DC):
                        nc.scalar.activation(yT[:, d, :], y_ps[d][:], ACT.Copy).then_inc(y_out, 1)

            for n in range(3):
                split_hi(0, 0, n)
            expert(0, 0)
            expert(1, 1)
            with act.Fori(1, E // 2 - 1) as i:
                expert(i * 2, 0)
                expert(i * 2 + 1, 1)
            expert(E - 2, 0)
            expert(E - 1, 1)

        @block.vector
        def _(dve):
            def split_lo(e, par, n):
                k = WK[n]
                dve.wait_ge(w_hi, e * 3 + n + 1)
                nc.vector.tensor_tensor(wlo[par][k][:], stage[:].rearrange("p (c i) -> p c i", c=shape[k][1]), whi[par][k][:],
                                        ALU.subtract).then_inc(w_split, 1)

            def rows_out(e, n):
                for g in range(2):
                    t = (e * NT + n) * 2 + g
                    dve.wait_ge(t_full, t + 1)
                    if g == 0 and (later(e) or n):
                        dve.wait_ge(stored, (e * NT + n) * 16 * 16)
                    nc.vector.tensor_copy(yr[:, 2 * g:2 * g + 2, :], t_ps[g][:]).then_inc(t_out, 1)

            def expert(e, par):
                for n in range(NT):
                    for j in range(FC):
                        t = (e * NT + n) * FC + j
                        dve.wait_ge(sg_ready, t + 1)
                        dve.wait_ge(u_full, t + 1)
                        if later(e) or n or j >= 2:
                            dve.wait_ge(h_used, t - 1)
                        nc.vector.tensor_tensor(hh[:, j % 2, :], u_ps[j % 2][:], sg[:, j % 2, :], ALU.mult).then_inc(hh_ready, 1)
                        dve.wait_ge(hh_ready, t + 1)
                        nc.vector.tensor_copy(hhi[:, j % 2, :], hh[:, j % 2, :]).then_inc(hhi_ready, 1)
                        dve.wait_ge(hhi_ready, t + 1)
                        nc.vector.tensor_tensor(hlo[:, j % 2, :], hh[:, j % 2, :], hhi[:, j % 2, :], ALU.subtract).then_inc(h_ready, 1)
                        if n < 3 and j == 5 and not (isinstance(e, int) and e == E - 1):
                            split_lo(e + 1, 1 - par, n)
                        if n and j == 2:
                            rows_out(e, n - 1)
                rows_out(e, NT - 1)

            for n in range(3):
                split_lo(0, 0, n)
            expert(0, 0)
            expert(1, 1)
            with dve.Fori(1, E // 2 - 1) as i:
                expert(i * 2, 0)
                expert(i * 2 + 1, 1)
            expert(E - 2, 0)
            expert(E - 1, 1)


def combine(nc, c, a, x2_dram, rows_out_dram, y_dram):
    CB = 2
    with ExitStack() as ctx:
        r = Room(nc, ctx, "o")
        rows = r.sb("rows", [P, 2, CB, DC, D], F32)
        xres = r.sb("xres", [P, 2, CB, D], F32)
        rhi = r.sb("rhi", [P, 2, CB, DC, D], F32R)
        rlo = r.sb("rlo", [P, 2, CB, DC, D], F32R)
        hot = r.sb("hot", [P, 2, CB, DC, S], F32R)
        gate = r.sb("gate", [P, 2, CB, DC], F32)
        y = r.sb("y", [P, 2, CB, D], F32)
        ps = [r.ps(f"ps{i}", [P, CB, D], F32) for i in range(2)]
        loaded = [r.sem("loaded0"), r.sem("loaded1")]
        res_loaded = [r.sem("res_loaded0"), r.sem("res_loaded1")]
        stored = [r.sem("stored0"), r.sem("stored1")]
        gate_ready, hi_ready, lo_ready, hot_ready, full, y_ready = (
            r.sem(n) for n in ("gate_ready", "hi_ready", "lo_ready", "hot_ready", "full", "y_ready"))
        rows_v = rows_out_dram.rearrange("(n b) (h e) k d -> n (e k) b h d", b=CB, e=EC)
        x2_v = x2_dram.rearrange("(n b) p d -> n p b d", b=CB)
        y_v = y_dram.rearrange("(n b) p d -> n p b d", b=CB)
        N = B // CB
        block = ctx.enter_context(nc.Block())

        def pairs(eng, step):
            step(0, 0)
            step(1, 1)
            with eng.Fori(1, N // 2) as i:
                step(i * 2, 0)
                step(i * 2 + 1, 1)

        def later(n, k=0):
            return not isinstance(n, int) or n > k

        @block.sync
        def _(sp):
            def step(n, par):
                if later(n, 1):
                    sp.wait_ge(lo_ready, n - 1)
                    sp.wait_ge(y_ready, n - 1)
                sp.dma_start(rows[:, par], rows_v[n]).then_inc(loaded[par], 16)
                sp.dma_start(xres[:, par], x2_v[n]).then_inc(res_loaded[par], 16)

            pairs(sp, step)

        @block.gpsimd
        def _(pool):
            def step(n, par):
                if later(n, 1):
                    pool.wait_ge(full, n - 1)
                nc.gpsimd.tensor_copy(hot[:, par], c["onehotT"][:, bass.ds(n * CB, CB)]).then_inc(hot_ready, 1)

            pairs(pool, step)

        @block.scalar
        def _(act):
            def step(n, par):
                act.wait_ge(gate_ready, n + 1)
                act.wait_ge(loaded[par], (n - par) * 8 + 16)
                if later(n, 1):
                    act.wait_ge(full, n - 1)
                for b in range(CB):
                    for h in range(DC):
                        last = nc.scalar.activation(rhi[:, par, b, h, :], rows[:, par, b, h, :], ACT.Copy,
                                                    scale=gate[:, par, b, h:h + 1])
                last.then_inc(hi_ready, 1)
                act.wait_ge(y_ready, n + 1)
                act.dma_start(y_v[n], y[:, par]).then_inc(stored[par], 16)

            pairs(act, step)
            for par in range(2):
                act.wait_ge(stored[par], 16 * N // 2)

        @block.tensor
        def _(pe):
            def step(n, par):
                pe.wait_ge(hot_ready, n + 1)
                pe.wait_ge(lo_ready, n + 1)
                if later(n, 1):
                    pe.wait_ge(y_ready, n - 1)
                for b in range(CB):
                    for h in range(DC):
                        for part, x in enumerate((rhi, rlo)):
                            last = nc.tensor.matmul(ps[par][:, b, :], hot[:, par, b, h, :], x[:, par, b, h, :],
                                                    start=(h == 0 and part == 0), stop=(h == DC - 1 and part == 1))
                last.then_inc(full, 1)

            pairs(pe, step)

        @block.vector
        def _(dve):
            def step(n, par):
                if later(n, 1):
                    dve.wait_ge(lo_ready, n - 1)
                    dve.wait_ge(hi_ready, n - 1)
                nc.vector.tensor_copy(gate[:, par], c["gating"][:, bass.ds(n * CB, CB), :]).then_inc(gate_ready, 1)
                dve.wait_ge(hi_ready, n + 1)
                for b in range(CB):
                    for h in range(DC):
                        last = nc.vector.scalar_tensor_tensor(out=rlo[:, par, b, h, :], in0=rows[:, par, b, h, :],
                                                              scalar=gate[:, par, b, h:h + 1], in1=rhi[:, par, b, h, :],
                                                              op0=ALU.mult, op1=ALU.subtract)
                last.then_inc(lo_ready, 1)
                dve.wait_ge(full, n + 1)
                dve.wait_ge(res_loaded[par], (n - par) * 8 + 16)
                if later(n, 1):
                    dve.wait_ge(stored[par], (n - par) * 8)
                nc.vector.scalar_tensor_tensor(out=y[:, par], in0=ps[par][:], scalar=c["tg"][:, 1:2], in1=xres[:, par],
                                               op0=ALU.mult, op1=ALU.add).then_inc(y_ready, 1)

            pairs(dve, step)


def program(nc, a, y_dram):
    x2_dram = nc.dram_tensor("x2_scratch", [B, S, D], F32, kind="Internal").ap()
    xln_dram = nc.dram_tensor("xln_scratch", [B, S, D], F32, kind="Internal").ap()
    rows_in = nc.dram_tensor("rows_in", [2, DC, G, E, P, GB * K], F32, kind="Internal").ap()
    rows_out = nc.dram_tensor("rows_out", [B, E, K, D], F32, kind="Internal").ap()
    with ExitStack() as ctx:
        keep = Room(nc, ctx, "keep")
        c = constants(nc, keep, a)
        attention(nc, c, a, x2_dram, xln_dram)
        c["onehotT"] = keep.sb("onehotT", [P, B, DC, S], BF16)
        gather(nc, c, a, xln_dram, rows_in)
        experts(nc, c, a, rows_in, rows_out)
        combine(nc, c, a, x2_dram, rows_out, y_dram)


def kernel(x, ctx_1024, mask_BxSxS2_ff1, g_xattn, g_ffn, L0_xattn_Wq, L0_xattn_bq, L0_xattn_Wk, L0_xattn_bk,
           L0_xattn_Wv, L0_xattn_bv, L0_xattn_Wo, L0_xattn_bo, L0_ffn_gate_w, L0_ffn_w_gate, L0_ffn_w_up, L0_ffn_w_down):
    import numpy as np
    import concourse.bacc as bacc
    from concourse.bass_utils import run_bass_kernel_spmd

    n = np.asarray
    arrays = {
        "x": n(x), "ctxT": n(ctx_1024).reshape(B * S, D).T, "mask": n(mask_BxSxS2_ff1), "g_xattn": n(g_xattn), "g_ffn": n(g_ffn),
        "wqT": n(L0_xattn_Wq).T, "wkT": n(L0_xattn_Wk).T, "wvT": n(L0_xattn_Wv).T, "woT": n(L0_xattn_Wo).T,
        "bq": n(L0_xattn_bq), "bk": n(L0_xattn_bk), "bv": n(L0_xattn_bv), "bo": n(L0_xattn_bo),
        "gateT": n(L0_ffn_gate_w).T, "wgT": n(L0_ffn_w_gate).transpose(0, 2, 1), "wuT": n(L0_ffn_w_up).transpose(0, 2, 1),
        "wdT": n(L0_ffn_w_down).transpose(0, 2, 1),
    }
    arrays = {k: np.ascontiguousarray(v) for k, v in arrays.items()}
    nc = bacc.Bacc("TRN2", target_bir_lowering=False, num_devices=1)
    aps = {k: nc.dram_tensor(k, v.shape, mybir.dt.from_np(v.dtype), kind="ExternalInput").ap() for k, v in arrays.items()}
    y = nc.dram_tensor("y", (B, S, D), F32, kind="ExternalOutput").ap()
    program(nc, aps, y)
    out = run_bass_kernel_spmd(nc, [arrays], core_ids=[0])
    return out.results[0]["y"]
```

```python
from contextlib import ExitStack

import concourse.bass as bass
from concourse import mybir

F32 = mybir.dt.float32
F32R = mybir.dt.float32r
F16 = mybir.dt.float16
BF16 = mybir.dt.bfloat16
ALU = mybir.AluOpType
ACT = mybir.ActivationFunctionType
AXX = mybir.AxisListType.X

B, S, D = 64, 128, 256
H, DH = 16, 16
E, FF, K = 8, 1024, 32
P = 128
DC = D // P
FC = FF // P
GB = 4
G = B // GB
T = GB * S
HU = 4
UB = H // HU
U = GB * UB
HC = P // DH
VP = 3 * DH
EPS = 1e-5
RB = P // E
RT = B // RB
EC = P // K
SLOTS = B * K
NT = SLOTS // 512


class Chain:

    def __init__(self, eng, sem, base=0):
        self.eng, self.sem, self.base, self.n = eng, sem, base, 0

    def mark(self, ins):
        self.n += 1
        ins.then_inc(self.sem, 1)

    def settle(self):
        self.eng.wait_ge(self.sem, self.base + self.n)

    def link(self, ins):
        self.mark(ins)
        self.settle()


WK = ("g", "u", "d")


class Room:

    def __init__(self, nc, ctx, tag):
        self.nc, self.ctx, self.tag = nc, ctx, tag

    def sb(self, name, shape, dt):
        return self.ctx.enter_context(self.nc.sbuf_tensor(f"{self.tag}_{name}", shape, dt))

    def ps(self, name, shape, dt):
        return self.ctx.enter_context(self.nc.psum_tensor(f"{self.tag}_{name}", shape, dt))

    def sem(self, name):
        return self.ctx.enter_context(self.nc.semaphore(f"{self.tag}_{name}"))


def raw(ap):
    return ap.bitcast(F32)


def constants(nc, keep, a):
    c = {
        "id32": keep.sb("id32", [P, P], F32),
        "id16": keep.sb("id16", [P, P], F16),
        "idb": keep.sb("idb", [P, P], BF16),
        "slot": keep.sb("slot", [P, K], F32),
        "own": keep.sb("own", [P, DC, 3, E], F32),
        "tg": keep.sb("tg", [P, 2], F32),
        "aff": keep.sb("aff", [P, B * E], F32),
        "gating": keep.sb("gating", [P, B, DC], F32),
    }
    with ExitStack() as ctx:
        r = Room(nc, ctx, "c")
        g = r.sb("g", [P, 2], F32)
        loaded, pooled, pool_link = r.sem("loaded"), r.sem("pooled"), r.sem("pool_link")
        block = ctx.enter_context(nc.Block())

        @block.sync
        def _(sp):
            sp.dma_start(g[:, 0:1], a["g_xattn"].partition_broadcast(P)).then_inc(loaded, 16)
            sp.dma_start(g[:, 1:2], a["g_ffn"].partition_broadcast(P)).then_inc(loaded, 16)

        @block.scalar
        def _(act):
            act.wait_ge(loaded, 32)
            nc.scalar.activation(c["tg"][:], g[:], ACT.Tanh).then_inc(pooled, 1)

        @block.gpsimd
        def _(pool):
            chain = Chain(pool, pool_link)
            for name in ("id32", "id16", "idb"):
                chain.mark(nc.gpsimd.memset(c[name][:], 0.0))
            chain.mark(nc.gpsimd.memset(c["own"][:], 1.0))
            chain.mark(nc.gpsimd.iota(c["slot"][:], pattern=[[1, K]], base=0, channel_multiplier=0,
                                      allow_small_or_imprecise_dtypes=True))
            chain.settle()
            for name in ("id32", "id16", "idb"):
                chain.mark(nc.gpsimd.affine_select(out=c[name][:], in_=c[name][:], compare_op=ALU.not_equal, fill=1.0,
                                                   base=0, pattern=[[-1, P]], channel_multiplier=1))
            for half in range(DC):
                v = c["own"][:, half, :, :]
                for sign, base in ((1, K * EC * half), (-1, K - 1 - K * EC * half)):
                    chain.link(nc.gpsimd.affine_select(out=v, in_=v, compare_op=ALU.is_ge, fill=0.0, base=base,
                                                       pattern=[[0, 3], [-sign * K, E]], channel_multiplier=sign))
            chain.settle()
    return c


LE, LH, LO, LT, LP, LD = 0, 2, 2, 4, 5, 6


def attention(nc, c, a, x2_dram, xln_dram):
    with ExitStack() as ctx:
        r = Room(nc, ctx, "a")
        WN = ("q", "k", "v", "o")
        wraw = r.sb("wraw", [P, DC, D], F32)
        whi = {n: r.sb(f"w{n}hi", [P, DC, D], F32R) for n in WN}
        wlo = {n: r.sb(f"w{n}lo", [P, DC, D], F32R) for n in WN}
        gateT = r.sb("gateT", [P, DC, E], F32)
        bqk = r.sb("bqk", [P, 2, DC], F32)
        bvo = r.sb("bvo", [P, 2, D], F32)
        minus_half = r.sb("minus_half", [P, GB], F32)
        after = r.sb("after", [P, 4], F32)
        eps = r.sb("eps", [P, GB], F32)
        x_in = r.sb("x_in", [P, GB, D], F32)
        x_res = r.sb("x_res", [P, GB, D], F32)
        yT = r.sb("yT", [P, DC, T], F32)
        yhi = r.sb("yhi", [P, DC, T], F32R)
        ylo = r.sb("ylo", [P, DC, T], F32R)
        mask = wraw[:].rearrange("p c n -> p (c n)").rearrange("p (b q) -> p b q", b=GB)
        far = r.sb("far", [P, 2, GB, S], F32)
        stats = r.sb("stats", [P, 2, GB, 6], F32)
        mv = r.sb("mv", [P, 2, GB, 2], F32)
        rstd = r.sb("rstd", [P, 2, GB], F32)
        xn = r.sb("xn", [P, GB, D], F32)
        xnhi = r.sb("xnhi", [P, DC, T], F32R)
        xnlo = r.sb("xnlo", [P, DC, T], F32R)
        qhi = r.sb("qhi", [P, 2, DC, T], F32R)
        qlo = r.sb("qlo", [P, 2, DC, T], F32R)
        kk = r.sb("kk", [P, 2, DC, T], F32R)
        kb = [r.sb(f"kb{i}", [P, 2, DC, HC, 2 * S], F32R) for i in range(2)]
        v32 = r.sb("v32", [P, 2, D], F32)
        vr = r.sb("vr", [P, 2, D], F32)
        v3 = r.sb("v3", [P, 2, GB, H, 3, DH], BF16)
        negs = r.sb("negs", [P, 2, HU, S], F32)
        negmax = r.sb("negmax", [P, 2, HU], F32)
        prob = r.sb("prob", [P, 4, HU, S], F32)
        sums = r.sb("sums", [P, GB, H], F32)
        rinv = r.sb("rinv", [P, 2, H], F32)
        phl = r.sb("phl", [P, 4, 2, HU, S], F16)
        pT = r.sb("pT", [P, 2, 2, HU, S], F16)
        osum = r.sb("osum", [P, 2, H // 2, DH], F32)
        on = r.sb("on", [P, 2, GB, D], F32)
        ohi, olo = xnhi, xnlo
        x2 = r.sb("x2", [P, GB, D], F32)
        xln = r.sb("xln", [P, GB, D], F32)
        xlnT = x_in[:].rearrange("p b d -> p (b d)").rearrange("p (c t) -> p c t", c=DC)
        lg = r.sb("lg", [P, GB, E], F32)
        lgx = r.sb("lgx", [P, GB, E], F32)
        lmax = r.sb("lmax", [P, GB], F32)
        lsum = r.sb("lsum", [P, GB], F32)
        score_ps = [r.ps(f"score{i}", [P, HU, S], F32) for i in range(2)]
        pT_ps = [r.ps(f"pT_ps{i}", [P, 2, HU, S], F16) for i in range(2)]
        o_ps = [r.ps(f"o_ps{i}", [P, 512], F32) for i in range(2)]
        m_ps = [r.ps(f"m_ps{i}", [P, 512], F32) for i in range(2)]

        w_loaded, w_split, w_link = r.sem("w_loaded"), r.sem("w_split"), r.sem("w_link")
        w_hi = r.sem("w_hi")
        const_loaded, bias_ready = r.sem("const_loaded"), r.sem("bias_ready")
        kb_zero = r.sem("kb_zero")
        x_loaded, y_loaded, mask_loaded, xres_loaded = (r.sem(n) for n in ("x_loaded", "y_loaded", "mask_loaded", "xres_loaded"))
        y_split, yhi_ready = r.sem("y_split"), r.sem("yhi_ready")
        ln_link, ln2_link, soft_link, on_link = (r.sem(n) for n in ("ln_link", "ln2_link", "soft_link", "on_link"))
        stats_ready, rstd_ready, xn_ready, rstd_link = (r.sem(n) for n in ("stats_ready", "rstd_ready", "xn_ready", "rstd_link"))
        xnT_full, xnhi_ready, xn_split = r.sem("xnT_full"), r.sem("xnhi_ready"), r.sem("xn_split")
        q_full, qhi_ready, q_split = r.sem("q_full"), r.sem("qhi_ready"), r.sem("q_split")
        k_full, khi_ready, k_split = r.sem("k_full"), r.sem("khi_ready"), r.sem("k_split")
        k_spread = [r.sem("k_spread0"), r.sem("k_spread1")]
        v_full, v_ready, far_ready = r.sem("v_full"), r.sem("v_ready"), r.sem("far_ready")
        v32_ready, v1_ready, vr_ready, v2_ready = (r.sem(n) for n in ("v32_ready", "v1_ready", "vr_ready", "v2_ready"))
        score_full, negs_ready, prob_ready = r.sem("score_full"), r.sem("negs_ready"), r.sem("prob_ready")
        phi_ready, plo_ready = r.sem("phi_ready"), r.sem("plo_ready")
        pT_full, pv_done = r.sem("pT_full"), r.sem("pv_done")
        pT_out = [r.sem("pT_out_even"), r.sem("pT_out_odd")]
        o_read, on_ready = r.sem("o_read"), r.sem("on_ready")
        oT_full, ohi_ready, o_split = r.sem("oT_full"), r.sem("ohi_ready"), r.sem("o_split")
        wo_full, x2_ready, stats2_ready, rstd2_ready, xln_ready = (
            r.sem(n) for n in ("wo_full", "x2_ready", "stats2_ready", "rstd2_ready", "xln_ready"))
        xres_biased = r.sem("xres_biased")
        xlnT_full, xlnT_out, lg_full, lg_out, lgx_ready, aff_ready = (
            r.sem(n) for n in ("xlnT_full", "xlnT_out", "lg_full", "lg_out", "lgx_ready", "aff_ready"))
        x2_stored, xln_stored = r.sem("x2_stored"), r.sem("xln_stored")

        x_v = a["x"].rearrange("(g b) p d -> g p b d", b=GB)
        y_v = a["ctxT"].rearrange("(c p) (g t) -> g p c t", p=P, t=T)
        mask_v = a["mask"].rearrange("(g b) q k -> g q b k", b=GB)
        x2_v = x2_dram.rearrange("(g b) p d -> g p b d", b=GB)
        xln_v = xln_dram.rearrange("(g b) p d -> g p b d", b=GB)

        def steps(eng, step):
            step(-1, 1, False, False, False, True)
            step(0, 0, True, False, False, True)
            step(1, 1, True, True, False, True)
            step(2, 0, True, True, True, True)
            step(3, 1, True, True, True, True)
            with eng.Fori(2, G // 2 - 1) as i:
                step(i * 2, 0, True, True, True, True)
                step(i * 2 + 1, 1, True, True, True, True)
            step(G - 2, 0, True, True, True, True)
            step(G - 1, 1, True, True, True, False)
            step(G, 0, False, True, True, False)
            step(G + 1, 1, False, False, True, False)

        def by_head(t):
            return t[:].rearrange("p b (h d) -> p (b h) d", d=DH)

        def v_parts(par, n):
            return [v3[:, par, 2 * n:2 * n + 2, :, i, :].rearrange("p b h d -> p (b h) d") for i in range(3)]

        def lagging(g, s, lag, has_b, has_c):
            if s >= lag:
                return (s - lag, 1, (g - 1) * U + s - lag) if has_b else None
            return (s - lag + U, 2, (g - 2) * U + s - lag + U) if has_c else None

        def early(n, first):
            return isinstance(n, int) and n < first

        A_XT, A_Q, A_K, A_V = 0, 1, 3, 4
        C_OT, C_WO, C_LNT, C_LG = 8, 9, 14, 15
        C_RSTD = 13
        L_STATS, L_Y, L_XN, A_FAR = 7, 8, 10, 3
        block = ctx.enter_context(nc.Block())

        @block.sync
        def _(sp):
            for n, name in enumerate(WN):
                if n:
                    sp.wait_ge(w_split, n)
                sp.dma_start(wraw[:], a[f"w{name}T"].rearrange("(c p) n -> p c n", p=P)).then_inc(w_loaded, 16)
            sp.dma_start(gateT[:], a["gateT"].rearrange("(c p) n -> p c n", p=P)).then_inc(const_loaded, 16)
            with nc.allow_non_contiguous_dma(reason="bias columns, once"):
                sp.dma_start(bqk[:, 0, :], a["bq"].rearrange("(c p) -> p c", p=P)).then_inc(const_loaded, 16)
                sp.dma_start(bqk[:, 1, :], a["bk"].rearrange("(c p) -> p c", p=P)).then_inc(const_loaded, 16)
            sp.dma_start(bvo[:, 0, :], a["bv"].partition_broadcast(P)).then_inc(const_loaded, 16)
            sp.dma_start(bvo[:, 1, :], a["bo"].partition_broadcast(P)).then_inc(const_loaded, 16)

            def step(g, par, has_a, has_b, has_c, has_l):
                if has_l:
                    if not early(g, 0):
                        if not early(g, 3):
                            sp.wait_ge(lg_full, g - 2)
                        sp.wait_ge(y_split, (g + 1) * 2)
                        sp.wait_ge(xn_ready, g + 1)
                    sp.dma_start(x_in[:], x_v[g + 1]).then_inc(x_loaded, 16)
                    sp.dma_start(yT[:], y_v[g + 1]).then_inc(y_loaded, 16)
                if has_a:
                    if not early(g, 1):
                        sp.wait_ge(far_ready, g)
                    else:
                        sp.wait_ge(w_split, 4)
                    sp.dma_start(mask, mask_v[g]).then_inc(mask_loaded, 16)
                if has_c:
                    if not early(g, 3):
                        sp.wait_ge(x2_ready, (g - 2) * 2)
                    sp.dma_start(x_res[:], x_v[g - 2]).then_inc(xres_loaded, 16)
                for pair in range(2):
                    if has_a:
                        sp.wait_ge(k_split, (g + 1) * 2)
                        if not early(g, 1):
                            sp.wait_ge(score_full, g * U - U // 2 + pair * U // 2)
                        for h in range(HC):
                            for x in range(2):
                                sp.dma_start(raw(kb[pair][h * DH:(h + 1) * DH, x, :, h, :]),
                                             raw(kk[h * DH:(h + 1) * DH, x, :, pair * 2 * S:(pair + 1) * 2 * S])
                                             ).then_inc(k_spread[pair], 16)
                    if has_c and pair == 0:
                        sp.wait_ge(x2_ready, (g - 1) * 2)
                        sp.dma_start(x2_v[g - 2], x2[:]).then_inc(x2_stored, 16)
                if has_c:
                    sp.wait_ge(xln_ready, g - 1)
                    sp.dma_start(xln_v[g - 2], xln[:]).then_inc(xln_stored, 16)

            sp.wait_ge(kb_zero, 2)
            steps(sp, step)
            sp.wait_ge(x2_stored, 16 * G)
            sp.wait_ge(xln_stored, 16 * G)

        @block.gpsimd
        def _(pool):
            nc.gpsimd.memset(eps[:], EPS)
            nc.gpsimd.memset(minus_half[:], -0.5).then_inc(rstd_link, 1)
            for i in range(2):
                nc.gpsimd.memset(raw(kb[i][:]), 0.0).then_inc(kb_zero, 1)
            pool.wait_ge(rstd_link, 1)
            pool.wait_ge(bias_ready, 1)

            def rsqrt(n, ready, done, base):
                nc.gpsimd.tensor_tensor(rstd[:, n, :], mv[:, n, :, 1], eps[:], ALU.add).then_inc(rstd_link, 1)
                pool.wait_ge(rstd_link, base)
                nc.gpsimd.tensor_tensor(rstd[:, n, :], rstd[:, n, :], minus_half[:], ALU.pow).then_inc(done, 1)

            def step(g, par, has_a, has_b, has_c, has_l):
                for s in range(U):
                    if at := lagging(g, s, LO, has_b, has_c):
                        v, back, u = at
                        pool.wait_ge(phi_ready, u + 1)
                        nc.gpsimd.tensor_tensor(phl[:, v % 4, 1], prob[:, v % 4], phl[:, v % 4, 0],
                                                ALU.subtract).then_inc(plo_ready, 1)
                    if has_l and s == L_STATS:
                        pool.wait_ge(stats_ready, g + 2)
                        rsqrt(0, stats_ready, rstd_ready, 1 + (g + 2) + (0 if early(g, 2) else g - 2))
                    if has_l and s == L_Y:
                        for h in range(DC):
                            pool.wait_ge(yhi_ready, g + 2)
                            nc.gpsimd.tensor_tensor(ylo[:, h, :], yT[:, h, :], yhi[:, h, :], ALU.subtract).then_inc(y_split, 1)
                    if has_c and s == 4:
                        pool.wait_ge(xres_loaded, (g - 1) * 16)
                        nc.gpsimd.tensor_tensor(x_res[:], x_res[:], bvo[:, 1:2, :].to_broadcast([P, GB, D]),
                                                ALU.add).then_inc(xres_biased, 1)
                    if has_c and s == C_RSTD:
                        pool.wait_ge(stats2_ready, g - 1)
                        norms = G if isinstance(g, int) and g >= G - 1 else g + 2
                        rsqrt(1, stats2_ready, rstd2_ready, 1 + norms + (g - 1))
                    if has_a and s in (A_V + 1, A_V + 3):
                        n = (s - A_V) // 2
                        pool.wait_ge(v1_ready, g * 2 + n + 1)
                        nc.gpsimd.tensor_tensor(by_head(vr), by_head(v32), v_parts(par, n)[0], ALU.subtract).then_inc(vr_ready, 1)
                    if has_a and s in (A_V + 2, A_V + 4):
                        n = (s - A_V) // 2 - 1
                        pool.wait_ge(v2_ready, g * 2 + n + 1)
                        nc.gpsimd.tensor_tensor(v_parts(par, n)[2], by_head(vr), v_parts(par, n)[1], ALU.subtract).then_inc(v_ready, 1)

            steps(pool, step)

        @block.tensor
        def _(pe):
            pe.wait_ge(w_split, 4)
            pe.wait_ge(const_loaded, 80)

            def three(out, whi_, wlo_, xhi_, xlo_, first, last):
                nc.tensor.matmul(out, whi_, xhi_, start=first, stop=False)
                nc.tensor.matmul(out, whi_, xlo_, start=False, stop=False)
                return nc.tensor.matmul(out, wlo_, xhi_, start=False, stop=last)

            def step(g, par, has_a, has_b, has_c, has_l):
                old = 1 - par

                def scores(g, old, s):
                    b, m = s // UB, s % UB
                    ch, h0 = m // 2, (m % 2) * HU
                    pair, t = b // 2, slice((b % 2) * S, (b % 2 + 1) * S)
                    u = (g - 1) * U + s
                    if s == 0:
                        pe.wait_ge(q_split, g * 2)
                    if s % (U // 2) == 0:
                        pe.wait_ge(k_spread[pair], g * 16 * 2 * HC)
                    if not isinstance(g, int) or g > 1 or s >= 2:
                        pe.wait_ge(negs_ready, u - 1)
                    q1 = qhi[:, old, ch, b * S:(b + 1) * S]
                    q2 = qlo[:, old, ch, b * S:(b + 1) * S]
                    k1 = kb[pair][:, 0, ch, h0:h0 + HU, t]
                    k2 = kb[pair][:, 1, ch, h0:h0 + HU, t]
                    three(score_ps[s % 2][:], q1, q2, k1, k2, True, True).then_inc(score_full, 1)

                def transposes(v, back, u):
                    pe.wait_ge(plo_ready, u + 1)
                    if not early(u, 2):
                        pe.wait_ge(pT_out[v % 2], (g - back) * (U // 2) + v // 2)
                    for part in range(2):
                        for h in range(HU):
                            last = nc.tensor.transpose(pT_ps[v % 2][:, part, h, :], phl[:, v % 4, part, h, :], c["id16"][:])
                    last.then_inc(pT_full, 1)

                def values(v, back, u):
                    b, m = v // UB, v % UB
                    pe.wait_ge(v_ready, (g - back + 1) * 2)
                    pe.wait_ge(pT_out[v % 2], (g - back) * (U // 2) + v // 2 + 1)
                    if m % 2 == 0 and not early(u, UB):
                        pe.wait_ge(o_read, (g - back) * GB * 2 + b * 2 + m // 2 - 1)
                    bank = o_ps[m // 2]
                    for h in range(HU):
                        at = ((m % 2) * HU + h) * VP
                        for part in range(2):
                            last = nc.tensor.matmul(bank[:, at:at + VP], pT[:, v % 2, part, h, :],
                                                    v3[:, old if back == 1 else par, b, m * HU + h, :, :].rearrange("p n d -> p (n d)"),
                                                    start=(part == 0), stop=(part == 1))
                    last.then_inc(pv_done, 1)

                for s in range(U):
                    if at := lagging(g, s, LT, has_b, has_c):
                        transposes(*at)
                    if at := lagging(g, s, LP, has_b, has_c):
                        values(*at)
                    if has_b and s + 1 < U:
                        scores(g, old, s + 1)
                    if has_a and s + 1 == U:
                        scores(g + 1, par, 0)
                    if has_c and s == C_OT:
                        pe.wait_ge(on_ready, (g - 1) * GB * 2)
                        if has_a:
                            pe.wait_ge(v32_ready, (g + 1) * 2)
                        else:
                            pe.wait_ge(v32_ready, G * 2)
                            pe.wait_ge(lgx_ready, g - 2)
                        for ch in range(DC):
                            for b in range(GB):
                                last = nc.tensor.transpose(m_ps[ch][:, b * S:(b + 1) * S],
                                                           on[:, par, b, ch * P:(ch + 1) * P], c["id32"][:])
                            last.then_inc(oT_full, 1)
                    if has_c and C_WO <= s < C_WO + GB:
                        b = s - C_WO
                        if b == 0:
                            pe.wait_ge(o_split, (g - 1) * 2)
                        t = slice(b * S, (b + 1) * S)
                        for ch in range(DC):
                            last = three(m_ps[b // 2][:, (b % 2) * D:(b % 2 + 1) * D], ohi[:, ch, t], olo[:, ch, t],
                                         whi["o"][:, ch, :], wlo["o"][:, ch, :], ch == 0, ch == DC - 1)
                        if b % 2:
                            last.then_inc(wo_full, 1)
                    if has_c and s == C_LNT:
                        pe.wait_ge(xln_ready, g - 1)
                        for ch in range(DC):
                            for b in range(GB):
                                last = nc.tensor.transpose(m_ps[ch][:, b * S:(b + 1) * S],
                                                           xln[:, b, ch * P:(ch + 1) * P], c["id32"][:])
                            last.then_inc(xlnT_full, 1)
                    if has_c and s == C_LG:
                        pe.wait_ge(xlnT_out, (g - 1) * 2)
                        for b in range(GB):
                            for ch in range(DC):
                                last = nc.tensor.matmul(m_ps[0][:, b * E:(b + 1) * E], xlnT[:, ch, b * S:(b + 1) * S],
                                                        gateT[:, ch, :], start=(ch == 0), stop=(ch == DC - 1))
                        last.then_inc(lg_full, 1)
                    if has_a and s == A_XT:
                        pe.wait_ge(xn_ready, g + 1)
                        if not early(g, 3):
                            pe.wait_ge(lgx_ready, g - 2)
                            pe.wait_ge(xlnT_out, (g - 2) * 2)
                        elif not early(g, 1):
                            pe.wait_ge(v32_ready, g * 2)
                        for ch in range(DC):
                            for b in range(GB):
                                last = nc.tensor.transpose(m_ps[ch][:, b * S:(b + 1) * S],
                                                           xn[:, b, ch * P:(ch + 1) * P], c["id32"][:])
                            last.then_inc(xnT_full, 1)
                    if has_a and s in (A_Q, A_K):
                        name, hi, lo, full = ("q", xnhi, xnlo, q_full) if s == A_Q else ("k", yhi, ylo, k_full)
                        if s == A_Q:
                            pe.wait_ge(xn_split, (g + 1) * 2)
                        else:
                            pe.wait_ge(y_split, (g + 1) * 2)
                            pe.wait_ge(yhi_ready, g + 1)
                            pe.wait_ge(q_split, (g + 1) * 2)
                        for n in range(DC):
                            for ch in range(DC):
                                last = three(m_ps[n][:], whi[name][:, ch, n * P:(n + 1) * P],
                                             wlo[name][:, ch, n * P:(n + 1) * P], hi[:, ch, :], lo[:, ch, :],
                                             ch == 0, ch == DC - 1)
                            last.then_inc(full, 1)
                    if has_a and A_V <= s < A_V + GB:
                        b = s - A_V
                        if b == 0:
                            pe.wait_ge(k_split, (g + 1) * 2)
                        t = slice(b * S, (b + 1) * S)
                        for ch in range(DC):
                            last = three(m_ps[b // 2][:, (b % 2) * D:(b % 2 + 1) * D], yhi[:, ch, t], ylo[:, ch, t],
                                         whi["v"][:, ch, :], wlo["v"][:, ch, :], ch == 0, ch == DC - 1)
                        if b % 2:
                            last.then_inc(v_full, 1)

            steps(pe, step)

        @block.scalar
        def _(act):
            for n, name in enumerate(WN):
                act.wait_ge(w_loaded, 16 * (n + 1))
                nc.scalar.activation(whi[name][:], wraw[:], ACT.Copy, scale=-0.25 if name == "q" else 1.0).then_inc(w_hi, 1)
            act.wait_ge(bias_ready, 1)

            def softmax(g):
                act.wait_ge(lgx_ready, g - 1)
                nc.scalar.activation(lgx[:], lg[:], ACT.Exp).then_inc(lg_out, 1)

            def step(g, par, has_a, has_b, has_c, has_l):
                for s in range(U):
                    if at := lagging(g, s, LE, has_b, has_c):
                        v, back, u = at
                        b, m = v // UB, v % UB
                        act.wait_ge(negs_ready, u + 1)
                        if not early(u, 4):
                            act.wait_ge(plo_ready, u - 3)
                        if m == 0 and not early(u, U):
                            act.wait_ge(on_ready, (g - back - 1) * GB * 2 + (b + 1) * 2)
                        for h in range(HU):
                            last = nc.scalar.activation(prob[:, v % 4, h, :], negs[:, v % 2, h, :], ACT.Exp, scale=-1.0,
                                                        bias=negmax[:, v % 2, h:h + 1],
                                                        accum_out=sums[:, b, m * HU + h:m * HU + h + 1])
                        last.then_inc(prob_ready, 1)
                    if s == 0 and not early(g, 3):
                        softmax(g - 1)
                    if (at := lagging(g, s, LT, has_b, has_c)) and at[0] % 2 == 0:
                        v, back, u = at
                        act.wait_ge(pT_full, u + 1)
                        if not early(u, 2):
                            act.wait_ge(pv_done, u - 1)
                        nc.scalar.activation(pT[:, 0], pT_ps[0][:], ACT.Copy).then_inc(pT_out[0], 1)
                    if has_c and s == C_OT:
                        for ch in range(DC):
                            act.wait_ge(oT_full, (g - 2) * 2 + ch + 1)
                            act.wait_ge(q_full, (g + 1 if has_a else G) * 2)
                            nc.scalar.activation(ohi[:, ch, :], m_ps[ch][:], ACT.Copy).then_inc(ohi_ready, 1)
                    if has_c and s == C_LNT:
                        for ch in range(DC):
                            act.wait_ge(xlnT_full, (g - 2) * 2 + ch + 1)
                            act.wait_ge(xn_ready, g + 2 if has_l else G)
                            nc.scalar.activation(xlnT[:, ch, :], m_ps[ch][:], ACT.Copy).then_inc(xlnT_out, 1)
                    if has_a and s == A_XT:
                        for ch in range(DC):
                            act.wait_ge(xnT_full, g * 2 + ch + 1)
                            if not early(g, 3):
                                act.wait_ge(wo_full, (g - 2) * 2)
                            elif not early(g, 1):
                                act.wait_ge(q_full, g * 2)
                            nc.scalar.activation(xnhi[:, ch, :], m_ps[ch][:], ACT.Copy).then_inc(xnhi_ready, 1)
                    if has_a and s == A_Q:
                        for ch in range(DC):
                            act.wait_ge(q_full, g * 2 + ch + 1)
                            if not early(g, 2):
                                act.wait_ge(score_full, (g - 1) * U)
                            nc.scalar.activation(qhi[:, par, ch, :], m_ps[ch][:], ACT.Identity,
                                                 bias=bqk[:, 0, ch:ch + 1]).then_inc(qhi_ready, 1)
                    if has_a and s == A_K:
                        for ch in range(DC):
                            act.wait_ge(k_full, g * 2 + ch + 1)
                            if not isinstance(g, int) or g > 0:
                                for pair in range(2):
                                    act.wait_ge(k_spread[pair], g * 16 * 2 * HC)
                            nc.scalar.activation(kk[:, 0, ch, :], m_ps[ch][:], ACT.Identity,
                                                 bias=bqk[:, 1, ch:ch + 1]).then_inc(khi_ready, 1)

                    if has_a and s in (A_V + 1, A_V + 3):
                        n = (s - A_V) // 2
                        act.wait_ge(v32_ready, g * 2 + n + 1)
                        if not early(g, 2):
                            act.wait_ge(pv_done, (g - 1) * U)
                        nc.scalar.activation(v_parts(par, n)[0], by_head(v32), ACT.Copy).then_inc(v1_ready, 1)
                    if has_a and s in (A_V + 2, A_V + 4):
                        n = (s - A_V) // 2 - 1
                        act.wait_ge(vr_ready, g * 2 + n + 1)
                        nc.scalar.activation(v_parts(par, n)[1], by_head(vr), ACT.Copy).then_inc(v2_ready, 1)

            steps(act, step)
            softmax(G + 1)

        @block.vector
        def _(dve):
            for n, name in enumerate(WN):
                dve.wait_ge(w_hi, n + 1)
                nc.vector.scalar_tensor_tensor(out=wlo[name][:], in0=wraw[:], scalar=-0.25 if name == "q" else 1.0,
                                               in1=whi[name][:], op0=ALU.mult, op1=ALU.subtract).then_inc(w_split, 1)
            dve.wait_ge(const_loaded, 80)
            nc.vector.tensor_scalar(bvo[:, 1, :], bvo[:, 1, :], c["tg"][:, 0:1], None, ALU.mult).then_inc(w_link, 1)
            nc.vector.tensor_scalar(bqk[:, 0, :], bqk[:, 0, :], -0.25, None, ALU.mult).then_inc(w_link, 1)
            dve.wait_ge(w_link, 2)
            nc.vector.tensor_copy(after[:, 0:2], bqk[:, 0, :]).then_inc(bias_ready, 1)

            def norm(x_tile, out, n, chain, ready, rstd_done, count, done):
                for b in range(GB):
                    chain.mark(nc.vector.bn_stats(stats[:, n, b, :], x_tile[:, b, :]))
                chain.settle()
                nc.vector.tensor_copy(after[:, 2 + n:3 + n], stats[:, n, 0, 0:1])
                for b in range(GB):
                    last = nc.vector.bn_aggr(mv[:, n, b, :], stats[:, n, b, :])
                last.then_inc(ready, 1)

            def normalise(x_tile, out, n, rstd_done, count, done):
                dve.wait_ge(rstd_done, count)
                for b in range(GB):
                    last = nc.vector.tensor_scalar(out[:, b, :], x_tile[:, b, :], mv[:, n, b, 0:1], rstd[:, n, b:b + 1],
                                                   ALU.subtract, ALU.mult)
                last.then_inc(done, 1)

            def softmax(g):
                chain = Chain(dve, soft_link, (g - 2) * 5)
                dve.wait_ge(lg_full, g - 1)
                l3 = m_ps[0][:, 0:GB * E].rearrange("p (b e) -> p b e", e=E)
                chain.link(nc.vector.tensor_reduce(lmax[:], l3, AXX, ALU.max))
                nc.vector.tensor_tensor(lg[:], l3, lmax[:].unsqueeze(2).to_broadcast([P, GB, E]),
                                        ALU.subtract).then_inc(lgx_ready, 1)
                return chain

            def softmax_end(g, chain):
                dve.wait_ge(lg_out, g - 1)
                chain.link(nc.vector.tensor_reduce(lsum[:], lgx[:], AXX, ALU.add))
                chain.link(nc.vector.reciprocal(lmax[:], lsum[:]))
                chain.link(nc.vector.tensor_tensor(lgx[:], lgx[:], lmax[:].unsqueeze(2).to_broadcast([P, GB, E]), ALU.mult))
                chain.link(nc.vector.tensor_copy(c["aff"][:, bass.ds((g - 2) * (GB * E), GB * E)],
                                                 lgx[:].rearrange("p b e -> p (b e)")))

            def step(g, par, has_a, has_b, has_c, has_l):
                old = 1 - par
                for s in range(U):
                    if has_b:
                        u = (g - 1) * U + s
                        b = s // UB
                        dve.wait_ge(score_full, u + 1)
                        if s == 0:
                            dve.wait_ge(far_ready, g)
                        if not early(u, 2):
                            dve.wait_ge(prob_ready, u - 1)
                        nc.vector.tensor_copy(after[:, s % 2:s % 2 + 1], score_ps[s % 2][:, 0, 0:1])
                        for h in range(HU):
                            last = nc.vector.tensor_tensor_reduce(
                                out=negs[:, s % 2, h, :], in0=score_ps[s % 2][:, h, :], in1=far[:, old, b, :], scale=1.0,
                                scalar=3.0e38, op0=ALU.add, op1=ALU.min, accum_out=negmax[:, s % 2, h:h + 1])
                        last.then_inc(negs_ready, 1)
                    if has_c and s == C_OT + 1:
                        for ch in range(DC):
                            dve.wait_ge(ohi_ready, (g - 2) * 2 + ch + 1)
                            nc.vector.tensor_tensor(olo[:, ch, :], m_ps[ch][:], ohi[:, ch, :], ALU.subtract).then_inc(o_split, 1)
                    if has_a and s == A_XT + 1:
                        for ch in range(DC):
                            dve.wait_ge(xnhi_ready, g * 2 + ch + 1)
                            nc.vector.tensor_tensor(xnlo[:, ch, :], m_ps[ch][:], xnhi[:, ch, :], ALU.subtract).then_inc(xn_split, 1)
                    if has_a and s == A_Q + 1:
                        for ch in range(DC):
                            dve.wait_ge(qhi_ready, g * 2 + ch + 1)
                            nc.vector.scalar_tensor_tensor(out=qlo[:, par, ch, :], in0=m_ps[ch][:], scalar=bqk[:, 0, ch:ch + 1],
                                                           in1=qhi[:, par, ch, :], op0=ALU.add, op1=ALU.subtract).then_inc(q_split, 1)
                    if has_a and s == A_K + 1:
                        for ch in range(DC):
                            dve.wait_ge(khi_ready, g * 2 + ch + 1)
                            nc.vector.scalar_tensor_tensor(out=kk[:, 1, ch, :], in0=m_ps[ch][:], scalar=bqk[:, 1, ch:ch + 1],
                                                           in1=kk[:, 0, ch, :], op0=ALU.add, op1=ALU.subtract).then_inc(k_split, 1)
                    if at := lagging(g, s, LH, has_b, has_c):
                        v, back, u = at
                        dve.wait_ge(prob_ready, u + 1)
                        if not early(u, 4):
                            dve.wait_ge(pT_full, u - 3)
                        nc.vector.tensor_copy(phl[:, v % 4, 0], prob[:, v % 4]).then_inc(phi_ready, 1)
                    if (at := lagging(g, s, LT, has_b, has_c)) and at[0] % 2:
                        v, back, u = at
                        dve.wait_ge(pT_full, u + 1)
                        if not early(u, 2):
                            dve.wait_ge(pv_done, u - 1)
                        nc.vector.tensor_copy(pT[:, 1], pT_ps[1][:]).then_inc(pT_out[1], 1)
                    if s == 0 and not early(g, 3):
                        chain = softmax(g - 1)
                    if (at := lagging(g, s, LD, has_b, has_c)) and at[0] % 2:
                        v, back, u = at
                        b, half = v // UB, (v % UB) // 2
                        n = (g - back) * (U // 2) + (v - 1) // 2
                        hs = slice(half * HC, (half + 1) * HC)
                        parts = Chain(dve, on_link, n)
                        parts.mark(nc.vector.reciprocal(rinv[:, b % 2, hs], sums[:, b, hs]))
                        dve.wait_ge(pv_done, u + 1)
                        nc.vector.tensor_reduce(osum[:, half], o_ps[half][:, 0:HC * VP].rearrange("p (h n d) -> p h d n", n=3, d=DH),
                                                AXX, ALU.add).then_inc(o_read, 1)
                        parts.settle()
                        dve.wait_ge(o_read, n + 1)
                        nc.vector.tensor_tensor(
                            on[:, old if back == 1 else par, b, half * P:(half + 1) * P].rearrange("p (h d) -> p h d", d=DH),
                            osum[:, half], rinv[:, b % 2, hs].unsqueeze(2).to_broadcast([P, HC, DH]), ALU.mult).then_inc(on_ready, 1)
                    if s == 0 and not early(g, 3):
                        softmax_end(g - 1, chain)
                    if has_a and s == A_FAR:
                        dve.wait_ge(mask_loaded, (g + 1) * 16)
                        nc.vector.tensor_scalar(far[:, par], mask, -1.0, -1e9, ALU.add, ALU.mult).then_inc(far_ready, 1)
                    if has_l and s == L_STATS:
                        dve.wait_ge(x_loaded, (g + 2) * 16)
                        norm(x_in, xn, 0, Chain(dve, ln_link, (g + 1) * GB), stats_ready, None, None, None)
                    if has_l and s == L_Y:
                        dve.wait_ge(y_loaded, (g + 2) * 16)
                        if has_a:
                            dve.wait_ge(v_full, (g + 1) * 2)
                        nc.vector.tensor_copy(yhi[:], yT[:]).then_inc(yhi_ready, 1)
                    if has_l and s == L_XN:
                        if has_a:
                            dve.wait_ge(xnT_full, (g + 1) * 2)
                        normalise(x_in, xn, 0, rstd_ready, g + 2, xn_ready)
                    if has_c and s in (C_WO + 1, C_WO + 3):
                        n = (s - C_WO) // 2
                        dve.wait_ge(wo_full, (g - 2) * 2 + n + 1)
                        if n == 0:
                            dve.wait_ge(xres_biased, g - 1)
                            if not early(g, 3):
                                dve.wait_ge(x2_stored, (g - 2) * 16)
                        nc.vector.scalar_tensor_tensor(
                            out=x2[:, 2 * n:2 * n + 2, :], in0=m_ps[n][:].rearrange("p (b d) -> p b d", b=2), scalar=c["tg"][:, 0:1],
                            in1=x_res[:, 2 * n:2 * n + 2, :], op0=ALU.mult, op1=ALU.add).then_inc(x2_ready, 1)
                    if has_c and s == C_WO + 3:
                        dve.wait_ge(x2_ready, (g - 1) * 2)
                        norm(x2, xln, 1, Chain(dve, ln2_link, (g - 2) * GB), stats2_ready, None, None, None)
                    if has_c and s == C_WO + 4:
                        if not isinstance(g, int) or g > 2:
                            dve.wait_ge(xln_stored, (g - 2) * 16)
                            dve.wait_ge(xlnT_full, (g - 2) * 2)
                        normalise(x2, xln, 1, rstd2_ready, g - 1, xln_ready)
                    if has_a and s in (A_V + 1, A_V + 3):
                        n = (s - A_V) // 2
                        dve.wait_ge(v_full, g * 2 + n + 1)
                        if not early(g, 1) or n:
                            dve.wait_ge(v_ready, g * 2 + n)
                        nc.vector.tensor_tensor(v32[:], m_ps[n][:].rearrange("p (b d) -> p b d", b=2),
                                                bvo[:, 0:1, :].to_broadcast([P, 2, D]), ALU.add).then_inc(v32_ready, 1)

            steps(dve, step)
            softmax_end(G + 1, softmax(G + 1))


def weights(nc, room, a):
    w = {
        "shape": {"g": [P, DC, FF], "u": [P, DC, FF], "d": [P, FC, D]},
        "view": {
            "g": a["wgT"].rearrange("e (c p) i -> e p c i", p=P),
            "u": a["wuT"].rearrange("e (c p) i -> e p c i", p=P),
            "d": a["wdT"].rearrange("e (c p) d -> e p c d", p=P),
        },
    }
    for part in ("hi", "lo"):
        w[part] = {k: room.sb(f"{k}{part}", w["shape"][k], F32R) for k in WK}
    return w


def gather(nc, c, w, xln_dram, rows_dram):
    with ExitStack() as ctx:
        r = Room(nc, ctx, "g")
        work = r.sb("work", [P, RT, S], F32)
        top = r.sb("top", [P, RT, 8], F32)
        sel = r.sb("sel", [P, RT, S], F32)
        ones = r.sb("ones", [P, S], F32)
        rank = r.sb("rank", [P, RT, S], F32)
        pos = r.sb("pos", [P, B * E], F32)
        aff3 = r.sb("aff3", [P, B, 3, E], BF16)
        rest = r.sb("rest", [P, B, E], F32)
        aff_now = r.sb("aff_now", [P, 2, GB, 3, E], BF16)
        xg = r.sb("xg", [P, 2, GB, D], F32)
        xhi = r.sb("xhi", [P, 2, GB, D], F32R)
        xlo = r.sb("xlo", [P, 2, GB, D], F32R)
        hot = r.sb("hot", [P, 2, GB, E, K], F32R)
        hotb = r.sb("hotb", [P, 2, GB, E, K], BF16)
        gsel = r.sb("gsel", [P, GB * DC, 3 * E], F32)
        w_raw = {k: r.sb(f"w_raw_{k}", w["shape"][k], F32) for k in WK}
        gx = r.sb("gx", [P, 2, E, DC, GB, K], F32)
        t_ps = r.ps("t", [P, RT, S], F32)
        hT_ps = r.ps("hT", [P, GB, DC, P], BF16)
        g_ps = r.ps("g", [P, GB * DC, 3 * E], F32)
        x_ps = [r.ps(f"x{i}", [P, 2, E, K], F32) for i in range(4)]
        link, tr_full, pos_full, pos_out, aff_split = (r.sem(n) for n in ("link", "tr_full", "pos_full", "pos_out", "aff_split"))
        rank_ready = r.sem("rank_ready")
        x_loaded = [r.sem("x_loaded0"), r.sem("x_loaded1")]
        xhi_ready, xlo_ready, hot_ready, hotb_ready = (r.sem(n) for n in ("xhi_ready", "xlo_ready", "hot_ready", "hotb_ready"))
        hT_full, hT_out, g_full, g_read, g_out, g_link = (r.sem(n) for n in ("hT_full", "hT_out", "g_full", "g_read", "g_out", "g_link"))
        x_full, w_loaded, w_hi, w_lo = (r.sem(n) for n in ("x_full", "w_loaded", "w_hi", "w_lo"))
        gx_ready = [r.sem(f"gx{ch}_ready") for ch in range(DC)]
        stored = [r.sem("stored0"), r.sem("stored1")]
        xln_v = xln_dram.rearrange("(g b) p d -> g p b d", b=GB)
        block = ctx.enter_context(nc.Block())

        def pairs(eng, prepare, work):
            prepare(0, 0)
            prepare(1, 1)
            work(0, 0)
            prepare(2, 0)
            work(1, 1)
            with eng.Fori(1, G // 2 - 1) as i:
                prepare(i * 2 + 1, 1)
                work(i * 2, 0)
                prepare(i * 2 + 2, 0)
                work(i * 2 + 1, 1)
            prepare(G - 1, 1)
            work(G - 2, 0)
            work(G - 1, 1)

        def nothing(g, par):
            pass

        def later(g):
            return not isinstance(g, int) or g > 1

        @block.sync
        def _(sp):
            def load(g, par):
                sp.dma_start(xg[:, par], xln_v[g]).then_inc(x_loaded[par], 16)

            load(0, 0)
            load(1, 1)
            for k in WK:
                sp.dma_start(w_raw[k][:], w["view"][k][0]).then_inc(w_loaded, 16)

            def step(g, par):
                for ch in range(DC):
                    sp.wait_ge(gx_ready[ch], (g + 1) * 2)
                sp.dma_start(rows_dram[g], gx[:, par].rearrange("p e c b k -> p (e c b k)")).then_inc(stored[par], 16)

            def step_and_load(g, par):
                sp.wait_ge(xlo_ready, g + 1)
                load(g + 2, par)
                step(g, par)

            step_and_load(0, 0)
            step_and_load(1, 1)
            with sp.Fori(1, G // 2 - 1) as i:
                step_and_load(i * 2, 0)
                step_and_load(i * 2 + 1, 1)
            step(G - 2, 0)
            step(G - 1, 1)
            for par in range(2):
                sp.wait_ge(stored[par], 16 * G // 2)

        @block.tensor
        def _(pe):
            for t in range(RT):
                last = nc.tensor.transpose(t_ps[:, t, :], c["aff"][:, t * P:(t + 1) * P], c["id32"][:])
            last.then_inc(tr_full, 1)
            pe.wait_ge(rank_ready, 1)
            for t in range(RT):
                last = nc.tensor.transpose(t_ps[:, t, :], rank[:, t, :], c["id32"][:])
            last.then_inc(pos_full, 1)

            def step(g, par):
                pe.wait_ge(hot_ready, g + 1)
                pe.wait_ge(xlo_ready, g + 1)
                for n in range(2):
                    for ch in range(DC):
                        bank = x_ps[n * DC + ch]
                        if not isinstance(g, int) or g > 0:
                            pe.wait_ge(gx_ready[ch], (g - 1) * 2 + n + 1)
                        for b in range(2):
                            for part, x in enumerate((xhi, xlo)):
                                last = nc.tensor.matmul(bank[:, b].rearrange("p e k -> p (e k)"),
                                                        x[:, par, 2 * n + b, ch * P:(ch + 1) * P],
                                                        hot[:, par, 2 * n + b].rearrange("p e k -> p (e k)"),
                                                        start=(part == 0), stop=(part == 1))
                        last.then_inc(x_full, 1)
                pe.wait_ge(hotb_ready, g + 1)
                if not isinstance(g, int) or g > 0:
                    pe.wait_ge(hT_out, g)
                    pe.wait_ge(g_read, g)
                for b in range(GB):
                    for half in range(DC):
                        last = nc.tensor.transpose(hT_ps[:, b, half, :],
                                                   hotb[:, par, b, half * EC:(half + 1) * EC, :].rearrange("p e k -> p (e k)"), c["idb"][:])
                last.then_inc(hT_full, 1)
                for b in range(GB):
                    for half in range(DC):
                        last = nc.tensor.matmul(g_ps[:, b * DC + half, :],
                                                hotb[:, par, b, half * EC:(half + 1) * EC, :].rearrange("p e k -> p (e k)"),
                                                aff_now[:, par, b].rearrange("p n e -> p (n e)"), start=True, stop=True)
                last.then_inc(g_full, 1)

            pairs(pe, nothing, step)

        @block.scalar
        def _(act):
            def prepare(g, par):
                act.wait_ge(x_loaded[par], (g - par) * 8 + 16)
                if later(g):
                    act.wait_ge(x_full, (g - 1) * 4)
                nc.scalar.activation(xhi[:, par], xg[:, par], ACT.Copy).then_inc(xhi_ready, 1)
                act.wait_ge(hot_ready, g + 1)
                if later(g):
                    act.wait_ge(g_full, g - 1)
                nc.scalar.activation(hotb[:, par], hot[:, par].bitcast(F32), ACT.Copy).then_inc(hotb_ready, 1)

            def step(g, par):
                for n in range(2):
                    act.wait_ge(x_full, g * 4 + n * DC + 1)
                    if later(g) and n == 0:
                        act.wait_ge(stored[par], (g - par) * 8)
                    nc.scalar.activation(gx[:, par, :, 0, 2 * n:2 * n + 2, :].rearrange("p e b k -> p b e k"),
                                         x_ps[n * DC][:], ACT.Copy).then_inc(gx_ready[0], 1)
                act.wait_ge(hT_full, g + 1)
                nc.scalar.activation(c["onehotT"][:, bass.ds(g * GB, GB)], hT_ps[:], ACT.Copy).then_inc(hT_out, 1)

            act.wait_ge(w_loaded, 16 * len(WK))
            for k in WK:
                nc.scalar.activation(w["hi"][k][:], w_raw[k][:], ACT.Copy).then_inc(w_hi, 1)
            pairs(act, prepare, step)

        @block.gpsimd
        def _(pool):
            def step(g, par):
                pool.wait_ge(xhi_ready, g + 1)
                nc.gpsimd.tensor_tensor(xlo[:, par], xg[:, par], xhi[:, par], ALU.subtract).then_inc(xlo_ready, 1)

            for n, k in enumerate(WK):
                pool.wait_ge(w_hi, n + 1)
                nc.gpsimd.tensor_tensor(w["lo"][k][:], w_raw[k][:], w["hi"][k][:], ALU.subtract).then_inc(w_lo, 1)
            pairs(pool, step, nothing)

        @block.vector
        def _(dve):
            chain = Chain(dve, link)
            aff = c["aff"][:].rearrange("p (b e) -> p b e", e=E)
            chain.link(nc.vector.tensor_copy(aff3[:, :, 0, :], aff))
            chain.link(nc.vector.tensor_tensor(rest[:], aff, aff3[:, :, 0, :], ALU.subtract))
            chain.link(nc.vector.tensor_copy(aff3[:, :, 1, :], rest[:]))
            chain.link(nc.vector.tensor_tensor(aff3[:, :, 2, :], rest[:], aff3[:, :, 1, :], ALU.subtract))
            chain.link(nc.vector.memset(ones[:], 1.0))
            dve.wait_ge(tr_full, 1)
            chain.link(nc.vector.tensor_copy(work[:], t_ps[:]))
            for _ in range(K // 8):
                for t in range(RT):
                    chain.mark(nc.vector.max(top[:, t, :], work[:, t, :]))
                chain.settle()
                for t in range(RT):
                    chain.mark(nc.vector.match_replace(work[:, t, :], top[:, t, :], work[:, t, :], -1.0))
                chain.settle()
            chain.link(nc.vector.tensor_scalar(sel[:], work[:], 0.0, None, ALU.is_lt))
            for t in range(RT):
                chain.mark(nc.vector.tensor_tensor_scan(rank[:, t, :], ones[:], sel[:, t, :], 0.0, ALU.mult, ALU.add))
            chain.settle()
            chain.link(nc.vector.tensor_tensor(rank[:], rank[:], sel[:], ALU.mult))
            nc.vector.tensor_scalar(rank[:], rank[:], -1.0, None, ALU.add).then_inc(rank_ready, 1)
            dve.wait_ge(pos_full, 1)
            chain.link(nc.vector.tensor_copy(pos[:], t_ps[:].rearrange("p t n -> p (t n)")))

            def prepare(g, par):
                if later(g):
                    dve.wait_ge(g_full, g - 1)
                nc.vector.tensor_copy(aff_now[:, par], aff3[:, bass.ds(g * GB, GB)]).then_inc(g_link, 1)
                nc.vector.tensor_tensor(hot[:, par].rearrange("p b e k -> p (b e) k"),
                                        pos[:, bass.ds(g * (GB * E), GB * E)].unsqueeze(2).to_broadcast([P, GB * E, K]),
                                        c["slot"][:].unsqueeze(1).to_broadcast([P, GB * E, K]), ALU.is_equal).then_inc(hot_ready, 1)

            def step(g, par):
                for n in range(2):
                    dve.wait_ge(x_full, g * 4 + n * DC + 2)
                    if later(g) and n == 0:
                        dve.wait_ge(stored[par], (g - par) * 8)
                    nc.vector.tensor_copy(gx[:, par, :, 1, 2 * n:2 * n + 2, :].rearrange("p e b k -> p b e k"),
                                          x_ps[n * DC + 1][:]).then_inc(gx_ready[1], 1)
                dve.wait_ge(g_full, g + 1)
                if not isinstance(g, int) or g > 0:
                    dve.wait_ge(g_out, g)
                nc.vector.tensor_tensor(gsel[:].rearrange("p (b h) n -> p b h n", h=DC),
                                        g_ps[:].rearrange("p (b h) n -> p b h n", h=DC),
                                        c["own"][:].rearrange("p h n e -> p h (n e)").unsqueeze(1).to_broadcast([P, GB, DC, 3 * E]),
                                        ALU.mult).then_inc(g_read, 1)
                dve.wait_ge(g_read, g + 1)
                nc.vector.tensor_reduce(c["gating"][:, bass.ds(g * GB, GB), :].rearrange("p b h -> p (b h)"),
                                        gsel[:], AXX, ALU.add).then_inc(g_out, 1)

            pairs(dve, prepare, step)


def experts(nc, c, w, rows_dram, out_dram):
    with ExitStack() as ctx:
        r = Room(nc, ctx, "e")
        NG = G // NT
        shape, w_view = w["shape"], w["view"]
        stage = r.sb("stage", [P, DC * FF], F32)
        whi = [w["hi"], {k: r.sb(f"w{k}hi", shape[k], F32R) for k in WK}]
        wlo = [w["lo"], {k: r.sb(f"w{k}lo", shape[k], F32R) for k in WK}]
        xf = r.sb("xf", [P, 2, NG, DC * GB * K], F32)
        xr = r.sb("xr", [P, 2, 2, DC, 512], F32R)
        sg = r.sb("sg", [P, 2, 512], F32)
        hh = r.sb("hh", [P, 2, 512], F32)
        hhi = r.sb("hhi", [P, 2, 512], F32R)
        hlo = r.sb("hlo", [P, 2, 512], F32R)
        yT = r.sb("yT", [P, DC, 512], F32)
        yr = r.sb("yr", [P, 4, D], F32)
        g_ps = [r.ps(f"g{i}", [P, 512], F32) for i in range(2)]
        u_ps = [r.ps(f"u{i}", [P, 512], F32) for i in range(2)]
        y_ps = [r.ps(f"y{i}", [P, 512], F32) for i in range(DC)]
        t_ps = [r.ps(f"t{i}", [P, 2, D], F32) for i in range(2)]
        w_loaded, w_hi, w_split = r.sem("w_loaded"), r.sem("w_hi"), r.sem("w_split")
        x_loaded = [r.sem("x_loaded0"), r.sem("x_loaded1")]
        g_full, u_full, sg_ready, hh_ready, hhi_ready, h_ready = (
            r.sem(n) for n in ("g_full", "u_full", "sg_ready", "hh_ready", "hhi_ready", "h_ready"))
        h_used, y_out, t_full, t_out, stored = (r.sem(n) for n in ("h_used", "y_out", "t_full", "t_out", "stored"))

        rows_v = rows_dram.rearrange("g p (e k) -> e p g k", e=E)
        out_v = out_dram.rearrange("(g b) e k d -> b e k g d", b=GB)
        xhi_ready, x_split = r.sem("xhi_ready"), r.sem("x_split")

        def turns(eng, expert):
            expert(0, 0)
            expert(1, 1)
            with eng.Fori(1, E // 2) as i:
                expert(i * 2, 0)
                expert(i * 2 + 1, 1)

        block = ctx.enter_context(nc.Block())

        def later(e, n=0):
            return not isinstance(e, int) or e > n

        @block.sync
        def _(sp):
            def load_weights(e, n):
                k = WK[n]
                if later(e, 1) or n:
                    sp.wait_ge(w_split, (e - 1) * 3 + n)
                sp.dma_start(stage[:].rearrange("p (c i) -> p c i", c=shape[k][1]), w_view[k][e]).then_inc(w_loaded, 16)

            def chunk_in(e, n):
                if later(e) or n >= 2:
                    sp.wait_ge(x_split, e * NT + n - 1)
                sp.dma_start(xf[:, n % 2], rows_v[e, :, n * NG:(n + 1) * NG, :]).then_inc(x_loaded[n % 2], 16)

            def chunk_out(e, n):
                sp.wait_ge(t_out, (e * NT + n) * 2 + 2)
                for b in range(GB):
                    sp.dma_start(out_v[b, e, :, n * 4:(n + 1) * 4, :], yr[b * K:(b + 1) * K]).then_inc(stored, 16)

            def expert(e, par):
                for n in range(NT):
                    if n < NT - 1:
                        chunk_in(e, n + 1)
                    elif not (isinstance(e, int) and e == E - 1):
                        chunk_in(e + 1, 0)
                    if n < 3 and not (isinstance(e, int) and e == E - 1):
                        load_weights(e + 1, n)
                    if later(e) or n:
                        if n:
                            chunk_out(e, n - 1)
                        else:
                            chunk_out(e - 1, NT - 1)

            chunk_in(0, 0)
            expert(0, 0)
            expert(1, 1)
            with sp.Fori(1, E // 2 - 1) as i:
                expert(i * 2, 0)
                expert(i * 2 + 1, 1)
            expert(E - 2, 0)
            expert(E - 1, 1)
            chunk_out(E - 1, NT - 1)
            sp.wait_ge(stored, 16 * GB * NT * E)

        @block.tensor
        def _(pe):
            def down(e, par, n, j):
                hi, lo = whi[par]["d"], wlo[par]["d"]
                t = (e * NT + n) * FC + j
                pe.wait_ge(h_ready, t + 1)
                pe.wait_ge(hhi_ready, t + 1)
                if j == 0 and (later(e) or n):
                    pe.wait_ge(y_out, (e * NT + n) * 2)
                for d in range(DC):
                    w1, w2 = hi[:, j, d * P:(d + 1) * P], lo[:, j, d * P:(d + 1) * P]
                    nc.tensor.matmul(y_ps[d][:], w1, hhi[:, j % 2, :], start=(j == 0), stop=False)
                    nc.tensor.matmul(y_ps[d][:], w1, hlo[:, j % 2, :], start=False, stop=False)
                    last = nc.tensor.matmul(y_ps[d][:], w2, hhi[:, j % 2, :], start=False, stop=(j == FC - 1))
                last.then_inc(h_used, 1)

            def rows(e, n):
                t = e * NT + n
                pe.wait_ge(y_out, (t + 1) * 2)
                for g in range(4):
                    if g % 2 == 0 and (later(e) or n):
                        pe.wait_ge(t_out, (t - 1) * 2 + g // 2 + 1)
                    for d in range(DC):
                        last = nc.tensor.transpose(t_ps[g // 2][:, g % 2, d * P:(d + 1) * P], yT[:, d, g * P:(g + 1) * P], c["id32"][:])
                    if g % 2:
                        last.then_inc(t_full, 1)

            def expert(e, par):
                hi, lo = whi[par], wlo[par]
                if later(e):
                    pe.wait_ge(w_split, e * 3)
                for n in range(NT):
                    t0 = (e * NT + n) * FC
                    pe.wait_ge(x_split, e * NT + n + 1)
                    for j in range(FC):
                        i = slice(j * P, (j + 1) * P)
                        if later(e) or n or j >= 2:
                            pe.wait_ge(hh_ready, t0 + j - 1)
                        for k, banks, full in (("g", g_ps, g_full), ("u", u_ps, u_full)):
                            for ch in range(DC):
                                nc.tensor.matmul(banks[j % 2][:], hi[k][:, ch, i], xr[:, n % 2, 0, ch, :], start=(ch == 0), stop=False)
                                nc.tensor.matmul(banks[j % 2][:], hi[k][:, ch, i], xr[:, n % 2, 1, ch, :], start=False, stop=False)
                                last = nc.tensor.matmul(banks[j % 2][:], lo[k][:, ch, i], xr[:, n % 2, 0, ch, :], start=False,
                                                        stop=(ch == DC - 1))
                            last.then_inc(full, 1)
                        if j:
                            down(e, par, n, j - 1)
                        elif n:
                            down(e, par, n - 1, FC - 1)
                        elif later(e):
                            down(e - 1, 1 - par, NT - 1, FC - 1)
                        if j == 1 and n:
                            rows(e, n - 1)
                        elif j == 1 and later(e):
                            rows(e - 1, NT - 1)

            turns(pe, expert)
            down(E - 1, (E - 1) % 2, NT - 1, FC - 1)
            rows(E - 1, NT - 1)

        @block.scalar
        def _(act):
            def split_hi(e, par, n):
                k = WK[n]
                act.wait_ge(w_loaded, ((e - 1) * 3 + n + 1) * 16)
                if n == 0 and later(e, 1):
                    act.wait_ge(h_used, (e - 1) * NT * FC)
                nc.scalar.activation(whi[par][k][:], stage[:].rearrange("p (c i) -> p c i", c=shape[k][1]), ACT.Copy).then_inc(w_hi, 1)

            def x_hi(e, n):
                act.wait_ge(x_loaded[n % 2], (e * (NT // 2) + n // 2 + 1) * 16)
                if later(e) or n >= 2:
                    act.wait_ge(u_full, (e * NT + n - 1) * FC)
                nc.scalar.activation(xr[:, n % 2, 0].rearrange("p c (g k) -> p g c k", g=NG),
                                     xf[:, n % 2].rearrange("p g (c k) -> p g c k", c=DC), ACT.Copy).then_inc(xhi_ready, 1)

            def y_evacuate(e, n):
                act.wait_ge(h_used, (e * NT + n + 1) * FC)
                if later(e) or n:
                    act.wait_ge(t_full, (e * NT + n) * 2)
                for d in range(DC):
                    nc.scalar.activation(yT[:, d, :], y_ps[d][:], ACT.Copy).then_inc(y_out, 1)

            def expert(e, par):
                for n in range(NT):
                    for j in range(FC):
                        t = (e * NT + n) * FC + j
                        act.wait_ge(g_full, t + 1)
                        if later(e) or n or j >= 2:
                            act.wait_ge(hh_ready, t - 1)
                        nc.scalar.activation(sg[:, j % 2, :], g_ps[j % 2][:], ACT.Silu).then_inc(sg_ready, 1)
                        if j == 0 and n:
                            y_evacuate(e, n - 1)
                        elif j == 0 and later(e):
                            y_evacuate(e - 1, NT - 1)
                        if j == 3 and n < NT - 1:
                            x_hi(e, n + 1)
                        elif j == 3 and not (isinstance(e, int) and e == E - 1):
                            x_hi(e + 1, 0)
                        if n < 3 and j == 4 and not (isinstance(e, int) and e == E - 1):
                            split_hi(e + 1, 1 - par, n)

            x_hi(0, 0)
            expert(0, 0)
            expert(1, 1)
            with act.Fori(1, E // 2 - 1) as i:
                expert(i * 2, 0)
                expert(i * 2 + 1, 1)
            expert(E - 2, 0)
            expert(E - 1, 1)
            y_evacuate(E - 1, NT - 1)

        @block.gpsimd
        def _(pool):
            def expert(e, par):
                for n in range(NT):
                    t = e * NT + n
                    x = xf[:, n % 2].rearrange("p g (c k) -> p g c k", c=DC)
                    hi, lo = (xr[:, n % 2, i].rearrange("p c (g k) -> p g c k", g=NG) for i in range(2))
                    pool.wait_ge(xhi_ready, t + 1)
                    nc.gpsimd.tensor_tensor(lo, x, hi, ALU.subtract).then_inc(x_split, 1)

            turns(pool, expert)

        @block.vector
        def _(dve):
            def split_lo(e, par, n):
                k = WK[n]
                dve.wait_ge(w_hi, (e - 1) * 3 + n + 1)
                nc.vector.tensor_tensor(wlo[par][k][:], stage[:].rearrange("p (c i) -> p c i", c=shape[k][1]), whi[par][k][:],
                                        ALU.subtract).then_inc(w_split, 1)

            def rows_out(e, n):
                for g in range(2):
                    t = (e * NT + n) * 2 + g
                    dve.wait_ge(t_full, t + 1)
                    if g == 0 and (later(e) or n):
                        dve.wait_ge(stored, (e * NT + n) * 16 * GB)
                    nc.vector.tensor_copy(yr[:, 2 * g:2 * g + 2, :], t_ps[g][:]).then_inc(t_out, 1)

            def expert(e, par):
                for n in range(NT):
                    for j in range(FC):
                        t = (e * NT + n) * FC + j
                        dve.wait_ge(sg_ready, t + 1)
                        dve.wait_ge(u_full, t + 1)
                        if later(e) or n or j >= 2:
                            dve.wait_ge(h_used, t - 1)
                        nc.vector.tensor_tensor(hh[:, j % 2, :], u_ps[j % 2][:], sg[:, j % 2, :], ALU.mult).then_inc(hh_ready, 1)
                        dve.wait_ge(hh_ready, t + 1)
                        nc.vector.tensor_copy(hhi[:, j % 2, :], hh[:, j % 2, :]).then_inc(hhi_ready, 1)
                        dve.wait_ge(hhi_ready, t + 1)
                        nc.vector.tensor_tensor(hlo[:, j % 2, :], hh[:, j % 2, :], hhi[:, j % 2, :], ALU.subtract).then_inc(h_ready, 1)
                        if n < 3 and j == 5 and not (isinstance(e, int) and e == E - 1):
                            split_lo(e + 1, 1 - par, n)
                        if n and j == 2:
                            rows_out(e, n - 1)
                        elif j == 2 and later(e):
                            rows_out(e - 1, NT - 1)

            expert(0, 0)
            expert(1, 1)
            with dve.Fori(1, E // 2 - 1) as i:
                expert(i * 2, 0)
                expert(i * 2 + 1, 1)
            expert(E - 2, 0)
            expert(E - 1, 1)
            rows_out(E - 1, NT - 1)


def combine(nc, c, a, x2_dram, rows_out_dram, y_dram):
    CB = 2
    NB = 4
    with ExitStack() as ctx:
        r = Room(nc, ctx, "o")
        rows = r.sb("rows", [P, NB, CB, DC, D], F32)
        xres = r.sb("xres", [P, NB, CB, D], F32)
        gated = r.sb("gated", [P, NB, CB, DC, D], F32)
        rhi = r.sb("rhi", [P, NB, CB, DC, D], F32R)
        rlo = r.sb("rlo", [P, NB, CB, DC, D], F32R)
        hot = r.sb("hot", [P, NB, CB, DC, S], F32R)
        y = r.sb("y", [P, NB, CB, D], F32)
        ps = [r.ps(f"ps{i}", [P, CB, D], F32) for i in range(NB)]
        loaded, res_loaded, stored = ([r.sem(f"{n}{k}") for k in range(NB)] for n in ("loaded", "res_loaded", "stored"))
        gated_ready, hi_ready, lo_ready, hot_ready, full, y_ready = (
            r.sem(n) for n in ("gated_ready", "hi_ready", "lo_ready", "hot_ready", "full", "y_ready"))
        rows_v = rows_out_dram.rearrange("(n b) (h e) k d -> n (e k) b h d", b=CB, e=EC)
        x2_v = x2_dram.rearrange("(n b) p d -> n p b d", b=CB)
        y_v = y_dram.rearrange("(n b) p d -> n p b d", b=CB)
        N = B // CB
        block = ctx.enter_context(nc.Block())

        def rounds(eng, step):
            for n in range(NB):
                step(n, n)
            with eng.Fori(1, N // NB - 1) as i:
                for k in range(NB):
                    step(i * NB + k, k)
            for n in range(N - NB, N):
                step(n, n % NB)

        def reused(n):
            return not isinstance(n, int) or n >= NB

        def uses(n, k):
            return (n - k) * (16 // NB)

        @block.sync
        def _(sp):
            def load(n, k):
                sp.dma_start(rows[:, k], rows_v[n]).then_inc(loaded[k], 16)
                sp.dma_start(xres[:, k], x2_v[n]).then_inc(res_loaded[k], 16)

            def step(n, k):
                sp.wait_ge(y_ready, n + 1)
                sp.dma_start(y_v[n], y[:, k]).then_inc(stored[k], 16)
                if not isinstance(n, int) or n + NB < N:
                    sp.wait_ge(gated_ready, n + 1)
                    load(n + NB, k)

            for n in range(NB):
                load(n, n)
            rounds(sp, step)
            for k in range(NB):
                sp.wait_ge(stored[k], 16 * N // NB)

        @block.gpsimd
        def _(pool):
            def step(n, k):
                if reused(n):
                    pool.wait_ge(full, n - NB + 1)
                nc.gpsimd.tensor_copy(hot[:, k], c["onehotT"][:, bass.ds(n * CB, CB)]).then_inc(hot_ready, 1)

            rounds(pool, step)

        @block.scalar
        def _(act):
            def step(n, k):
                act.wait_ge(gated_ready, n + 1)
                if reused(n):
                    act.wait_ge(full, n - NB + 1)
                nc.scalar.activation(rhi[:, k], gated[:, k], ACT.Copy).then_inc(hi_ready, 1)

            rounds(act, step)

        @block.tensor
        def _(pe):
            def step(n, k):
                pe.wait_ge(hot_ready, n + 1)
                pe.wait_ge(lo_ready, n + 1)
                if reused(n):
                    pe.wait_ge(y_ready, n - NB + 1)
                for b in range(CB):
                    for h in range(DC):
                        for part, x in enumerate((rhi, rlo)):
                            last = nc.tensor.matmul(ps[k][:, b, :], hot[:, k, b, h, :], x[:, k, b, h, :],
                                                    start=(h == 0 and part == 0), stop=(h == DC - 1 and part == 1))
                last.then_inc(full, 1)

            rounds(pe, step)

        @block.vector
        def _(dve):
            def gate(n, k):
                dve.wait_ge(loaded[k], uses(n, k) + 16)
                if reused(n):
                    dve.wait_ge(lo_ready, n - NB + 1)
                nc.vector.tensor_tensor(gated[:, k].rearrange("p b h d -> p (b h) d"),
                                        rows[:, k].rearrange("p b h d -> p (b h) d"),
                                        c["gating"][:, bass.ds(n * CB, CB), :].rearrange("p b h -> p (b h)").unsqueeze(2)
                                        .to_broadcast([P, CB * DC, D]), ALU.mult).then_inc(gated_ready, 1)

            def low(n, k):
                dve.wait_ge(hi_ready, n + 1)
                nc.vector.tensor_tensor(rlo[:, k], gated[:, k], rhi[:, k], ALU.subtract).then_inc(lo_ready, 1)

            def out(n, k):
                dve.wait_ge(full, n + 1)
                dve.wait_ge(res_loaded[k], uses(n, k) + 16)
                if reused(n):
                    dve.wait_ge(stored[k], uses(n, k))
                nc.vector.scalar_tensor_tensor(out=y[:, k], in0=ps[k][:], scalar=c["tg"][:, 1:2], in1=xres[:, k],
                                               op0=ALU.mult, op1=ALU.add).then_inc(y_ready, 1)

            def step(n, k):
                if not isinstance(n, int) or n + 2 < N:
                    gate(n + 2, (k + 2) % NB)
                if not isinstance(n, int) or n + 1 < N:
                    low(n + 1, (k + 1) % NB)
                out(n, k)

            gate(0, 0)
            gate(1, 1)
            low(0, 0)
            rounds(dve, step)


def program(nc, a, y_dram):
    x2_dram = nc.dram_tensor("x2_scratch", [B, S, D], F32, kind="Internal").ap()
    xln_dram = nc.dram_tensor("xln_scratch", [B, S, D], F32, kind="Internal").ap()
    rows_in = nc.dram_tensor("rows_in", [G, P, E * DC * GB * K], F32, kind="Internal").ap()
    rows_out = nc.dram_tensor("rows_out", [B, E, K, D], F32, kind="Internal").ap()
    with ExitStack() as ctx:
        keep = Room(nc, ctx, "keep")
        c = constants(nc, keep, a)
        attention(nc, c, a, x2_dram, xln_dram)
        c["onehotT"] = keep.sb("onehotT", [P, B, DC, S], BF16)
        with ExitStack() as inner:
            w = weights(nc, Room(nc, inner, "w"), a)
            gather(nc, c, w, xln_dram, rows_in)
            experts(nc, c, w, rows_in, rows_out)
        combine(nc, c, a, x2_dram, rows_out, y_dram)


def kernel(x, ctx_1024, mask_BxSxS2_ff1, g_xattn, g_ffn, L0_xattn_Wq, L0_xattn_bq, L0_xattn_Wk, L0_xattn_bk,
           L0_xattn_Wv, L0_xattn_bv, L0_xattn_Wo, L0_xattn_bo, L0_ffn_gate_w, L0_ffn_w_gate, L0_ffn_w_up, L0_ffn_w_down):
    import numpy as np
    import concourse.bacc as bacc
    from concourse.bass_utils import run_bass_kernel_spmd

    n = np.asarray
    arrays = {
        "x": n(x), "ctxT": n(ctx_1024).reshape(B * S, D).T, "mask": n(mask_BxSxS2_ff1), "g_xattn": n(g_xattn), "g_ffn": n(g_ffn),
        "wqT": n(L0_xattn_Wq).T, "wkT": n(L0_xattn_Wk).T, "wvT": n(L0_xattn_Wv).T, "woT": n(L0_xattn_Wo).T,
        "bq": n(L0_xattn_bq), "bk": n(L0_xattn_bk), "bv": n(L0_xattn_bv), "bo": n(L0_xattn_bo),
        "gateT": n(L0_ffn_gate_w).T, "wgT": n(L0_ffn_w_gate).transpose(0, 2, 1), "wuT": n(L0_ffn_w_up).transpose(0, 2, 1),
        "wdT": n(L0_ffn_w_down).transpose(0, 2, 1),
    }
    arrays = {k: np.ascontiguousarray(v) for k, v in arrays.items()}
    nc = bacc.Bacc("TRN2", target_bir_lowering=False, num_devices=1)
    aps = {k: nc.dram_tensor(k, v.shape, mybir.dt.from_np(v.dtype), kind="ExternalInput").ap() for k, v in arrays.items()}
    y = nc.dram_tensor("y", (B, S, D), F32, kind="ExternalOutput").ap()
    program(nc, aps, y)
    out = run_bass_kernel_spmd(nc, [arrays], core_ids=[0])
    return out.results[0]["y"]
```
